# Optimizing a Trainium2 kernel written in Bass

```python
import numpy as np
import jax
import jax.numpy as jnp

def _softmax(x, axis=-1):
    return jax.nn.softmax(x, axis=axis)

def _gelu(x):
    return jax.nn.gelu(x, approximate=True)

def _silu(x):
    return jax.nn.silu(x)

def _sigmoid(x):
    return jax.nn.sigmoid(x)

def _layernorm(x, axis=-1, eps=1e-05):
    m = jnp.mean(x, axis=axis, keepdims=True)
    v = jnp.var(x, axis=axis, keepdims=True)
    return (x - m) / jnp.sqrt(v + eps)

def _scatter_add(tgt, idx, src, axis=0):
    return tgt.at[idx].add(src)

def _segment_sum(src, seg, n):
    return jax.ops.segment_sum(src, seg, n)
kernel_name = 'mk_xattn_ffn_d1_seqx_r2_28fecd'

def setup_inputs(seed: int=0):
    np.random.seed(seed)
    _w = jnp.asarray

    def _rec_inputs():
        import jax
        import jax.numpy as jnp
        _rk = jax.random.key(seed)
        x = -0.0002928 + 1 * jax.random.normal(jax.random.fold_in(_rk, 1), (4, 2048, 512), jnp.float32)
        _lenS = 2048 - jax.random.randint(jax.random.fold_in(_rk, 7), (4,), 0, max(1, 2048 // 4) + 1, jnp.int32)
        _lenS2 = 154 - jax.random.randint(jax.random.fold_in(_rk, 8), (4,), 0, max(1, 154 // 4) + 1, jnp.int32)
        _ctx_1024P = jax.random.normal(jax.random.fold_in(_rk, 11), (4, 16, 512), jnp.float32)
        _ctx_1024c = jax.random.dirichlet(jax.random.fold_in(_rk, 511), 0.3 * jnp.ones((16,), jnp.float32), (4, 154))
        _ctx_1024t = jnp.einsum('bsk,bkd->bsd', _ctx_1024c, _ctx_1024P)
        _ctx_1024t = _ctx_1024t * jax.lax.rsqrt(jnp.mean(jnp.square(_ctx_1024t)) + 1e-12) * 0.953939
        ctx_1024 = -0.000191848 + 0.999787 * (_ctx_1024t + 0.3 * jax.random.normal(jax.random.fold_in(_rk, 611), (4, 154, 512), jnp.float32))
        return (x, ctx_1024)
    x, ctx_1024 = _rec_inputs()

    def _L0_xattn_setup():
        import jax, jax.numpy as jnp
        import numpy as np
        D_MODEL = 512
        NUM_HEADS = 16
        DEPTH = D_MODEL // NUM_HEADS
        key = jax.random.key(seed)
        ks = jax.random.split(key, 10)
        B, T, C = (2, 1024, 1536)
        s = 1.0 / np.sqrt(D_MODEL)
        inp = {'x': jax.random.normal(ks[0], (B, T, D_MODEL), dtype=jnp.float32), 'context': jax.random.normal(ks[1], (B, C, D_MODEL), dtype=jnp.float32), 'Wq': jax.random.normal(ks[2], (D_MODEL, D_MODEL), dtype=jnp.float32) * s, 'bq': jnp.zeros((D_MODEL,), dtype=jnp.float32), 'Wk': jax.random.normal(ks[3], (D_MODEL, D_MODEL), dtype=jnp.float32) * s, 'bk': jnp.zeros((D_MODEL,), dtype=jnp.float32), 'Wv': jax.random.normal(ks[4], (D_MODEL, D_MODEL), dtype=jnp.float32) * s, 'bv': jnp.zeros((D_MODEL,), dtype=jnp.float32), 'Wo': jax.random.normal(ks[5], (D_MODEL, D_MODEL), dtype=jnp.float32) * s, 'bo': jnp.zeros((D_MODEL,), dtype=jnp.float32)}
        return inp
    _L0_xattn_all = _L0_xattn_setup()
    _L0_xattn_in = {k: v for k, v in _L0_xattn_all.items() if k in ('Wq', 'bq', 'Wk', 'bk', 'Wv', 'bv', 'Wo', 'bo')}
    del _L0_xattn_all

    def _L0_ffn_setup():
        import jax, jax.numpy as jnp
        import numpy as np
        IN_F = 512
        OUT_F = 512
        N_EXPERTS = 8
        TOP_K = 2
        key = jax.random.key(seed)
        ks = jax.random.split(key, 5)
        scale_in = 1.0 / np.sqrt(IN_F)
        x = jax.random.normal(ks[0], (4, 1024, IN_F), dtype=jnp.float32)
        W_experts = jax.random.uniform(ks[1], (N_EXPERTS, OUT_F, IN_F), jnp.float32, -scale_in, scale_in)
        b_experts = jax.random.uniform(ks[2], (N_EXPERTS, OUT_F), jnp.float32, -scale_in, scale_in)
        W_router = jax.random.uniform(ks[3], (N_EXPERTS, IN_F), jnp.float32, -scale_in, scale_in)
        b_router = jax.random.uniform(ks[4], (N_EXPERTS,), jnp.float32, -scale_in, scale_in)
        return {'x': x, 'W_experts': W_experts, 'b_experts': b_experts, 'W_router': W_router, 'b_router': b_router}
    _L0_ffn_all = _L0_ffn_setup()
    _L0_ffn_in = {k: v for k, v in _L0_ffn_all.items() if k in ('W_experts', 'b_experts', 'W_router', 'b_router')}
    del _L0_ffn_all
    return {'x': x, 'ctx_1024': ctx_1024, 'L0_xattn_Wq': _L0_xattn_in['Wq'], 'L0_xattn_bq': _L0_xattn_in['bq'], 'L0_xattn_Wk': _L0_xattn_in['Wk'], 'L0_xattn_bk': _L0_xattn_in['bk'], 'L0_xattn_Wv': _L0_xattn_in['Wv'], 'L0_xattn_bv': _L0_xattn_in['bv'], 'L0_xattn_Wo': _L0_xattn_in['Wo'], 'L0_xattn_bo': _L0_xattn_in['bo'], 'L0_ffn_W_experts': _L0_ffn_in['W_experts'], 'L0_ffn_b_experts': _L0_ffn_in['b_experts'], 'L0_ffn_W_router': _L0_ffn_in['W_router'], 'L0_ffn_b_router': _L0_ffn_in['b_router']}

def reference(x, ctx_1024, L0_xattn_Wq, L0_xattn_bq, L0_xattn_Wk, L0_xattn_bk, L0_xattn_Wv, L0_xattn_bv, L0_xattn_Wo, L0_xattn_bo, L0_ffn_W_experts, L0_ffn_b_experts, L0_ffn_W_router, L0_ffn_b_router):
    import jax
    import jax.numpy as jnp

    def _L0_xattn_ref(x, context, Wq, bq, Wk, bk, Wv, bv, Wo, bo):
        import jax, jax.numpy as jnp
        import numpy as np
        D_MODEL = 512
        NUM_HEADS = 16
        DEPTH = D_MODEL // NUM_HEADS
        B, T, D = x.shape
        C = context.shape[1]
        H, d = (NUM_HEADS, DEPTH)
        q = x @ Wq.T + bq
        k = context @ Wk.T + bk
        v = context @ Wv.T + bv
        q = q.reshape(B, T, H, d).transpose(0, 2, 1, 3)
        k = k.reshape(B, C, H, d).transpose(0, 2, 1, 3)
        v = v.reshape(B, C, H, d).transpose(0, 2, 1, 3)
        scores = jnp.einsum('bhtd,bhcd->bhtc', q, k) / jnp.sqrt(jnp.asarray(d, x.dtype))
        attn = jax.nn.softmax(scores, axis=-1)
        out = jnp.einsum('bhtc,bhcd->bhtd', attn, v)
        out = out.transpose(0, 2, 1, 3).reshape(B, T, D)
        return out @ Wo.T + bo

    def _L0_ffn_ref(x, W_experts, b_experts, W_router, b_router):
        import jax, jax.numpy as jnp
        import numpy as np
        IN_F = 512
        OUT_F = 512
        N_EXPERTS = 8
        TOP_K = 2
        router_logits = jnp.einsum('bsd,ed->bse', x, W_router) + b_router
        router_weights = jax.nn.softmax(router_logits, axis=-1)
        if TOP_K < N_EXPERTS:
            topk_w, topk_idx = jax.lax.top_k(router_weights, TOP_K)
            sparse = jnp.zeros_like(router_weights)
            router_weights = jnp.take_along_axis(sparse, topk_idx, axis=-1)
            router_weights = sparse.at[..., :].set(0.0)
            b_idx = jnp.arange(sparse.shape[0])[:, None, None]
            s_idx = jnp.arange(sparse.shape[1])[None, :, None]
            router_weights = sparse.at[b_idx, s_idx, topk_idx].set(topk_w)
        expert_out = jnp.einsum('bsd,eod->bseo', x, W_experts) + b_experts
        return jnp.einsum('bseo,bse->bso', expert_out, router_weights)
    x = x + _L0_xattn_ref(_layernorm(x, axis=-1), ctx_1024, L0_xattn_Wq, L0_xattn_bq, L0_xattn_Wk, L0_xattn_bk, L0_xattn_Wv, L0_xattn_bv, L0_xattn_Wo, L0_xattn_bo)
    x = x + _L0_ffn_ref(_layernorm(x, axis=-1), L0_ffn_W_experts, L0_ffn_b_experts, L0_ffn_W_router, L0_ffn_b_router)
    return x

_drawn_inputs = setup_inputs


def setup_inputs(seed=0):
    import zlib

    import numpy as np

    out = dict(_drawn_inputs(seed))
    spreads = {'L0_xattn_bq': (0.0, 0.315),
     'L0_xattn_bk': (0.0, 0.8),
     'L0_xattn_bv': (0.0, 0.1),
     'L0_xattn_bo': (0.0, 0.1)}
    factors = {'L0_ffn_b_experts': 8.0}
    for name, (base, spread) in spreads.items():
        noise = np.random.default_rng([zlib.crc32(name.encode()), seed]).standard_normal(out[name].shape)
        drawn = base * np.exp(spread * noise) if base else spread * noise
        out[name] = jnp.asarray(drawn.astype(out[name].dtype))
    for name, factor in factors.items():
        out[name] = (out[name] * factor).astype(out[name].dtype)
    return out
```

```python
import math
from contextlib import ExitStack

import concourse.bass as bass
import numpy as np
from concourse import mybir

F32, F16 = mybir.dt.float32, mybir.dt.float16
I32, U32 = mybir.dt.int32, mybir.dt.uint32
ALU = mybir.AluOpType
ACT = mybir.ActivationFunctionType
AX = mybir.AxisListType.X

B, T, D, C = 4, 2048, 512, 154
H, HD = 16, 32
NE, TOPK = 8, 2
N = B * T
P = 128
TB = 512
NB = N // TB
NJ = TB // P
KC = D // P
NG = H // 4
CR = C - P
CP = 160
EPS = 1e-5

XS, WS1 = 2.0, 8.0
QS = XS * WS1
KS = 4.0
SS = QS * KS
PSC = 4096.0
VS = 16.0
WS = 64.0
XS2 = 32.0
OSC = 1.0 / (VS * WS)
ESC = 1.0 / (XS2 * WS)
ROOT = math.sqrt(HD)
MSHIFT = math.log(PSC) * ROOT

REGION = N + P
MAXT = N * TOPK // P + NE
AHEAD = 4
NDUMMY = MAXT + AHEAD - N * TOPK // P
ROWS = NE * REGION + NDUMMY * P


class Blk:

    def __init__(self, c, reg=None):
        self.c, self.reg = c, reg

    def __add__(self, k):
        return Blk(self.c + k, self.reg)

    @property
    def par(self):
        return self.c % 2

    def at(self, n, k=0):
        return n * self.c + k if self.reg is None else self.reg * (2 * n) + (n * self.c + k)

    def half(self, n, k=0):
        return n * (self.c // 2) + k if self.reg is None else self.reg * n + (n * (self.c // 2) + k)

    def here(self, last=NB - 1):
        return self.reg is not None or 0 <= self.c <= last


def build(nc, x, ctxT, ctxR, wqT, bq, wkT, bk, wvT, bv, woT, bo, weT, be, wrT, br, out):
    top = ExitStack()
    keep = top.enter_context
    k_d = nc.dram_tensor("k_scratch", (B, 96, H * CP), F16)
    vm_d = nc.dram_tensor("vm_scratch", (B, P, H * 2 * 33), F16)
    vr_d = nc.dram_tensor("vr_scratch", (B, P, NG * 2 * 4 * 33), F16)
    x1_d = nc.dram_tensor("x1_scratch", (N, D), F32)
    xs_d = nc.dram_tensor("dispatched", (ROWS, D), F32)
    ys_d = nc.dram_tensor("expert_out", (MAXT * P, D), F32)

    tick = {}

    def sem(name, ctx=keep, prime=0):
        s = ctx(nc.semaphore(name))
        primes[name] = prime
        names[id(s)] = name
        held.append(s)
        return s

    primes, names, held = {}, {}, []

    def start_counts(e, first):
        for s in held[first:]:
            if primes[names[id(s)]]:
                e.sem_inc(s, primes[names[id(s)]])

    def wait(e, s, v):
        if isinstance(v, int) and v <= 0:
            return
        e.wait_ge(s, v + primes[names[id(s)]])
        if e is nc.sync and not isinstance(v, int):
            hold(e)

    def hold(e):
        e.sem_inc(tick[id(e)], 1)

    for nm, e in (("dve", nc.vector), ("pool", nc.gpsimd), ("sp", nc.sync)):
        tick[id(e)] = keep(nc.semaphore("tick_" + nm))

    idx_all = keep(nc.sbuf_tensor("idx_all", [P, NB * 8], I32))
    w_all = keep(nc.sbuf_tensor("w_all", [P, NB * 8], F32))
    row_t = keep(nc.sbuf_tensor("row_t", [1, MAXT + AHEAD], I32))
    exp_t = keep(nc.sbuf_tensor("exp_t", [1, MAXT + AHEAD], I32))
    ident = keep(nc.sbuf_tensor("ident", [P, P], F32))

    attend = ExitStack()
    a = attend.enter_context
    wq_s = a(nc.sbuf_tensor("wq_s", [P, 2, KC, D], F16))
    wo_s = a(nc.sbuf_tensor("wo_s", [P, 2, KC, D], F16))
    wr_s = a(nc.sbuf_tensor("wr_s", [P, 2, KC, NE], F16))
    bqs = a(nc.sbuf_tensor("bqs", [P, NG], F32))
    bo_b = a(nc.sbuf_tensor("bo_b", [P, D], F32))
    br_b = a(nc.sbuf_tensor("br_b", [P, NE], F32))

    with ExitStack() as prep:
        t = prep.enter_context
        ctx_sb = t(nc.sbuf_tensor("ctx_sb", [P, KC, B * C], F32))
        ctr_sb = t(nc.sbuf_tensor("ctr_sb", [P, KC, P], F32))
        w_sb = {n: t(nc.sbuf_tensor("w32_" + n, [P, KC, D], F32)) for n in ("q", "o", "k", "v")}
        wr32 = t(nc.sbuf_tensor("wr32", [P, KC, NE], F32))
        bk_s = t(nc.sbuf_tensor("bk_s", [P, NG], F32))
        bv_b = t(nc.sbuf_tensor("bv_b", [P, D], F32))
        k32 = [t(nc.sbuf_tensor(f"k32_{i}", [P, B * C], F32)) for i in range(2)]
        kk = [t(nc.sbuf_tensor("k_" + n, [P, NG, B, CP], F16)) for n in ("hi", "lo")]
        v32 = [t(nc.sbuf_tensor(f"v32_{i}", [P, H, HD], F32)) for i in range(2)]
        vm = [t(nc.sbuf_tensor(f"vm_{i}", [P, H, 2, 33], F16)) for i in range(2)]
        vr = t(nc.sbuf_tensor("vr", [P, 2, H, 33], F16))
        zero = t(nc.sbuf_tensor("zero", [P, NG * 2 * 4 * 33], F16))
        kp = t(nc.psum_tensor("kp", [P, 4, 512], F32))
        vp = t(nc.psum_tensor("vp", [P, 2, 512], F32))
        L = {n: sem("ld_" + n, t) for n in ("bias", "ctx", "q", "o", "k", "v", "r")}
        p_id, p_hi, p_bk, p_kp, p_k32 = (sem(n, t) for n in ("p_id", "p_hi", "p_bk", "p_kp", "p_k32"))
        p_kh, p_kl, p_vp, p_v32, p_vh = (sem(n, t) for n in ("p_kh", "p_kl", "p_vp", "p_v32", "p_vh"))
        p_v, p_set, p_vd, p_kd, p_vz, p_lo = (sem(n, t) for n in ("p_v", "p_set", "p_vd", "p_kd", "p_vz", "p_lo"))
        p_vd2 = sem("p_vd2", t)
        block = t(nc.Block())

        @block.sync
        def _(e):
            e.dma_start(ctx_sb[:, :, :], ctxT.rearrange("(k p) n -> p k n", p=P)).then_inc(L["ctx"], 16)
            e.dma_start(ctr_sb[:, :, :], ctxR.rearrange("(k p) n -> p k n", p=P)).then_inc(L["ctx"], 16)
            for n, src in (("k", wkT), ("v", wvT), ("q", wqT), ("o", woT)):
                e.dma_start(w_sb[n][:, :, :], src.rearrange("(k p) n -> p k n", p=P)).then_inc(L[n], 16)
            wait(e, p_kh, NG)
            wait(e, p_kl, NG)
            for g in range(4):
                for part, row in ((0, 0), (1, 32), (0, 64)):
                    for b in range(B):
                        e.dma_start(k_d[b, row:row + 32, :].rearrange("r (G g c) -> r G g c", g=4, c=CP)[:, :, g, :],
                                    kk[part][32 * g:32 * g + 32, :, b, :]).then_inc(p_kd, 16)
            wait(e, p_vd, 16 * B // 2)
            wait(e, p_vd2, 16 * B // 2)
            wait(e, p_vz, 16 * B)
            wait(e, p_v, B + 1)
            for b in range(B):
                for g in range(4):
                    for part in range(2):
                        e.dma_start(vr_d[b, 32 * g:32 * g + CR, :].rearrange("r (G l g c) -> r G l g c", l=2, g=4, c=33)[:, :, part, g, :],
                                    vr[32 * b:32 * b + CR, part, g::4, :]).then_inc(p_kd, 16)
            wait(e, p_kd, 16 * (12 * B + 8 * B))

        @block.gpsimd
        def _(e):
            e.memset(ident[:, :], 0.0).then_inc(p_id, 1)
            e.memset(zero[:, :], 0.0).then_inc(p_set, 1)
            for n, tile in enumerate(vm):
                e.memset(tile[:, :, 0, 32:33], 1.0).then_inc(p_set, 1)
                e.memset(tile[:, :, 1, 32:33], 0.0).then_inc(p_set, 1)
            e.memset(vr[:, 0, :, 32:33], 1.0).then_inc(p_set, 1)
            e.memset(vr[:, 1, :, 32:33], 0.0).then_inc(p_set, 1)
            wait(e, p_id, 1)
            e.affine_select(out=ident[:, :], in_=ident[:, :], compare_op=ALU.not_equal, fill=1.0, base=0,
                            pattern=[[-1, P]], channel_multiplier=1).then_inc(p_id, 1)

        @block.scalar
        def _(e):
            e.dma_start(bk_s[:, :], bk).then_inc(L["bias"], 16)
            e.dma_start(bqs[:, :], bq).then_inc(L["bias"], 16)
            e.dma_start(bv_b[:, :], bv.rearrange("(a n) -> a n", a=1).broadcast_to([P, D])).then_inc(L["bias"], 16)
            e.dma_start(bo_b[:, :], bo.rearrange("(a n) -> a n", a=1).broadcast_to([P, D])).then_inc(L["bias"], 16)
            e.dma_start(br_b[:, :], br.rearrange("(a n) -> a n", a=1).broadcast_to([P, NE])).then_inc(L["bias"], 16)
            e.dma_start(wr32[:, :, :], wrT.rearrange("(k p) n -> p k n", p=P)).then_inc(L["r"], 16)
            wait(e, p_set, 7)
            for b in range(B):
                e.dma_start(vr_d[b, :, :], zero[:, :]).then_inc(p_vz, 16)
            wait(e, p_bk, 1)
            for G in range(NG):
                wait(e, p_kp, G + 1)
                if G >= 2:
                    wait(e, p_kl, G - 1)
                e.activation(k32[G % 2][:, :].rearrange("p (a n) -> p a n", a=2), kp[:, 2 * (G % 2):2 * (G % 2) + 2, 0:2 * C],
                             ACT.Identity, bias=bk_s[:, G:G + 1], scale=KS).then_inc(p_k32, 1)
            for n, (w, dst, scale) in enumerate(((w_sb["q"], wq_s, WS1), (w_sb["o"], wo_s, WS), (wr32, wr_s, WS))):
                wait(e, L["qor"[n]], 16)
                e.activation(dst[:, 0, :, :], w[:, :, :], ACT.Copy, scale=scale).then_inc(p_hi, 1)
            for b in range(B):
                wait(e, p_v, b + 1)
                e.dma_start(vm_d[b, :, :], vm[b % 2][:, :, :, :].rearrange("p h l c -> p (h l c)")).then_inc((p_vd, p_vd2)[b % 2], 16)

        @block.vector
        def _(e):
            wait(e, L["bias"], 80)
            e.tensor_scalar(bk_s[:, :], bk_s[:, :], KS, None, ALU.mult).then_inc(p_bk, 1)
            e.tensor_scalar(bqs[:, :], bqs[:, :], QS, None, ALU.mult).then_inc(p_bk, 1)
            e.tensor_scalar(bv_b[:, :], bv_b[:, :], VS, None, ALU.mult).then_inc(p_bk, 1)
            for G in range(NG):
                wait(e, p_k32, G + 1)
                k4 = k32[G % 2][:, :].rearrange("p (b c) -> p b c", b=B)
                e.tensor_copy(kk[0][:, G, :, 0:C], k4).then_inc(p_lo, 1)
                wait(e, p_lo, 2 * G + 1)
                e.tensor_tensor(kk[1][:, G, :, 0:C], k4, kk[0][:, G, :, 0:C], ALU.subtract).then_inc(p_lo, 1)
                wait(e, p_lo, 2 * G + 2)
                e.tensor_copy(kk[0][:, G, :, C:CP], kk[0][:, G, :, P:P + CP - C]).then_inc(p_kh, 1)
                e.tensor_copy(kk[1][:, G, :, C:CP], kk[1][:, G, :, P:P + CP - C]).then_inc(p_kl, 1)
            wait(e, p_set, 7)
            wait(e, p_bk, 3)
            for b in range(B + 1):
                wait(e, p_vp, b + 1)
                if b >= 2:
                    wait(e, (p_vd, p_vd2)[b % 2], 16 * (b // 2))
                e.scalar_tensor_tensor(v32[b % 2][:, :, :].rearrange("p h d -> p (h d)"), vp[:, b % 2, :], VS, bv_b[:, :],
                                       ALU.mult, ALU.add).then_inc(p_v32, 1)
                wait(e, p_v32, b + 1)
                hi, lo = (vm[b % 2][:, :, 0, 0:HD], vm[b % 2][:, :, 1, 0:HD]) if b < B else (vr[:, 0, :, 0:HD], vr[:, 1, :, 0:HD])
                e.tensor_copy(hi, v32[b % 2][:, :, :]).then_inc(p_vh, 1)
                wait(e, p_vh, b + 1)
                e.tensor_tensor(lo, v32[b % 2][:, :, :], hi, ALU.subtract).then_inc(p_v, 1)
                wait(e, p_v, b + 1)
            for n, (w, dst, scale) in enumerate(((w_sb["q"], wq_s, WS1), (w_sb["o"], wo_s, WS), (wr32, wr_s, WS))):
                wait(e, p_hi, n + 1)
                e.scalar_tensor_tensor(dst[:, 1, :, :].rearrange("p k n -> p (k n)"), w[:, :, :].rearrange("p k n -> p (k n)"), scale,
                                       dst[:, 0, :, :].rearrange("p k n -> p (k n)"), ALU.mult, ALU.subtract).then_inc(p_bk, 1)

        @block.tensor
        def _(e):
            wait(e, L["ctx"], 32)
            wait(e, L["k"], 16)
            for G in range(NG):
                if G >= 2:
                    wait(e, p_k32, G - 1)
                for half in range(2):
                    for k in range(KC):
                        m = e.matmul(kp[:, 2 * (G % 2) + half, 0:2 * C], w_sb["k"][:, k, G * P:(G + 1) * P],
                                     ctx_sb[:, k, half * 2 * C:(half + 1) * 2 * C], start=(k == 0), stop=(k == KC - 1))
                m.then_inc(p_kp, 1)
            wait(e, L["v"], 16)
            for b in range(B + 1):
                if b >= 2:
                    wait(e, p_v32, b - 1)
                for k in range(KC):
                    lhs = ctx_sb[:, k, b * C:b * C + P] if b < B else ctr_sb[:, k, :]
                    m = e.matmul(vp[:, b % 2, :], lhs, w_sb["v"][:, k, :], start=(k == 0), stop=(k == KC - 1))
                m.then_inc(p_vp, 1)

    xA = [a(nc.sbuf_tensor(f"xA{i}", [P, NJ, D], F32)) for i in range(2)]
    xR = [a(nc.sbuf_tensor(f"xR{i}", [P, NJ, D], F32)) for i in range(2)]
    xn1 = a(nc.sbuf_tensor("xn1", [P, NJ, D], F32))
    xnT = [a(nc.sbuf_tensor("xnT_" + n, [P, KC, TB], F16)) for n in ("hi", "lo")]
    qs = [a(nc.sbuf_tensor("q_" + n, [P, NG, TB], F16)) for n in ("hi", "lo")]
    Qst = [a(nc.sbuf_tensor(f"Qst{i}", [97, H, TB], F16)) for i in range(2)]
    Kst = [a(nc.sbuf_tensor(f"Kst{i}", [97, H, CP], F16)) for i in range(2)]
    Vm = [a(nc.sbuf_tensor(f"Vm{i}", [P, H, 2, 33], F16)) for i in range(2)]
    Vr = [a(nc.sbuf_tensor(f"Vr{i}", [P, NG, 2, 4 * 33], F16)) for i in range(2)]
    mx_sb = a(nc.sbuf_tensor("mx_sb", [P, NJ * H], F32))
    mT = a(nc.sbuf_tensor("mT", [H, TB], F16))
    P32 = [a(nc.sbuf_tensor(f"P32_{i}", [P, 2, TB], F32)) for i in range(2)]
    Pst = [a(nc.sbuf_tensor("P_" + n, [P, 10, TB], F16)) for n in ("hi", "lo")]
    att = a(nc.sbuf_tensor("att", [P, NJ, H, HD], F32))
    aT = [a(nc.sbuf_tensor("aT_" + n, [P, KC, TB], F16)) for n in ("hi", "lo")]
    xn2 = [a(nc.sbuf_tensor(f"xn2_{i}", [P, NJ, D], F32)) for i in range(2)]
    x2T = [a(nc.sbuf_tensor("x2T_" + n, [P, KC, TB], F16)) for n in ("hi", "lo")]
    rcp = a(nc.sbuf_tensor("rcp", [P, 2, 2, 4], F32))
    stats = [a(nc.sbuf_tensor(f"stats{i}", [P, NJ, 6], F32)) for i in range(2)]
    aggr = [a(nc.sbuf_tensor(f"aggr{i}", [P, NJ, 2], F32)) for i in range(2)]
    nrm = [a(nc.sbuf_tensor(f"nrm{i}", [P, 7, NJ], F32)) for i in range(2)]
    lg = a(nc.sbuf_tensor("lg", [P, NJ, NE + 1], F32))
    top8 = a(nc.sbuf_tensor("top8", [P, NJ, 8], F32))
    topi = a(nc.sbuf_tensor("topi", [P, NJ, 8], U32))
    topf = a(nc.sbuf_tensor("topf", [P, TOPK, NJ], F32))
    lgd = a(nc.sbuf_tensor("lgd", [P, NJ, NE + 1], F32))
    ex9 = a(nc.sbuf_tensor("ex9", [P, NJ, NE + 1], F32))
    sm = a(nc.sbuf_tensor("sm", [P, 2, NJ], F32))
    wts = a(nc.sbuf_tensor("wts", [P, TOPK, NJ], F32))
    io8 = a(nc.sbuf_tensor("io8", [P, NJ, NE], F32))
    oneh = a(nc.sbuf_tensor("oneh", [P, TOPK, NJ, NE], F32))
    msk = a(nc.sbuf_tensor("msk", [P, NJ, NE], F16))
    posb = a(nc.sbuf_tensor("posb", [P, NJ, NE], F32))
    seld = a(nc.sbuf_tensor("seld", [P, TOPK, NJ, NE], F32))
    idf = a(nc.sbuf_tensor("idf", [P, TOPK, NJ], F32))
    idx = [a(nc.sbuf_tensor(f"idx{i}", [P, TOPK * NJ], I32)) for i in range(2)]
    base = a(nc.sbuf_tensor("base", [P, NE], F32))
    tri = a(nc.sbuf_tensor("tri", [P, P], F16))
    ones = a(nc.sbuf_tensor("ones", [P, P], F16))
    zrow = a(nc.sbuf_tensor("zrow", [P, D], F32))
    baseI = a(nc.sbuf_tensor("baseI", [1, NE], I32))
    NT = MAXT + AHEAD
    tile_no = a(nc.sbuf_tensor("tile_no", [1, NT], F32))
    tb = a(nc.sbuf_tensor("tb", [P, 6, NE], F32))
    tbi = a(nc.sbuf_tensor("tbi", [P, 2, NE], I32))
    idxf = a(nc.sbuf_tensor("idxf", [P, 2, NB * 8], F32))
    tg = att[0:1, :, :, :].rearrange("p j h d -> p (j h d)")[:, 0:NT * NE].rearrange("p (n e) -> p n e", e=NE)
    te = a(nc.sbuf_tensor("te", [1, 3, NT], F32))

    S = a(nc.psum_tensor("S", [P, 4, 512], F32))
    PVp = a(nc.psum_tensor("PVp", [P, 2, 512], F32))
    W = a(nc.psum_tensor("W", [P, 2, 512], F32))

    def s_(name, prime=0):
        return sem(name, a, prime)

    attend_sems = len(held)
    g_set = s_("g_set")
    ld_xA = [s_(f"ld_xA{i}") for i in range(2)]
    ld_xR = [s_(f"ld_xR{i}") for i in range(2)]
    ld_kv = [s_(f"ld_kv{i}") for i in range(2)]
    restack = [s_(f"restack{i}") for i in range(2)]
    mrow = [s_(f"mrow{i}") for i in range(2)]
    st_x1 = [s_(f"st_x1_{i}") for i in range(2)]
    scat = [s_(f"scat{i}") for i in range(2)]
    nch = [s_(f"nch{i}") for i in range(2)]
    nvar = [s_(f"nvar{i}") for i in range(2)]
    nln = [s_(f"nln{i}") for i in range(2)]
    nrs = [s_(f"nrs{i}") for i in range(2)]
    nap = [s_(f"nap{i}") for i in range(2)]
    xrb = s_("xrb")
    t1p, t1h, t1e = s_("t1p"), s_("t1h"), s_("t1e")
    qp, qhe, qle = s_("qp"), s_("qhe"), s_("qle")
    mxp, mxr, mtp, mte = s_("mxp"), s_("mxr"), s_("mtp"), s_("mte")
    stp, exd, phd, pld = s_("stp"), s_("exd"), s_("phd"), s_("pld")
    pvt, rcd, nmd = s_("pvt"), s_("rcd"), s_("nmd")
    atp, ath, ate = s_("atp"), s_("ath"), s_("ate")
    op_, x1s = s_("op_"), s_("x1s")
    t2p, t2h, t2e = s_("t2p", 8), s_("t2h"), s_("t2e")
    lgp, lge, rch, rex = s_("lgp"), s_("lge"), s_("rch"), s_("rex")
    rcd2, mskd, rp, rev, ridx = s_("rcd2"), s_("mskd"), s_("rp"), s_("rev", 2), s_("ridx")
    tbd, tbz, zst = s_("tbd"), s_("tbz"), s_("zst")

    class Chain:

        def __init__(self, e, s, blk, n):
            self.e, self.s, self.blk, self.n, self.k = e, s, blk, n, 0

        def do(self, ins):
            ins.then_inc(self.s, 1)
            self.k += 1

        def sync(self):
            wait(self.e, self.s, self.blk.at(self.n, self.k))

        def end(self):
            assert self.k == self.n, (self.k, self.n)

    NCH = 2 * NJ + 6

    def dve_norm_stats(e, n, b, src, tiles=range(NJ)):
        for j in tiles:
            e.bn_stats(stats[n][:, j, :], src[:, j, :]).then_inc(nch[n], 1)

    def dve_norm_var(e, n, b):
        ch = Chain(e, nch[n], b, NCH)
        ch.k = NJ
        ch.sync()
        hold(e)
        for j in range(NJ):
            ch.do(e.bn_aggr(aggr[n][:, j, :], stats[n][:, j, :]))
        ch.sync()
        ch.do(e.tensor_scalar(nrm[n][:, 0, :], aggr[n][:, :, 1], EPS, None, ALU.add))
        ch.sync()
        e.tensor_copy(nrm[n][:, 1, :], nrm[n][:, 0, :]).then_inc(nvar[n], 1)

    def dve_norm_coef(e, n, b, scale):
        v = nrm[n]
        ch = Chain(e, nch[n], b, NCH)
        ch.k = 2 * NJ + 1
        wait(e, nrs[n], b.at(1, 1))
        ch.do(e.tensor_tensor(v[:, 3, :], v[:, 2, :], v[:, 2, :], ALU.mult))
        ch.sync()
        ch.do(e.tensor_tensor(v[:, 4, :], v[:, 3, :], v[:, 0, :], ALU.mult))
        ch.sync()
        ch.do(e.tensor_scalar(v[:, 3, :], v[:, 4, :], -0.5 * scale, 1.5 * scale, ALU.mult, ALU.add))
        ch.sync()
        wait(e, nap[n], b.at(1))
        ch.do(e.tensor_tensor(v[:, 5, :], v[:, 3, :], v[:, 2, :], ALU.mult))
        ch.sync()
        ch.do(e.scalar_tensor_tensor(v[:, 6, :], aggr[n][:, :, 0], -1.0, v[:, 5, :], ALU.mult, ALU.mult))
        ch.end()

    def act_norm(e, n, b):
        wait(e, nvar[n], b.at(1, 1))
        e.activation(nrm[n][:, 1, :], nrm[n][:, 1, :], ACT.Ln).then_inc(nln[n], 1)
        wait(e, nln[n], b.at(1, 1))
        e.activation(nrm[n][:, 2, :], nrm[n][:, 1, :], ACT.Exp, scale=-0.5).then_inc(nrs[n], 1)

    def pool_norm_apply(e, n, b, src, dst):
        wait(e, nch[n], b.at(NCH, NCH))
        hold(e)
        for j in range(NJ):
            i = e.tensor_scalar(dst[:, j, :], src[:, j, :], nrm[n][:, 5, j:j + 1], nrm[n][:, 6, j:j + 1], ALU.mult, ALU.add)
        i.then_inc(nap[n], 1)

    wprev = {0: None, 1: None}

    def w_take(e, bank, slot, seq, s, n, k, off):
        if wprev[bank] is not None:
            s0, n0, k0, off0, seq0 = wprev[bank]
            wait(e, s0, (slot + (off0 - (seq - seq0))).at(n0, k0))
        wprev[bank] = (s, n, k, off, seq)

    def w_skip(n):
        for bank in range(2):
            wprev[bank] = (*wprev[bank][:4], wprev[bank][4] + n)

    def pe_T(e, bank, slot, seq, src, i, done, ev, off, n=NG):
        w_take(e, bank, slot, seq, ev, n, i + 1, off)
        for j in range(NJ):
            m = e.transpose(W[:, bank, j * P:(j + 1) * P], src(j, i), ident[:, :])
        m.then_inc(done, 1)

    def split3(k):
        return ((0, 0, k), (1, 0, k), (0, 1, k))

    def pe_T1(e, b, i, bank, slot, seq):
        if i == 0:
            wait(e, nap[0], b.at(1, 1))
        pe_T(e, bank, slot, seq, lambda j, k: xn1[:, j, k * P:(k + 1) * P], i, t1p, t1e, b.c - slot.c)

    def pe_Q(e, b, G, slot, seq):
        if G == 0:
            wait(e, t1e, b.at(4, 4))
        w_take(e, G % 2, slot, seq, qle, 4, G + 1, b.c - slot.c)
        seqs = [t for k in range(KC) for t in split3(k)]
        for n, (wp, xp, k) in enumerate(seqs):
            m = e.matmul(W[:, G % 2, :], wq_s[:, wp, k, G * P:(G + 1) * P], xnT[xp][:, k, :], start=(n == 0), stop=(n == 11))
        m.then_inc(qp, 1)

    def pe_MX(e, b, n):
        p = b.par
        if n == 0:
            wait(e, restack[p], b.half(192, 192))
            wait(e, ld_kv[p], b.half(48, 48))
        if n < 2:
            wait(e, exd, b.at(10))
        else:
            wait(e, mxr, b.at(11, n - 1))
        for u in range(6 * n, min(6 * n + 6, NJ * H)):
            j, h = u // H, u % H
            m = e.matmul(S[:, 2 * (n % 2) + u % 6 // 3, (u % 3) * C:(u % 3 + 1) * C], Qst[p][0:96, h, j * P:(j + 1) * P],
                         Kst[p][0:96, h, 0:C], start=True, stop=True)
        m.then_inc(mxp, 1)

    def pe_O(e, b, j, part, slot, seq):
        if j == 0 and part == 0:
            wait(e, ate, b.at(4, 4))
        if part == 0:
            w_take(e, 0, slot, seq, x1s, 4, j + 1, b.c - slot.c)
        seqs = [t for k in range(KC) for t in split3(k)]
        for n in range(4 * part, 4 * part + 4):
            ap, wp, k = seqs[n]
            m = e.matmul(W[:, 0, :], aT[ap][:, k, j * P:(j + 1) * P], wo_s[:, wp, k, :], start=(n == 0), stop=(n == 11))
        if part == 2:
            m.then_inc(op_, 1)

    def pe_MT(e, b, slot, seq):
        wait(e, mxr, b.at(11, 11))
        w_take(e, 1, slot, seq, mte, 1, 1, b.c - slot.c)
        for j in range(NJ):
            m = e.transpose(W[0:H, 1, j * P:(j + 1) * P], mx_sb[:, j * H:(j + 1) * H], ident[:, :])
        m.then_inc(mtp, 1)

    def pe_R(e, b, slot, seq):
        wait(e, mskd, b.at(1, 1))
        w_take(e, 0, slot, seq, rev, 1, 1, b.c - slot.c)
        mm = msk[:, :, :].rearrange("p j e -> p (j e)")
        e.matmul(W[:, 0, 0:NJ * NE], tri[:, :], mm, start=True, stop=False)
        for d in range(1, NJ):
            m = e.matmul(W[:, 0, d * NE:NJ * NE], ones[:, :], mm[:, 0:(NJ - d) * NE], start=False, stop=(d == NJ - 1))
        for j in range(NJ):
            m = e.matmul(W[:, 0, NJ * NE:(NJ + 1) * NE], ones[:, :], mm[:, j * NE:(j + 1) * NE], start=(j == 0), stop=(j == NJ - 1))
        m.then_inc(rp, 1)

    def pe_ST(e, b, n):
        p = b.par
        if n == 0:
            wait(e, mrow[p], b.half(16, 16))
        if n < 2:
            wait(e, mxr, b.at(11, 11))
        else:
            wait(e, exd, b.at(10, n - 1))
        for u in (2 * n, 2 * n + 1):
            G, r, bank = u // 5, u % 5, 2 * (n % 2) + u % 2
            if r < 4:
                m = e.matmul(S[:, bank, :], Kst[p][0:97, 4 * G + r, 0:P], Qst[p][0:97, 4 * G + r, :], start=True, stop=True)
            else:
                for g in range(4):
                    m = e.matmul(S[32 * g:32 * g + 32, bank, :], Kst[p][0:97, 4 * G + g, P:CP], Qst[p][0:97, 4 * G + g, :],
                                 start=True, stop=True)
        m.then_inc(stp, 1)

    def pe_PV(e, b, G):
        p = b.par
        wait(e, pld, b.at(10, (5 * G + 4) // 2 + 1))
        for q in range(2):
            w = 2 * G + q
            wait(e, nmd, b.at(8, w - 1))
            for jj in range(2):
                j = 2 * q + jj
                tok = slice(j * P, (j + 1) * P)
                o = PVp[:, q, jj * 132:(jj + 1) * 132]
                for n, (pp, vv) in enumerate(((0, 0), (0, 1), (1, 0))):
                    e.matmul(o, Pst[pp][:, (5 * G + 4) % 10, tok], Vr[p][:, G, vv, :], start=(n == 0), stop=(n == 2))
                for g in range(4):
                    for pp, vv in ((0, 0), (0, 1), (1, 0)):
                        m = e.matmul(o[:, g * 33:(g + 1) * 33], Pst[pp][:, (5 * G + g) % 10, tok], Vm[p][:, 4 * G + g, vv, :],
                                     start=False, stop=True, skip_group_check=True)
            m.then_inc(pvt, 1)

    def pe_AT(e, b, G, slot, seq):
        wait(e, nmd, b.at(8, 2 * G + 2))
        pe_T(e, (G + 1) % 2, slot, seq, lambda j, k: att[:, j, 4 * k:4 * k + 4, :].rearrange("p h d -> p (h d)"), G, atp, ate, b.c - slot.c)

    def pe_T2(e, b, i, slot, seq):
        if i == 0:
            wait(e, nap[1], b.at(1, 1))
        pe_T(e, i % 2, slot, seq, lambda j, k: xn2[b.par][:, j, k * P:(k + 1) * P], i, t2p, t2e, b.c - slot.c)

    def pe_LG(e, b, slot, seq):
        wait(e, t2e, b.at(4, 4))
        w_take(e, 0, slot, seq, lge, 1, 1, b.c - slot.c)
        for j in range(NJ):
            seqs = [t for k in range(KC) for t in split3(k)]
            for n, (xp, wp, k) in enumerate(seqs):
                m = e.matmul(W[:, 0, j * NE:(j + 1) * NE], x2T[xp][:, k, j * P:(j + 1) * P], wr_s[:, wp, k, :],
                             start=(n == 0), stop=(n == 11))
        m.then_inc(lgp, 1)

    Z = ["ST0", "ST1", "T2_0", "T2_1", "ST2", "T2_2", "ST3", "T2_3", "ST4", "PV0", "LG", "ST5", "ST6", "PV1", "AT0",
         "ST7", "ST8", "AT1", "ST9", "PV2", "PV3", "AT2", "AT3"]

    def pe_slot(e, s, seq):
        bm, bo_, bn, br_ = s, s + -1, s + 1, s + -2
        for n in range(12):
            if bm.here() and n < 11:
                pe_MX(e, bm, n)
            if bo_.here():
                pe_O(e, bo_, n // 3, n % 3, s, seq)
            if bn.here() and n % 3 == 1:
                pe_T1(e, bn, n // 3, 1, s, seq)
        if br_.here():
            pe_R(e, br_, s, seq)
        if bm.here():
            pe_MT(e, bm, s, seq)
        if bn.here():
            for G in range(NG):
                pe_Q(e, bn, G, s, seq)
        for step in Z:
            kind, i = step[:2], int(step[-1]) if step[-1].isdigit() else 0
            if kind in ("ST", "PV", "AT") and bm.here():
                if kind == "ST":
                    pe_ST(e, bm, i)
                elif kind == "PV":
                    pe_PV(e, bm, i)
                else:
                    pe_AT(e, bm, i, s, seq)
            if bo_.here():
                if kind == "T2":
                    pe_T2(e, bo_, i, s, seq)
                elif kind == "LG":
                    pe_LG(e, bo_, s, seq)

    def act_hi(e, dst, bank, i, b, done, free, hi_sem, fn=None):
        wait(e, done, b.at(4, i + 1))
        if i == 0:
            free()
        if fn is None:
            e.activation(dst[:, i, :], W[:, bank, :], ACT.Copy).then_inc(hi_sem, 1)
        else:
            fn().then_inc(hi_sem, 1)

    def act_T1(e, b, i, bank=1):
        act_hi(e, xnT[0], bank, i, b, t1p, lambda: wait(e, qp, b.at(4)), t1h)

    def act_Q(e, b, G):
        act_hi(e, None, G % 2, G, b, qp, lambda: wait(e, restack[1 - b.par], (b + -1).half(192, 192)), qhe,
               lambda: e.activation(qs[0][:, G, :], W[:, G % 2, :], ACT.Identity, bias=bqs[:, G:G + 1]))

    def act_T2(e, b, i):
        act_hi(e, x2T[0], i % 2, i, b, t2p, lambda: wait(e, lgp, b.at(1)), t2h)

    def act_AT(e, b, G):
        act_hi(e, aT[0], (G + 1) % 2, G, b, atp, lambda: wait(e, op_, b.at(4)), ath)

    def act_exp(e, b, n):
        wait(e, stp, b.at(10, n + 1))
        wait(e, pld, b.at(10, n - 1))
        e.activation(P32[n % 2][:, :, :], S[:, 2 * (n % 2):2 * (n % 2) + 2, :], ACT.Exp, scale=1.0 / (SS * ROOT)).then_inc(exd, 1)

    def act_ph(e, b, n):
        wait(e, exd, b.at(10, n + 1))
        done = (2 * n - 9) // 5 if n >= 5 else (2 * n + 11) // 5 - 4
        wait(e, pvt, b.at(8, 2 * done + 2))
        r = 2 * (n % 5)
        e.activation(Pst[0][:, r:r + 2, :], P32[n % 2][:, :, :], ACT.Copy).then_inc(phd, 1)

    ZA = ["ex0", "ex1", "ph0", "T20", "ph1", "T21", "ex2", "T22", "ph2", "ex3", "T23", "ph3", "ex4", "ph4", "ex5", "ph5",
          "rx0", "ex6", "ph6", "AT0", "ex7", "ph7", "ex8", "ph8", "AT1", "ex9", "ph9", "AT2", "AT3"]

    def act_slot(e, s):
        bm, bo_, bn = s, s + -1, s + 1
        if bn.here():
            for i in range(4):
                act_T1(e, bn, i)
        if bo_.here():
            act_norm(e, 1, bo_)
        if bn.here():
            for G in range(NG):
                act_Q(e, bn, G)
        if (s + 2).here():
            act_norm(e, 0, s + 2)
        for step in ZA:
            kind, i = step[:2], int(step[2])
            if bm.here():
                if kind == "ex":
                    act_exp(e, bm, i)
                elif kind == "ph":
                    act_ph(e, bm, i)
                elif kind == "AT":
                    act_AT(e, bm, i)
            if bo_.here():
                if kind == "T2":
                    act_T2(e, bo_, i)
                elif kind == "rx":
                    wait(e, rch, bo_.at(RCH, RCH))
                    e.activation(ex9[:, :, :], lgd[:, :, :], ACT.Exp).then_inc(rex, 1)

    def dve_lo(e, dst, hi, bank, i, b, hi_sem, ev):
        wait(e, hi_sem, b.at(4, i + 1))
        e.tensor_tensor(dst[:, i, :], W[:, bank, :], hi[:, i, :], ALU.subtract).then_inc(ev, 1)

    def dve_Q(e, b, G):
        wait(e, qhe, b.at(4, G + 1))
        e.scalar_tensor_tensor(qs[1][:, G, :], W[:, G % 2, :], bqs[:, G:G + 1], qs[0][:, G, :], ALU.add, ALU.subtract).then_inc(qle, 1)

    def dve_MX(e, b, n):
        wait(e, mxp, b.at(11, n + 1))
        if n == 0:
            wait(e, mtp, b.at(1))
        k = 3 if n < 10 else 2
        if n < 10:
            e.tensor_reduce(mx_sb[:, 6 * n:6 * n + 6].rearrange("p (a k) -> p a k", a=2),
                            S[:, 2 * (n % 2):2 * (n % 2) + 2, 0:3 * C].rearrange("p a (k c) -> p a k c", c=C),
                            AX, ALU.max).then_inc(mxr, 1)
        else:
            e.tensor_reduce(mx_sb[:, 60:63], S[:, 0, 0:3 * C].rearrange("p (k c) -> p k c", c=C), AX, ALU.max)
            e.tensor_reduce(mx_sb[:, 63:64], S[:, 1, 0:C], AX, ALU.max).then_inc(mxr, 1)

    def dve_O(e, b, j):
        wait(e, op_, b.at(4, j + 1))
        if j == 0:
            wait(e, xrb, b.at(1, 1))
        e.scalar_tensor_tensor(xR[b.par][:, j, :], W[:, 0, :], OSC, xR[b.par][:, j, :], ALU.mult, ALU.add).then_inc(x1s, 1)

    def dve_MT(e, b):
        wait(e, mtp, b.at(1, 1))
        wait(e, mrow[1 - b.par], (b + -1).half(16, 16))
        e.tensor_scalar(mT[:, :], W[0:H, 1, :], 1.0 / SS, MSHIFT, ALU.mult, ALU.subtract).then_inc(mte, 1)

    RCH = 4 + 8 + 1

    def dve_RT1(e, b):
        ch = Chain(e, rch, b, RCH)
        wait(e, lgp, b.at(1, 1))
        wait(e, rcd2, b.at(RC2))
        e.scalar_tensor_tensor(lg[:, :, 0:NE], W[:, 0, 0:NJ * NE].rearrange("p (j e) -> p j e", e=NE), ESC,
                               br_b[:, :].rearrange("p (o e) -> p o e", o=1).broadcast_to([P, NJ, NE]),
                               ALU.mult, ALU.add).then_inc(lge, 1)
        wait(e, lge, b.at(1, 1))
        hold(e)
        for j in range(NJ):
            ch.do(e.max(top8[:, j, :], lg[:, j, 0:NE]))
        ch.sync()
        hold(e)
        for j in range(NJ):
            ch.do(e.max_index(topi[:, j, :], top8[:, j, :], lg[:, j, 0:NE]))
        ch.do(e.tensor_copy(lg[:, :, NE:NE + 1], top8[:, :, 1:2]))
        ch.sync()
        ch.do(e.tensor_tensor(lgd[:, :, :], lg[:, :, :], top8[:, :, 0:1].broadcast_to([P, NJ, NE + 1]), ALU.subtract))
        ch.do(e.tensor_copy(topf[:, :, :].rearrange("p k j -> p j k"), topi[:, :, 0:TOPK]))
        ch.sync()
        for k in range(TOPK):
            ch.do(e.tensor_tensor(oneh[:, k, :, :], io8[:, :, :],
                                  topf[:, k, :].rearrange("p (j o) -> p j o", o=1).broadcast_to([P, NJ, NE]), ALU.is_equal))
        ch.sync()
        ch.end()
        e.tensor_tensor(msk[:, :, :], oneh[:, 0, :, :], oneh[:, 1, :, :], ALU.add).then_inc(mskd, 1)

    RC2 = 9

    def dve_R(e, b):
        p = b.par
        ch = Chain(e, rcd2, b, RC2)
        wait(e, rp, b.at(1, 1))
        wait(e, rev, b.at(1))
        ch.do(e.tensor_tensor(posb[:, :, :], W[:, 0, 0:NJ * NE].rearrange("p (j e) -> p j e", e=NE),
                              base[:, :].rearrange("p (o e) -> p o e", o=1).broadcast_to([P, NJ, NE]), ALU.add))
        ch.sync()
        e.tensor_tensor(base[:, :], base[:, :], W[:, 0, NJ * NE:(NJ + 1) * NE], ALU.add).then_inc(rev, 1)
        for k in range(TOPK):
            i = e.tensor_tensor(seld[:, k, :, :], oneh[:, k, :, :], posb[:, :, :], ALU.mult)
            ch.do(i)
        wait(e, rex, b.at(1, 1))
        ch.do(e.tensor_reduce(sm[:, 0, :], ex9[:, :, 0:NE], AX, ALU.add))
        ch.sync()
        ch.do(e.tensor_reduce(idf[:, :, :], seld[:, :, :, :], AX, ALU.add))
        ch.do(e.reciprocal(wts[:, 0, :], sm[:, 0, :]))
        ch.sync()
        ch.do(e.tensor_tensor(wts[:, 1, :], wts[:, 0, :], ex9[:, :, NE], ALU.mult))
        wait(e, scat[p], b.half(128))
        ch.do(e.tensor_copy(idx[p][:, :], idf[:, :, :].rearrange("p k j -> p (k j)")))
        ch.sync()
        e.tensor_copy(idxf[:, 0, bass.ds(b.at(8), 8)], idf[:, :, :].rearrange("p k j -> p (k j)")).then_inc(ridx, 1)
        ch.do(e.tensor_copy(w_all[:, bass.ds(b.at(8), 8)], wts[:, :, :].rearrange("p k j -> p (k j)")))
        ch.end()

    def dve_pl(e, b, n):
        wait(e, phd, b.at(10, n + 1))
        r = 2 * (n % 5)
        e.tensor_tensor(Pst[1][:, r:r + 2, :], P32[n % 2][:, :, :], Pst[0][:, r:r + 2, :], ALU.subtract).then_inc(pld, 1)

    def dve_nm(e, b, w):
        G, q = w // 2, w % 2
        wait(e, pvt, b.at(8, w + 1))
        if w == 0:
            wait(e, atp, b.at(4))
        src = PVp[:, q, 0:264].rearrange("p (j g c) -> p j g c", j=2, c=33)
        e.reciprocal(rcp[:, q, :, :], src[:, :, :, HD]).then_inc(rcd, 1)
        wait(e, rcd, b.at(8, w + 1))
        e.tensor_tensor(att[:, 2 * q:2 * q + 2, 4 * G:4 * G + 4, :], src[:, :, :, 0:HD],
                        rcp[:, q, :, :].rearrange("p j (g o) -> p j g o", o=1).broadcast_to([P, 2, 4, HD]), ALU.mult).then_inc(nmd, 1)

    ZD = ["pl0", "T20", "pl1", "T21", "T22", "pl2", "T23", "pl3", "pl4", "nm0", "nm1", "RT0", "pl5", "pl6", "nm2", "nm3",
          "AT0", "pl7", "pl8", "AT1", "pl9", "nm4", "nm5", "nm6", "nm7", "AT2", "AT3"]

    def dve_slot(e, s):
        bm, bo_, bn = s, s + -1, s + 1
        for n in range(12):
            if bm.here() and n < 11:
                dve_MX(e, bm, n)
            if bo_.here() and n % 3 == 2:
                j = n // 3
                dve_O(e, bo_, j)
                if j:
                    wait(e, x1s, bo_.at(4, j))
                    dve_norm_stats(e, 1, bo_, xR[bo_.par], [j - 1])
            if bn.here() and n % 3 == 1:
                dve_lo(e, xnT[1], xnT[0], 1, n // 3, bn, t1h, t1e)
        if bo_.here():
            wait(e, x1s, bo_.at(4, 4))
            dve_norm_stats(e, 1, bo_, xR[bo_.par], [3])
            dve_norm_var(e, 1, bo_)
        if bm.here():
            dve_MT(e, bm)
        if bo_.here():
            dve_norm_coef(e, 1, bo_, XS2)
        if (s + -2).here():
            dve_R(e, s + -2)
        for G in range(NG):
            if bn.here():
                dve_Q(e, bn, G)
        if (s + 2).here():
            b2 = s + 2
            wait(e, ld_xA[b2.par], b2.half(16, 16))
            dve_norm_stats(e, 0, b2, xA[b2.par])
            dve_norm_var(e, 0, b2)
        for step in ZD:
            kind, i = step[:2], int(step[2])
            if bm.here():
                if kind == "pl":
                    dve_pl(e, bm, i)
                elif kind == "nm":
                    dve_nm(e, bm, i)
                elif kind == "AT":
                    dve_lo(e, aT[1], aT[0], (i + 1) % 2, i, bm, ath, ate)
            if bo_.here():
                if kind == "T2":
                    dve_lo(e, x2T[1], x2T[0], i % 2, i, bo_, t2h, t2e)
                elif kind == "RT":
                    dve_RT1(e, bo_)
            if step == "pl3" and (s + 2).here():
                dve_norm_coef(e, 0, s + 2, XS)

    def tables(e):
        k = [0]

        def do(ins):
            ins.then_inc(tbd, 1)
            k[0] += 1
            wait(e, tbd, k[0])

        idxc = xn1[:, 0, 0:NB * 8]
        reg0, cnt, nt, cum, first, tmp = (tb[:, i, :] for i in range(6))
        row = lambda v: v[0:1, :]
        wide = lambda v: v.rearrange("p (o e) -> p o e", o=1).broadcast_to([1, NT, NE])
        deep = lambda v: v.rearrange("p (n o) -> p n o", o=1).broadcast_to([1, NT, NE])
        wait(e, rev, NB)
        e.tensor_copy(baseI[:, :], base[0:1, :]).then_inc(tbz, 1)
        do(e.tensor_scalar(reg0, io8[:, 0, :], float(REGION), None, ALU.mult))
        do(e.tensor_tensor(cnt, base[:, :], reg0, ALU.subtract))
        do(e.tensor_scalar(tbi[:, 0, :], cnt, float(P - 1), None, ALU.add))
        do(e.tensor_scalar(tbi[:, 1, :], tbi[:, 0, :], P.bit_length() - 1, None, ALU.arith_shift_right))
        do(e.tensor_copy(nt, tbi[:, 1, :]))
        do(e.tensor_copy(cum, nt))
        for n in range(1, NE):
            do(e.tensor_tensor(cum[:, n:n + 1], cum[:, n - 1:n], nt[:, n:n + 1], ALU.add))
        do(e.scalar_tensor_tensor(tmp, cum, -float(P), reg0, ALU.mult, ALU.add))
        do(e.scalar_tensor_tensor(first, nt, float(P), tmp, ALU.mult, ALU.add))
        do(e.tensor_tensor(tmp[:, 1:NE], first[:, 1:NE], first[:, 0:NE - 1], ALU.subtract))
        for n in range(1, NE):
            do(e.tensor_scalar(idxf[:, 1, :], idxf[:, 0, :], n * REGION - 0.5, tmp[:, n:n + 1], ALU.is_ge, ALU.mult)
               if n == 1 else e.tensor_scalar(idxc, idxf[:, 0, :], n * REGION - 0.5, tmp[:, n:n + 1], ALU.is_ge, ALU.mult))
            if n > 1:
                do(e.tensor_tensor(idxf[:, 1, :], idxf[:, 1, :], idxc, ALU.add))
        do(e.tensor_tensor(idx_all[:, :], idxf[:, 0, :], idxf[:, 1, :], ALU.subtract))
        do(e.tensor_tensor(tg[:, :, :], deep(tile_no[:, :]), wide(row(cum)), ALU.is_ge))
        do(e.tensor_reduce(te[:, 0, :], tg[:, :, :], AX, ALU.add))
        do(e.tensor_tensor(tg[:, :, :], wide(io8[0:1, 0, :]), deep(te[:, 0, :]), ALU.is_equal))
        do(e.tensor_tensor(tg[:, :, :], tg[:, :, :], wide(row(first)), ALU.mult))
        do(e.tensor_reduce(te[:, 1, :], tg[:, :, :], AX, ALU.add))
        do(e.tensor_scalar(te[:, 2, :], te[:, 0, :], NE - 0.5, float(NE * REGION - N * TOPK), ALU.is_ge, ALU.mult))
        do(e.tensor_tensor(te[:, 1, :], te[:, 1, :], te[:, 2, :], ALU.add))
        do(e.scalar_tensor_tensor(te[:, 2, :], tile_no[:, :], float(P), te[:, 1, :], ALU.mult, ALU.add))
        do(e.tensor_copy(row_t[:, :], te[:, 2, :]))
        do(e.tensor_scalar(exp_t[:, :], te[:, 0, :], float(NE - 1), None, ALU.min))

    def pool_slot(e, s):
        if s.here():
            p = s.par
            wait(e, ld_xR[p], s.half(16, 16))
            hold(e)
            for j in range(NJ):
                i = e.tensor_tensor(xR[p][:, j, :], xR[p][:, j, :], bo_b[:, :], ALU.add)
            i.then_inc(xrb, 1)
        bo_ = s + -1
        if bo_.here():
            wait(e, scat[bo_.par], bo_.half(128))
            wait(e, t2p, bo_.at(4, -4))
            pool_norm_apply(e, 1, bo_, xR[bo_.par], xn2[bo_.par])
        br_ = s + -2
        if br_.here():
            p = br_.par
            wait(e, ridx, br_.at(1, 1))
            hold(e)
            for k in range(TOPK):
                for j in range(NJ):
                    e.indirect_dma_start(xs_d.ap(), bass.IndirectOffsetOnAxis(ap=idx[p][:, k * NJ + j:k * NJ + j + 1], axis=0),
                                         xn2[p][:, j, :], None).then_inc(scat[p], 16)
        b2 = s + 2
        if b2.here():
            wait(e, t1p, b2.at(4))
            pool_norm_apply(e, 0, b2, xA[b2.par], xn1)

    def blk_rows(src, b):
        return src[bass.ds(b.at(TB), TB), :].rearrange("(j p) d -> p j d", p=P)

    def sp_xA(e, b):
        wait(e, nap[0], b.at(1, -1))
        e.dma_start(xA[b.par][:, :, :], blk_rows(x, b)).then_inc(ld_xA[b.par], 16)

    def sp_kv(e, b):
        p = b.par
        wait(e, pvt, b.at(8, -8))
        bt = b.c // 4 if b.reg is None else (b.reg * 2 + b.c) // 4
        e.dma_start(Kst[p][0:96, :, :].rearrange("p h c -> p (h c)"), k_d[bass.ds(bt, 1), :, :].rearrange("o p n -> (o p) n")).then_inc(ld_kv[p], 16)
        e.dma_start(Vm[p][:, :, :, :].rearrange("p h l c -> p (h l c)"), vm_d[bass.ds(bt, 1), :, :].rearrange("o p n -> (o p) n")).then_inc(ld_kv[p], 16)
        e.dma_start(Vr[p][:, :, :, :].rearrange("p g l c -> p (g l c)"), vr_d[bass.ds(bt, 1), :, :].rearrange("o p n -> (o p) n")).then_inc(ld_kv[p], 16)

    def sp_restack(e, b):
        p = b.par
        wait(e, qle, b.at(4, 4))
        wait(e, stp, b.at(10, -10))
        for g in range(4):
            for part, row in ((0, 0), (0, 32), (1, 64)):
                e.dma_start(Qst[p][row:row + 32, g::4, :], qs[part][32 * g:32 * g + 32, :, :]).then_inc(restack[p], 16)

    def sp_xR(e, b):
        wait(e, st_x1[b.par], b.half(16))
        wait(e, nap[1], b.at(1, -1))
        e.dma_start(xR[b.par][:, :, :], blk_rows(x, b)).then_inc(ld_xR[b.par], 16)

    def sp_slot(e, s):
        if (s + 3).here():
            sp_xA(e, s + 3)
        if (s + 1).here():
            sp_kv(e, s + 1)
        bo_ = s + -1
        if bo_.here():
            wait(e, x1s, bo_.at(4, 4))
            e.dma_start(blk_rows(x1_d, bo_), xR[bo_.par][:, :, :]).then_inc(st_x1[bo_.par], 16)
        if s.here():
            wait(e, mte, s.at(1, 1))
            e.dma_start(Qst[s.par][96:97, :, :], mT[:, :]).then_inc(mrow[s.par], 16)
        if (s + 1).here():
            sp_restack(e, s + 1)
            sp_xR(e, s + 1)

    def slots(e, fn, first, last, lo, hi, after=None):
        n = (hi - lo + 1) // 2
        for s in range(first, lo):
            fn(Blk(s), s)
        with e.Fori(0, n) as it:
            for u in range(2):
                fn(Blk(lo + u, it), lo + u)
        if after is not None:
            after(2 * n - 2)
        for s in range(lo + 2 * n, last + 1):
            fn(Blk(s), s)

    LAST = NB + 1
    LO, HI = 2, NB - 3
    LO4 = 4

    with nc.Block() as block:
        @block.sync
        def _(e):
            start_counts(e, attend_sems)
            e.dma_start(xR[0][:, :, :], blk_rows(x, Blk(0))).then_inc(ld_xR[0], 16)
            for b in range(2):
                sp_xA(e, Blk(b))
            sp_kv(e, Blk(0))
            sp_xA(e, Blk(2))
            sp_restack(e, Blk(0))
            slots(e, lambda s, q: sp_slot(e, s), 0, LAST, LO, NB - 5)
            wait(e, g_set, 6)
            e.dma_start(xs_d[NE * REGION:ROWS, :].rearrange("(n p) d -> p n d", p=P),
                        zrow[:, :].rearrange("p (o d) -> p o d", o=1).broadcast_to([P, NDUMMY, D])).then_inc(zst, 16)
            wait(e, tbz, 1)
            for n in range(NE):
                r = e.value_load(baseI[0:1, n:n + 1], min_val=0, max_val=NE * REGION - P)
                e.dma_start(xs_d[bass.ds(r, P), :], zrow[:, :]).then_inc(zst, 16)
            wait(e, zst, 16 * (NE + 1))
            for p in range(2):
                wait(e, st_x1[p], 16 * NB // 2)
                wait(e, scat[p], 128 * NB // 2)

        @block.gpsimd
        def _(e):
            e.memset(Kst[0][96:97, :, :], -SS).then_inc(g_set, 1)
            wait(e, g_set, 1)
            e.memset(Kst[1][96:97, :, :], -SS).then_inc(g_set, 1)
            wait(e, g_set, 2)
            e.memset(ones[:, :], 1.0).then_inc(g_set, 1)
            e.memset(tri[:, :], 1.0).then_inc(g_set, 1)
            e.memset(zrow[:, :], 0.0).then_inc(g_set, 1)
            wait(e, g_set, 5)
            e.affine_select(out=tri[:, :], in_=tri[:, :], compare_op=ALU.is_gt, fill=0.0, base=0,
                            pattern=[[1, P]], channel_multiplier=-1).then_inc(g_set, 1)
            e.iota(io8[:, :, :], [[0, NJ], [1, NE]], base=0, channel_multiplier=0, allow_small_or_imprecise_dtypes=True).then_inc(g_set, 1)
            e.iota(base[:, :], [[REGION, NE]], base=0, channel_multiplier=0, allow_small_or_imprecise_dtypes=True).then_inc(g_set, 1)
            e.iota(tile_no[:, :], [[1, NT]], base=0, channel_multiplier=0, allow_small_or_imprecise_dtypes=True).then_inc(g_set, 1)
            for b in range(2):
                if b:
                    wait(e, t1p, 4 * b)
                pool_norm_apply(e, 0, Blk(b), xA[b], xn1)
            slots(e, lambda s, q: pool_slot(e, s), 0, LAST, LO4, HI)

        @block.scalar
        def _(e):
            e.preload_act_table_set("natural_log_exp_and_others")
            for b in range(2):
                act_norm(e, 0, Blk(b))
            for i in range(4):
                act_T1(e, Blk(0), i, 1)
            for G in range(NG):
                act_Q(e, Blk(0), G)
            slots(e, lambda s, q: act_slot(e, s), 0, LAST, LO, HI)

        @block.vector
        def _(e):
            for b in range(2):
                wait(e, ld_xA[b], 16)
                dve_norm_stats(e, 0, Blk(b), xA[b])
                dve_norm_var(e, 0, Blk(b))
                dve_norm_coef(e, 0, Blk(b), XS)
            for i in range(4):
                dve_lo(e, xnT[1], xnT[0], 1, i, Blk(0), t1h, t1e)
            for G in range(NG):
                dve_Q(e, Blk(0), G)
            wait(e, g_set, 9)
            slots(e, lambda s, q: dve_slot(e, s), 0, LAST, LO4, HI)
            tables(e)

        @block.tensor
        def _(e):
            wait(e, g_set, 6)
            for i in range(4):
                pe_T1(e, Blk(0), i, 1, Blk(-1), -1)
            for G in range(NG):
                pe_Q(e, Blk(0), G, Blk(-1), -1)
            slots(e, lambda s, q: pe_slot(e, s, q), 0, LAST, LO, HI, w_skip)
    attend.close()

    TU = 4
    with ExitStack() as ex:
        t = ex.enter_context
        we_s = t(nc.sbuf_tensor("we_s", [P, NE * 2 * KC * D], F16))
        be_s = t(nc.sbuf_tensor("be_s", [P, NE * D], F32))
        w32 = [t(nc.sbuf_tensor(f"w32_{i}", [P, KC * D], F32)) for i in range(3)]
        xg = [t(nc.sbuf_tensor(f"xg{i}", [P, D], F32)) for i in range(TU)]
        gT = [[t(nc.sbuf_tensor(f"gT{i}_{n}", [P, KC, P], F16)) for n in ("hi", "lo")] for i in range(2)]
        yb = [t(nc.sbuf_tensor(f"yb{i}", [P, D], F32)) for i in range(TU)]
        Tp = t(nc.psum_tensor("Tp", [P, 2, 512], F32))
        Yp = t(nc.psum_tensor("Yp", [P, 2, 512], F32))
        expert_sems = len(held)
        ld_w = [sem(f"ld_w{i}", t) for i in range(3)]
        ld_ws = [sem(f"ld_ws{i}", t) for i in range(3)]
        ld_be = sem("ld_be", t)
        ld_g = [sem(f"ld_g{i}", t) for i in range(TU)]
        st_y = [sem(f"st_y{i}", t, 16) for i in range(TU)]
        w0h, w0r = sem("w0h", t), sem("w0r", t)
        wch, wrd = sem("wch", t), sem("wrd", t, 1)
        gp, gh, gl = sem("gp", t, 4), sem("gh", t, 4), sem("gl", t, 4)
        yp, ye = sem("yp", t, 4), sem("ye", t, 4)
        WN = 2 * KC * D
        block = t(nc.Block())

        def tile(it, u):
            return it * TU + u

        def sp_load(e, it, u):
            i = tile(it, u)
            r = e.value_load(row_t[0:1, bass.ds(i, 1)], min_val=0, max_val=ROWS - P)
            wait(e, gp, i + (1 - TU))
            e.dma_start(xg[u % TU][:, :], xs_d[bass.ds(r, P), :]).then_inc(ld_g[u % TU], 16)

        @block.sync
        def _(e):
            start_counts(e, expert_sems)
            e.dma_start(w32[0][:, :].rearrange("p (k n) -> p k n", n=D), weT[0].rearrange("(k p) n -> p k n", p=P)).then_inc(ld_w[0], 16)
            for u in range(TU):
                sp_load(e, 0, u)
            e.dma_start(be_s[:, :], be.rearrange("(a e) n -> a (e n)", a=1).broadcast_to([P, NE * D])).then_inc(ld_be, 16)
            for n in (1, 2):
                e.dma_start(w32[n][:, :].rearrange("p (k n) -> p k n", n=D), weT[n].rearrange("(k p) n -> p k n", p=P)).then_inc(ld_w[n], 16)
            with e.Fori(0, MAXT // TU) as it:
                for u in range(TU):
                    sp_load(e, it, u + TU)
            for u in range(TU):
                wait(e, ld_g[u], 16 * (MAXT // TU + 1))

        @block.gpsimd
        def _(e):
            for n in range(1, NE):
                w, o = w32[n % 3], n * WN
                if n >= 3:
                    if n == 3:
                        wait(e, w0r, 1)
                    else:
                        wait(e, wrd, n - 3)
                    e.dma_start(w[:, :].rearrange("p (k n) -> p k n", n=D), weT[n].rearrange("(k p) n -> p k n", p=P)).then_inc(ld_ws[n % 3], 16)
                wait(e, ld_ws[n % 3] if n >= 3 else ld_w[n], 16 * max(1, n // 3))
                e.tensor_scalar(w[:, :], w[:, :], WS, None, ALU.mult).then_inc(wch, 1)
                wait(e, wch, 2 * n - 1)
                e.tensor_scalar(we_s[:, o:o + KC * D], w[:, :], 1.0, None, ALU.mult).then_inc(wch, 1)
                wait(e, wch, 2 * n)
                e.tensor_tensor(we_s[:, o + KC * D:o + WN], w[:, :], we_s[:, o:o + KC * D], ALU.subtract).then_inc(wrd, 1)

        @block.scalar
        def _(e):
            wait(e, ld_w[0], 16)
            e.activation(we_s[:, 0:KC * D], w32[0][:, :], ACT.Copy, scale=WS).then_inc(w0h, 1)

            def hi(it, u):
                i = tile(it, u)
                wait(e, gp, i + 1)
                wait(e, yp, i - 1)
                e.activation(gT[u % 2][0][:, :, :].rearrange("p k n -> p (k n)"), Tp[:, u % 2, :], ACT.Copy).then_inc(gh, 1)

            hi(0, 0)
            with e.Fori(0, MAXT // TU) as it:
                for u in range(TU):
                    hi(it, u + 1)
                    i = tile(it, u)
                    wait(e, ye, i + 1)
                    e.dma_start(ys_d[bass.ds(i * P, P), :], yb[u][:, :]).then_inc(st_y[u], 16)
            for u in range(TU):
                wait(e, st_y[u], 16 * (MAXT // TU))

        @block.vector
        def _(e):
            wait(e, w0h, 1)
            e.scalar_tensor_tensor(we_s[:, KC * D:WN], w32[0][:, :], WS, we_s[:, 0:KC * D], ALU.mult, ALU.subtract).then_inc(w0r, 1)

            def lo(it, u):
                i = tile(it, u)
                wait(e, gh, i + 1)
                e.tensor_tensor(gT[u % 2][1][:, :, :].rearrange("p k n -> p (k n)"), Tp[:, u % 2, :],
                                gT[u % 2][0][:, :, :].rearrange("p k n -> p (k n)"), ALU.subtract).then_inc(gl, 1)

            lo(0, 0)
            wait(e, ld_be, 16)
            with e.Fori(0, MAXT // TU) as it:
                for u in range(TU):
                    lo(it, u + 1)
                    i = tile(it, u)
                    n = e.value_load(exp_t[0:1, bass.ds(i, 1)], min_val=0, max_val=NE - 1)
                    wait(e, yp, i + 1)
                    wait(e, st_y[u], it * 16)
                    e.scalar_tensor_tensor(yb[u][:, :], Yp[:, u % 2, :], ESC, be_s[:, bass.ds(n * D, D)], ALU.mult, ALU.add).then_inc(ye, 1)

        @block.tensor
        def _(e):
            def turn(it, u):
                i = tile(it, u)
                wait(e, ld_g[u % TU], it * 16 + 16 * (u // TU + 1))
                wait(e, gl, i - 1)
                for k in range(KC):
                    m = e.transpose(Tp[:, u % 2, k * P:(k + 1) * P], xg[u % TU][:, k * P:(k + 1) * P], ident[:, :])
                m.then_inc(gp, 1)

            turn(0, 0)
            wait(e, w0r, 1)
            with e.Fori(0, MAXT // TU) as it:
                for u in range(TU):
                    turn(it, u + 1)
                    i = tile(it, u)
                    n = e.value_load(exp_t[0:1, bass.ds(i, 1)], min_val=0, max_val=NE - 1)
                    wait(e, wrd, n)
                    wait(e, gl, i + 1)
                    wait(e, ye, i - 1)
                    seqs = [q for k in range(KC) for q in split3(k)]
                    for c, (xp, wp, k) in enumerate(seqs):
                        m = e.matmul(Yp[:, u % 2, :], gT[u % 2][xp][:, k, :], we_s[:, bass.ds(n * WN + (wp * KC + k) * D, D)],
                                     start=(c == 0), stop=(c == 11))
                    m.then_inc(yp, 1)

    with ExitStack() as cx:
        t = cx.enter_context
        ig = [t(nc.sbuf_tensor(f"ig{i}", [P, 8], I32)) for i in range(2)]
        wg = [t(nc.sbuf_tensor(f"wg{i}", [P, 8], F32)) for i in range(2)]
        yg = [[t(nc.sbuf_tensor(f"yg{i}_{k}", [P, D], F32)) for k in range(TOPK)] for i in range(8)]
        xc = [t(nc.sbuf_tensor(f"xc{i}", [P, NJ, D], F32)) for i in range(2)]
        oc = [t(nc.sbuf_tensor(f"oc{i}", [P, NJ, D], F32)) for i in range(2)]
        combine_sems = len(held)
        gi = [sem(f"gi{i}", t) for i in range(2)]
        gat = [sem(f"gat{i}", t) for i in range(8)]
        ld_x = [sem(f"ld_x{i}", t) for i in range(2)]
        st_o = [sem(f"st_o{i}", t, 16) for i in range(2)]
        wcp, cm, cd = sem("wcp", t), sem("cm", t), sem("cd", t, 8)
        block = t(nc.Block())

        @block.sync
        def _(e):
            start_counts(e, combine_sems)
            with e.Fori(0, NB // 2) as it:
                for p in range(2):
                    wait(e, cd, it * 8 + 4 * p - 4)
                    e.dma_start(xc[p][:, :, :], x1_d[bass.ds(it * (2 * TB) + p * TB, TB), :].rearrange("(j p) d -> p j d", p=P)).then_inc(ld_x[p], 16)

        @block.scalar
        def _(e):
            with e.Fori(0, NB // 2) as it:
                for p in range(2):
                    wait(e, cd, it * 8 + 4 * p + 4)
                    e.dma_start(out[bass.ds(it * (2 * TB) + p * TB, TB), :].rearrange("(j p) d -> p j d", p=P), oc[p][:, :, :]).then_inc(st_o[p], 16)
            for p in range(2):
                wait(e, st_o[p], 16 * NB // 2)

        @block.gpsimd
        def _(e):
            with e.Fori(0, NB // 2) as it:
                for p in range(2):
                    wait(e, cd, it * 8 + 4 * p - 4)
                    hold(e)
                    e.tensor_copy(ig[p][:, :], idx_all[:, bass.ds(it * 16 + 8 * p, 8)]).then_inc(gi[p], 1)
                    wait(e, gi[p], it + 1)
                    hold(e)
                    for j in range(NJ):
                        for k in range(TOPK):
                            e.indirect_dma_start(yg[4 * p + j][k][:, :], None, ys_d.ap(),
                                                 bass.IndirectOffsetOnAxis(ap=ig[p][:, k * NJ + j:k * NJ + j + 1], axis=0)).then_inc(gat[4 * p + j], 16)

        @block.vector
        def _(e):
            with e.Fori(0, NB // 2) as it:
                for p in range(2):
                    e.tensor_copy(wg[p][:, :], w_all[:, bass.ds(it * 16 + 8 * p, 8)]).then_inc(wcp, 1)
                    wait(e, wcp, it * 2 + p + 1)
                    wait(e, ld_x[p], it * 16 + 16)
                    wait(e, st_o[p], it * 16)
                    for j in range(NJ):
                        wait(e, gat[4 * p + j], it * 32 + 32)
                        e.scalar_tensor_tensor(yg[4 * p + j][0][:, :], yg[4 * p + j][0][:, :], wg[p][:, j:j + 1], xc[p][:, j, :],
                                               ALU.mult, ALU.add).then_inc(cm, 1)
                        wait(e, cm, it * 8 + 4 * p + j + 1)
                        e.scalar_tensor_tensor(oc[p][:, j, :], yg[4 * p + j][1][:, :], wg[p][:, NJ + j:NJ + j + 1], yg[4 * p + j][0][:, :],
                                               ALU.mult, ALU.add).then_inc(cd, 1)
    top.close()


_P = "L0_xattn_"
_F = "L0_ffn_"


def kernel(**inputs):
    import concourse.bacc as bacc
    from concourse.bass_utils import run_bass_kernel_spmd

    ctx = np.asarray(inputs["ctx_1024"]).reshape(B * C, D)
    rem = np.concatenate([ctx.reshape(B, C, D)[:, P:C], ctx.reshape(B, C, D)[:, P:P + CP - C]], axis=1)
    arrays = {
        "x": np.asarray(inputs["x"]).reshape(N, D),
        "ctxT": ctx.T, "ctxR": rem.reshape(B * (CP - P), D).T,
        "wqT": np.asarray(inputs[_P + "Wq"]).T, "bq": np.asarray(inputs[_P + "bq"]).reshape(NG, P).T,
        "wkT": np.asarray(inputs[_P + "Wk"]).T, "bk": np.asarray(inputs[_P + "bk"]).reshape(NG, P).T,
        "wvT": np.asarray(inputs[_P + "Wv"]).T, "bv": inputs[_P + "bv"],
        "woT": np.asarray(inputs[_P + "Wo"]).T, "bo": inputs[_P + "bo"],
        "weT": np.asarray(inputs[_F + "W_experts"]).transpose(0, 2, 1), "be": inputs[_F + "b_experts"],
        "wrT": np.asarray(inputs[_F + "W_router"]).T, "br": inputs[_F + "b_router"],
    }
    arrays = {"in_" + n: np.ascontiguousarray(v) for n, v in arrays.items()}
    nc = bacc.Bacc("TRN2", target_bir_lowering=False, num_devices=1)
    args = [nc.dram_tensor(n, v.shape, mybir.dt.from_np(v.dtype), kind="ExternalInput").ap() for n, v in arrays.items()]
    args.append(nc.dram_tensor("out", (N, D), F32, kind="ExternalOutput").ap())
    build(nc, *args)
    got = run_bass_kernel_spmd(nc, [arrays], core_ids=[0]).results[0]["out"]
    return got.reshape(B, T, D)
```

```python
import math
from contextlib import ExitStack

import concourse.bass as bass
import numpy as np
from concourse import mybir

F32, F16 = mybir.dt.float32, mybir.dt.float16
I32, U32 = mybir.dt.int32, mybir.dt.uint32
ALU = mybir.AluOpType
ACT = mybir.ActivationFunctionType
AX = mybir.AxisListType.X

B, T, D, C = 4, 2048, 512, 154
H, HD = 16, 32
NE, TOPK = 8, 2
N = B * T
P = 128
TB = 512
NB = N // TB
NJ = TB // P
KC = D // P
NG = H // 4
CR = C - P
CP = 160
EPS = 1e-5

XS, WS1 = 2.0, 8.0
QS = XS * WS1
KS = 4.0
SS = QS * KS
PSC = 4096.0
VS = 16.0
WS = 64.0
XS2 = 32.0
OSC = 1.0 / (VS * WS)
ESC = 1.0 / (XS2 * WS)
ROOT = math.sqrt(HD)
MSHIFT = math.log(PSC) * ROOT

RW = D + 2
TILE = 2 * P
REGION = N + TILE
MAXT = N * TOPK // TILE + NE
AHEAD = 2
SPARE = NE * REGION
ROWS = SPARE + TILE
NOWHERE = float(1 << 20)


ORDER_PE = """
    YT1-2 PV2-1 PV3-1 ST8-1 AT0-1 YT2-2 ST9-1 PV4-1 YT3-2 AT1-1 PV5-1 MX0 PV6-1 AT2-1 PV7-1 MX1 MX2 AT3-1 LG0-2
    MX3 O0-1 O1-1 O2-1 O3-1 MX4 XT2+1 O4-1 O5-1 MX5 MX6 O6-1 XT3+1 O7-1 MX7 O8-1 MX8 O9-1 MX9 O10-1 MX10 O11-1
    Q0+1 MT0 Q1+1 Q2+1 Q3+1 Q4+1 Q5+1 ST0 ST1 Q6+1 ST2 R0-2 Q7+1 Q8+1 ST3 ST4 Q9+1 Q10+1 Q11+1 ST5 XT0+2 PV0 XT1+2
    PV1 ST6 YT0-1 ST7
"""
ORDER_ACT = """
    EX2 Qh2+1 PH2 EX3 PH3 Qh3+1 EX4 XTh0+2 PH4 XTh1+2 EX5 PH5 EX6 YTh0-1 YTh1-1 PH6 EX7 PH7 EX8 ATh0 YTh2-1 PH8
    EX9 PH9 YTh3-1 ATh1 ATh2 ATh3 XTh2+2 XTh3+2 NN0+3 Qh0+2 Qh1+2 NN1 EX0+1 PH0+1 RX0-1 EX1+1 PH1+1
"""
ORDER_DVE = """
    NM1-1 PL5-1 YTl0-2 YTl1-2 NV0+2 PL6-1 NM2-1 PL7-1 NM3-1 ATl0-1 YTl2-2 PL8-1 NM4-1 PL9-1 NM5-1 YTl3-2 ATl1-1
    DMX0 NM6-1 NM7-1 ATl2-1 DMX1 ATl3-1 RT0-2 DMX2 Oe0-1 DMX3 DMX4 XTl2+1 Oe1-1 DMX5 DMX6 XTl3+1 DMX7 Oe2-1 DMX8
    DMX9 DMX10 Oe3-1 SN0-1 MTe0 NC0+2 SN1-1 SN2-1 SN3-1 Ql0+1 NV1-1 SA0+3 Ql1+1 NC1-1 SA1+3 PL0 RR0-2 PL1 SA2+3
    SA3+3 Ql2+1 PL2 Ql3+1 PL3 XTl0+2 NM0 PL4 XTl1+2
"""
ORDER_POOL = """
    SD0-3 WH0 NA1-1 NA0+2 SC0-2 XB0
"""
ORDER_SP = """
    KV0 RS0 WW0-1 XR0 MR0 WL0+1 XA0+4 XS0-1
"""
BANK = {"XT0": 0, "O0": 0, "Q0": 0, "YT0": 0, "AT0": 1, "XT1": 1, "O3": 1, "Q3": 1, "YT1": 1, "AT1": 0, "XT2": 0,
        "O6": 0, "Q6": 0, "YT2": 0, "AT2": 1, "XT3": 1, "O9": 1, "Q9": 1, "YT3": 1, "AT3": 0, "R0": 1, "MT0": 1,
        "LG0": 1}


class Blk:

    def __init__(self, c, reg=None):
        self.c, self.reg = c, reg

    def __add__(self, k):
        return Blk(self.c + k, self.reg)

    @property
    def par(self):
        return self.c % 2

    @property
    def first(self):
        return self.reg is None and self.c == 0

    def at(self, n, k=0):
        return n * self.c + k if self.reg is None else self.reg * (2 * n) + (n * self.c + k)

    def half(self, n, k=0):
        return n * (self.c // 2) + k if self.reg is None else self.reg * n + (n * (self.c // 2) + k)

    def here(self, last=NB - 1):
        return self.reg is not None or 0 <= self.c <= last


def build(nc, x, ctxT, ctxR, wqT, bq, wkT, bk, wvT, bv, woT, bo, weT, be, wrT, br, out):
    top = ExitStack()
    keep = top.enter_context
    k_d = nc.dram_tensor("k_scratch", (96, 4, B, NG * CP), F16)
    vm_d = nc.dram_tensor("vm_scratch", (B, P, H * 2 * 33), F16)
    vr_d = nc.dram_tensor("vr_scratch", (B, P, 2 * NG * 4 * 33), F16)
    xs_d = nc.dram_tensor("dispatched", (ROWS, RW), F32)
    we_d = nc.dram_tensor("we_scratch", (NE, P, 2, KC, D), F16)

    tick = {}

    def sem(name, ctx=keep, prime=0):
        s = ctx(nc.semaphore(name))
        primes[name] = prime
        names[id(s)] = name
        held.append(s)
        return s

    primes, names, held = {}, {}, []

    def start_counts(e, first):
        for s in held[first:]:
            if primes[names[id(s)]]:
                e.sem_inc(s, primes[names[id(s)]])

    def wait(e, s, v):
        if isinstance(v, int) and v <= 0:
            return
        e.wait_ge(s, v + primes[names[id(s)]])
        if e is nc.sync and not isinstance(v, int):
            hold(e)

    def hold(e):
        e.sem_inc(tick[id(e)], 1)

    for nm, e in (("dve", nc.vector), ("pool", nc.gpsimd), ("sp", nc.sync)):
        tick[id(e)] = keep(nc.semaphore("tick_" + nm))

    row_t = keep(nc.sbuf_tensor("row_t", [1, MAXT + AHEAD], I32))
    exp_t = keep(nc.sbuf_tensor("exp_t", [1, MAXT + AHEAD], I32))
    ident = keep(nc.sbuf_tensor("ident", [P, P], F32))

    WN = 2 * KC * D
    we_s = keep(nc.sbuf_tensor("we_s", [P, NE * WN], F16))
    be_s = keep(nc.sbuf_tensor("be_s", [P, NE * D], F32))
    carved = [0]

    def carve(n, size):
        first = carved[0]
        carved[0] += n * size
        return we_s[:, first:carved[0]].rearrange("p (n c) -> p n c", c=size)

    attend = ExitStack()
    a = attend.enter_context
    wq_s = a(nc.sbuf_tensor("wq_s", [P, 2, KC, D], F16))
    wo_s = a(nc.sbuf_tensor("wo_s", [P, 2, KC, D], F16))
    wr_s = a(nc.sbuf_tensor("wr_s", [P, 2, KC, NE], F16))
    bqs = a(nc.sbuf_tensor("bqs", [P, NG], F32))
    bo_b = a(nc.sbuf_tensor("bo_b", [P, D], F32))
    br_b = a(nc.sbuf_tensor("br_b", [P, NE], F32))

    with ExitStack() as prep:
        t = prep.enter_context
        ctx_sb = t(nc.sbuf_tensor("ctx_sb", [P, KC, B * C], F32))
        ctr_sb = t(nc.sbuf_tensor("ctr_sb", [P, KC, P], F32))
        w_sb = {n: t(nc.sbuf_tensor("w32_" + n, [P, KC, D], F32)) for n in ("q", "o", "k", "v")}
        wr32 = t(nc.sbuf_tensor("wr32", [P, KC, NE], F32))
        bk_s = t(nc.sbuf_tensor("bk_s", [P, NG], F32))
        bv_b = t(nc.sbuf_tensor("bv_b", [P, D], F32))
        k32 = [t(nc.sbuf_tensor(f"k32_{i}", [P, B * C], F32)) for i in range(2)]
        kk = [t(nc.sbuf_tensor("k_" + n, [P, B, NG, CP], F16)) for n in ("hi", "lo")]
        v32 = [t(nc.sbuf_tensor(f"v32_{i}", [P, H, HD], F32)) for i in range(2)]
        vm = [t(nc.sbuf_tensor(f"vm_{i}", [P, H, 2, 33], F16)) for i in range(2)]
        vr = t(nc.sbuf_tensor("vr", [P, 2, H, 33], F16))
        zero = t(nc.sbuf_tensor("zero", [P, NG * 2 * 4 * 33], F16))
        kp = t(nc.psum_tensor("kp", [P, 4, 512], F32))
        vp = t(nc.psum_tensor("vp", [P, 2, 512], F32))
        L = {n: sem("ld_" + n, t) for n in ("bias", "ctx", "q", "o", "k", "v", "r")}
        p_id, p_hi, p_bk, p_kp, p_k32 = (sem(n, t) for n in ("p_id", "p_hi", "p_bk", "p_kp", "p_k32"))
        p_kh, p_kl, p_vp, p_v32, p_vh = (sem(n, t) for n in ("p_kh", "p_kl", "p_vp", "p_v32", "p_vh"))
        p_v, p_set, p_vd, p_kd, p_vz, p_lo = (sem(n, t) for n in ("p_v", "p_set", "p_vd", "p_kd", "p_vz", "p_lo"))
        p_vd2 = sem("p_vd2", t)
        block = t(nc.Block())

        @block.sync
        def _(e):
            e.dma_start(ctx_sb[:, :, :], ctxT.rearrange("(k p) n -> p k n", p=P)).then_inc(L["ctx"], 16)
            e.dma_start(ctr_sb[:, :, :], ctxR.rearrange("(k p) n -> p k n", p=P)).then_inc(L["ctx"], 16)
            for n, src in (("k", wkT), ("v", wvT), ("q", wqT), ("o", woT)):
                e.dma_start(w_sb[n][:, :, :], src.rearrange("(k p) n -> p k n", p=P)).then_inc(L[n], 16)
            wait(e, p_kh, NG)
            wait(e, p_kl, NG)
            for g in range(4):
                for part, row in ((0, 0), (1, 32), (0, 64)):
                    e.dma_start(k_d[row:row + 32, g, :, :].rearrange("r b n -> r (b n)"),
                                kk[part][32 * g:32 * g + 32, :, :, :].rearrange("r b G c -> r (b G c)")).then_inc(p_kd, 16)
            wait(e, p_vd, 16 * B // 2)
            wait(e, p_vd2, 16 * B // 2)
            wait(e, p_vz, 16 * B)
            wait(e, p_v, B + 1)
            for b in range(B):
                for g in range(4):
                    e.dma_start(vr_d[b, 32 * g:32 * g + CR, :].rearrange("r (k g c) -> r k g c", g=4, c=33)[:, :, g, :],
                                vr[32 * b:32 * b + CR, :, :, :].rearrange("r l (G g) c -> r (l G) g c", g=4)[:, :, g, :]).then_inc(p_kd, 16)
            wait(e, p_kd, 16 * (12 + 4 * B))

        @block.gpsimd
        def _(e):
            e.memset(ident[:, :], 0.0).then_inc(p_id, 1)
            e.memset(zero[:, :], 0.0).then_inc(p_set, 1)
            for n, tile in enumerate(vm):
                e.memset(tile[:, :, 0, 32:33], 1.0).then_inc(p_set, 1)
                e.memset(tile[:, :, 1, 32:33], 0.0).then_inc(p_set, 1)
            e.memset(vr[:, 0, :, 32:33], 1.0).then_inc(p_set, 1)
            e.memset(vr[:, 1, :, 32:33], 0.0).then_inc(p_set, 1)
            wait(e, p_id, 1)
            e.affine_select(out=ident[:, :], in_=ident[:, :], compare_op=ALU.not_equal, fill=1.0, base=0,
                            pattern=[[-1, P]], channel_multiplier=1).then_inc(p_id, 1)

        @block.scalar
        def _(e):
            e.dma_start(bk_s[:, :], bk).then_inc(L["bias"], 16)
            e.dma_start(bqs[:, :], bq).then_inc(L["bias"], 16)
            e.dma_start(bv_b[:, :], bv.rearrange("(a n) -> a n", a=1).broadcast_to([P, D])).then_inc(L["bias"], 16)
            e.dma_start(bo_b[:, :], bo.rearrange("(a n) -> a n", a=1).broadcast_to([P, D])).then_inc(L["bias"], 16)
            e.dma_start(br_b[:, :], br.rearrange("(a n) -> a n", a=1).broadcast_to([P, NE])).then_inc(L["bias"], 16)
            e.dma_start(wr32[:, :, :], wrT.rearrange("(k p) n -> p k n", p=P)).then_inc(L["r"], 16)
            wait(e, p_set, 7)
            for b in range(B):
                e.dma_start(vr_d[b, :, :], zero[:, :]).then_inc(p_vz, 16)
            wait(e, p_bk, 1)
            for G in range(NG):
                wait(e, p_kp, G + 1)
                if G >= 2:
                    wait(e, p_kl, G - 1)
                e.activation(k32[G % 2][:, :].rearrange("p (a n) -> p a n", a=2), kp[:, 2 * (G % 2):2 * (G % 2) + 2, 0:2 * C],
                             ACT.Identity, bias=bk_s[:, G:G + 1], scale=KS).then_inc(p_k32, 1)
            for n, (w, dst, scale) in enumerate(((w_sb["q"], wq_s, WS1), (w_sb["o"], wo_s, WS), (wr32, wr_s, WS))):
                wait(e, L["qor"[n]], 16)
                e.activation(dst[:, 0, :, :], w[:, :, :], ACT.Copy, scale=scale).then_inc(p_hi, 1)
            for b in range(B):
                wait(e, p_v, b + 1)
                e.dma_start(vm_d[b, :, :], vm[b % 2][:, :, :, :].rearrange("p h l c -> p (h l c)")).then_inc((p_vd, p_vd2)[b % 2], 16)

        @block.vector
        def _(e):
            wait(e, L["bias"], 80)
            e.tensor_scalar(bk_s[:, :], bk_s[:, :], KS, None, ALU.mult).then_inc(p_bk, 1)
            e.tensor_scalar(bqs[:, :], bqs[:, :], QS, None, ALU.mult).then_inc(p_bk, 1)
            e.tensor_scalar(bv_b[:, :], bv_b[:, :], VS, None, ALU.mult).then_inc(p_bk, 1)
            for G in range(NG):
                wait(e, p_k32, G + 1)
                k4 = k32[G % 2][:, :].rearrange("p (b c) -> p b c", b=B)
                e.tensor_copy(kk[0][:, :, G, 0:C], k4).then_inc(p_lo, 1)
                wait(e, p_lo, 2 * G + 1)
                e.tensor_tensor(kk[1][:, :, G, 0:C], k4, kk[0][:, :, G, 0:C], ALU.subtract).then_inc(p_lo, 1)
                wait(e, p_lo, 2 * G + 2)
                e.tensor_copy(kk[0][:, :, G, C:CP], kk[0][:, :, G, P:P + CP - C]).then_inc(p_kh, 1)
                e.tensor_copy(kk[1][:, :, G, C:CP], kk[1][:, :, G, P:P + CP - C]).then_inc(p_kl, 1)
            wait(e, p_set, 7)
            wait(e, p_bk, 3)
            for b in range(B + 1):
                wait(e, p_vp, b + 1)
                if b >= 2:
                    wait(e, (p_vd, p_vd2)[b % 2], 16 * (b // 2))
                e.scalar_tensor_tensor(v32[b % 2][:, :, :].rearrange("p h d -> p (h d)"), vp[:, b % 2, :], VS, bv_b[:, :],
                                       ALU.mult, ALU.add).then_inc(p_v32, 1)
                wait(e, p_v32, b + 1)
                hi, lo = (vm[b % 2][:, :, 0, 0:HD], vm[b % 2][:, :, 1, 0:HD]) if b < B else (vr[:, 0, :, 0:HD], vr[:, 1, :, 0:HD])
                e.tensor_copy(hi, v32[b % 2][:, :, :]).then_inc(p_vh, 1)
                wait(e, p_vh, b + 1)
                e.tensor_tensor(lo, v32[b % 2][:, :, :], hi, ALU.subtract).then_inc(p_v, 1)
                wait(e, p_v, b + 1)
            for n, (w, dst, scale) in enumerate(((w_sb["q"], wq_s, WS1), (w_sb["o"], wo_s, WS), (wr32, wr_s, WS))):
                wait(e, p_hi, n + 1)
                e.scalar_tensor_tensor(dst[:, 1, :, :].rearrange("p k n -> p (k n)"), w[:, :, :].rearrange("p k n -> p (k n)"), scale,
                                       dst[:, 0, :, :].rearrange("p k n -> p (k n)"), ALU.mult, ALU.subtract).then_inc(p_bk, 1)

        @block.tensor
        def _(e):
            wait(e, L["ctx"], 32)
            wait(e, L["k"], 16)
            for G in range(NG):
                if G >= 2:
                    wait(e, p_k32, G - 1)
                for half in range(2):
                    for k in range(KC):
                        m = e.matmul(kp[:, 2 * (G % 2) + half, 0:2 * C], w_sb["k"][:, k, G * P:(G + 1) * P],
                                     ctx_sb[:, k, half * 2 * C:(half + 1) * 2 * C], start=(k == 0), stop=(k == KC - 1))
                m.then_inc(p_kp, 1)
            wait(e, L["v"], 16)
            for b in range(B + 1):
                if b >= 2:
                    wait(e, p_v32, b - 1)
                for k in range(KC):
                    lhs = ctx_sb[:, k, b * C:b * C + P] if b < B else ctr_sb[:, k, :]
                    m = e.matmul(vp[:, b % 2, :], lhs, w_sb["v"][:, k, :], start=(k == 0), stop=(k == KC - 1))
                m.then_inc(p_vp, 1)

    xA = [be_s[:, i * NJ * D:(i + 1) * NJ * D].rearrange("p (j d) -> p j d", d=D) for i in range(2)]
    xR = [a(nc.sbuf_tensor(f"xR{i}", [P, NJ, D], F32)) for i in range(2)]
    xn1 = a(nc.sbuf_tensor("xn1", [P, NJ, D], F32))
    xnT = [carve(KC, TB), a(nc.sbuf_tensor("xnT_lo", [P, KC, TB], F16))]
    qs = [carve(NG, TB) for _ in range(2)]
    Qst = [carve(H, TB) for _ in range(2)]
    Kst = [a(nc.sbuf_tensor(f"Kst{i}", [97, H, CP], F16)) for i in range(2)]
    Vm = [a(nc.sbuf_tensor(f"Vm{i}", [P, H, 2, 33], F16)) for i in range(2)]
    Vr = [a(nc.sbuf_tensor(f"Vr{i}", [P, 2, NG, 4 * 33], F16)) for i in range(2)]
    mx_sb = a(nc.sbuf_tensor("mx_sb", [P, NJ * H], F32))
    mT = a(nc.sbuf_tensor("mT", [H, TB], F16))
    P32 = [a(nc.sbuf_tensor(f"P32_{i}", [P, 2, TB], F32)) for i in range(2)]
    Pst = [carve(10, TB) for _ in range(2)]
    assert carved[0] == NE * WN
    att = a(nc.sbuf_tensor("att", [P, NJ, H, HD], F32))
    aT = [a(nc.sbuf_tensor("aT_" + n, [P, KC, TB], F16)) for n in ("hi", "lo")]
    xn2 = [a(nc.sbuf_tensor(f"xn2_{i}", [P, NJ, RW], F32)) for i in range(2)]
    x2T = [a(nc.sbuf_tensor("x2T_" + n, [P, KC, TB], F16)) for n in ("hi", "lo")]
    rcp = a(nc.sbuf_tensor("rcp", [P, 2, 2, 4], F32))
    stats = [a(nc.sbuf_tensor(f"stats{i}", [P, NJ, 6], F32)) for i in range(2)]
    aggr = [a(nc.sbuf_tensor(f"aggr{i}", [P, NJ, 2], F32)) for i in range(2)]
    nrm = [a(nc.sbuf_tensor(f"nrm{i}", [P, 7, NJ], F32)) for i in range(2)]
    lg = a(nc.sbuf_tensor("lg", [P, NJ, NE + 1], F32))
    top8 = a(nc.sbuf_tensor("top8", [P, NJ, 8], F32))
    topi = a(nc.sbuf_tensor("topi", [P, NJ, 8], U32))
    topf = a(nc.sbuf_tensor("topf", [P, TOPK, NJ], F32))
    lgd = a(nc.sbuf_tensor("lgd", [P, NJ, NE + 1], F32))
    ex9 = a(nc.sbuf_tensor("ex9", [P, NJ, NE + 1], F32))
    sm = a(nc.sbuf_tensor("sm", [P, 2, NJ], F32))
    wts = [a(nc.sbuf_tensor(f"wts{i}", [P, TOPK, NJ], F32)) for i in range(2)]
    tok = a(nc.sbuf_tensor("tok", [P, NJ], F32))
    wst = a(nc.sbuf_tensor("wst", [P, 2 * D], F32))
    zrow = wst[:, 0:RW]
    wsp = a(nc.sbuf_tensor("wsp", [P, 2, 2 * D], F16))
    io8 = a(nc.sbuf_tensor("io8", [P, NJ, NE], F32))
    oneh = a(nc.sbuf_tensor("oneh", [P, TOPK, NJ, NE], F32))
    msk = a(nc.sbuf_tensor("msk", [P, NJ, NE], F16))
    posb = a(nc.sbuf_tensor("posb", [P, NJ, NE], F32))
    seld = a(nc.sbuf_tensor("seld", [P, TOPK, NJ, NE], F32))
    idf = a(nc.sbuf_tensor("idf", [P, TOPK, NJ], F32))
    idx = [a(nc.sbuf_tensor(f"idx{i}", [P, TOPK * NJ], I32)) for i in range(2)]
    base = a(nc.sbuf_tensor("base", [P, NE], F32))
    tri = a(nc.sbuf_tensor("tri", [P, P], F16))
    ones = a(nc.sbuf_tensor("ones", [P, P], F16))
    baseI = a(nc.sbuf_tensor("baseI", [1, NE], I32))
    NT = MAXT + AHEAD
    tile_no = a(nc.sbuf_tensor("tile_no", [1, NT], F32))
    tb = a(nc.sbuf_tensor("tb", [P, 6, NE], F32))
    tbi = a(nc.sbuf_tensor("tbi", [P, 2, NE], I32))
    tg = att[0:1, :, :, :].rearrange("p j h d -> p (j h d)")[:, 0:NT * NE].rearrange("p (n e) -> p n e", e=NE)
    te = a(nc.sbuf_tensor("te", [1, 3, NT], F32))

    S = a(nc.psum_tensor("S", [P, 4, 512], F32))
    PVp = a(nc.psum_tensor("PVp", [P, 2, 512], F32))
    W = a(nc.psum_tensor("W", [P, 2, 512], F32))

    def s_(name, prime=0):
        return sem(name, a, prime)

    attend_sems = len(held)
    g_set = s_("g_set")
    ld_xA = [s_(f"ld_xA{i}") for i in range(2)]
    ld_xR = [s_(f"ld_xR{i}") for i in range(2)]
    ld_kv = [s_(f"ld_kv{i}") for i in range(2)]
    restack = [s_(f"restack{i}") for i in range(2)]
    mrow = [s_(f"mrow{i}") for i in range(2)]
    st_x1 = [s_(f"st_x1_{i}") for i in range(2)]
    scat = [[s_(f"scat{i}_{k}") for k in range(TOPK)] for i in range(2)]
    zset, ld_ew = s_("zset"), s_("ld_ew")
    ld_we, wech, st_we, wcol = s_("ld_we"), s_("wech"), s_("st_we"), s_("wcol")
    nch = [s_(f"nch{i}") for i in range(2)]
    nvar = [s_(f"nvar{i}") for i in range(2)]
    nln = [s_(f"nln{i}") for i in range(2)]
    nrs = [s_(f"nrs{i}") for i in range(2)]
    nap = [s_(f"nap{i}") for i in range(2)]
    xrb = s_("xrb")
    t1p, t1h, t1e = s_("t1p"), s_("t1h"), s_("t1e")
    qp, qhe, qle = s_("qp"), s_("qhe"), s_("qle")
    mxp, mxr, mtp, mte = s_("mxp"), s_("mxr"), s_("mtp"), s_("mte")
    stp, exd, phd, pld = s_("stp"), s_("exd"), s_("phd"), s_("pld")
    pvt, rcd, nmd = s_("pvt"), s_("rcd"), s_("nmd")
    atp, ath, ate = s_("atp"), s_("ath"), s_("ate")
    op_, x1s = s_("op_"), s_("x1s")
    t2p, t2h, t2e = s_("t2p"), s_("t2h"), s_("t2e")
    lgp, lge, rch, rex = s_("lgp"), s_("lge"), s_("rch"), s_("rex")
    rcd2, mskd, rp, rev, ridx = s_("rcd2"), s_("mskd"), s_("rp"), s_("rev"), s_("ridx")
    tbd, tbz, zst = s_("tbd"), s_("tbz"), s_("zst")

    class Chain:

        def __init__(self, e, s, blk, n):
            self.e, self.s, self.blk, self.n, self.k = e, s, blk, n, 0

        def do(self, ins):
            ins.then_inc(self.s, 1)
            self.k += 1

        def sync(self):
            wait(self.e, self.s, self.blk.at(self.n, self.k))

        def end(self):
            assert self.k == self.n, (self.k, self.n)

    NCH = 2 * NJ + 6

    def dve_norm_stats(e, n, src, j):
        e.bn_stats(stats[n][:, j, :], src[:, j, :]).then_inc(nch[n], 1)

    def dve_norm_var(e, n, b):
        ch = Chain(e, nch[n], b, NCH)
        ch.k = NJ
        ch.sync()
        hold(e)
        for j in range(NJ):
            ch.do(e.bn_aggr(aggr[n][:, j, :], stats[n][:, j, :]))
        ch.sync()
        ch.do(e.tensor_scalar(nrm[n][:, 0, :], aggr[n][:, :, 1], EPS, None, ALU.add))
        ch.sync()
        e.tensor_copy(nrm[n][:, 1, :], nrm[n][:, 0, :]).then_inc(nvar[n], 1)

    def dve_norm_coef(e, n, b, scale):
        v = nrm[n]
        ch = Chain(e, nch[n], b, NCH)
        ch.k = 2 * NJ + 1
        wait(e, nrs[n], b.at(1, 1))
        ch.do(e.tensor_tensor(v[:, 3, :], v[:, 2, :], v[:, 2, :], ALU.mult))
        ch.sync()
        ch.do(e.tensor_tensor(v[:, 4, :], v[:, 3, :], v[:, 0, :], ALU.mult))
        ch.sync()
        ch.do(e.tensor_scalar(v[:, 3, :], v[:, 4, :], -0.5 * scale, 1.5 * scale, ALU.mult, ALU.add))
        ch.sync()
        wait(e, nap[n], b.at(1))
        ch.do(e.tensor_tensor(v[:, 5, :], v[:, 3, :], v[:, 2, :], ALU.mult))
        ch.sync()
        ch.do(e.scalar_tensor_tensor(v[:, 6, :], aggr[n][:, :, 0], -1.0, v[:, 5, :], ALU.mult, ALU.mult))
        ch.end()

    def act_norm(e, n, b):
        wait(e, nvar[n], b.at(1, 1))
        e.activation(nrm[n][:, 1, :], nrm[n][:, 1, :], ACT.Ln).then_inc(nln[n], 1)
        wait(e, nln[n], b.at(1, 1))
        e.activation(nrm[n][:, 2, :], nrm[n][:, 1, :], ACT.Exp, scale=-0.5).then_inc(nrs[n], 1)

    def pool_norm_apply(e, n, b, src, dst):
        wait(e, nch[n], b.at(NCH, NCH))
        hold(e)
        for j in range(NJ):
            i = e.tensor_scalar(dst[:, j, :], src[:, j, :], nrm[n][:, 5, j:j + 1], nrm[n][:, 6, j:j + 1], ALU.mult, ALU.add)
        i.then_inc(nap[n], 1)

    wprev = {0: None, 1: None}

    def w_take(e, bank, slot, seq, s, n, k, off):
        if wprev[bank] is not None:
            s0, n0, k0, off0, seq0 = wprev[bank]
            wait(e, s0, (slot + (off0 - (seq - seq0))).at(n0, k0))
        wprev[bank] = (s, n, k, off, seq)

    def w_skip(n):
        for bank in range(2):
            wprev[bank] = (*wprev[bank][:4], wprev[bank][4] + n)

    def pe_T(e, step, b, slot, seq, src, i, done, ev):
        w_take(e, BANK[step], slot, seq, ev, 4, i + 1, b.c - slot.c)
        for j in range(NJ):
            m = e.transpose(W[:, BANK[step], j * P:(j + 1) * P], src(j, i), ident[:, :])
        m.then_inc(done, 1)

    def split3(k):
        return ((0, 0, k), (1, 0, k), (0, 1, k))

    def pe_XT(e, b, i, slot, seq):
        if i == 0:
            wait(e, nap[0], b.at(1, 1))
        pe_T(e, f"XT{i}", b, slot, seq, lambda j, k: xn1[:, j, k * P:(k + 1) * P], i, t1p, t1e)

    def pe_Q(e, b, i, slot, seq):
        G, part = i // 3, i % 3
        bank = BANK[f"Q{3 * G}"]
        if i == 0:
            wait(e, t1e, b.at(4, 4))
        if part == 0:
            w_take(e, bank, slot, seq, qle, 4, G + 1, b.c - slot.c)
        seqs = [t for k in range(KC) for t in split3(k)]
        for n in range(4 * part, 4 * part + 4):
            wp, xp, k = seqs[n]
            m = e.matmul(W[:, bank, :], wq_s[:, wp, k, G * P:(G + 1) * P], xnT[xp][:, k, :], start=(n == 0), stop=(n == 11))
        if part == 2:
            m.then_inc(qp, 1)

    def pe_MX(e, b, n, slot, seq):
        p = b.par
        if n == 0:
            wait(e, restack[p], b.half(192, 192))
            wait(e, ld_kv[p], b.half(48, 48))
        if n < 2:
            wait(e, exd, b.at(10, n - 1))
        else:
            wait(e, mxr, b.at(11, n - 1))
        for u in range(6 * n, min(6 * n + 6, NJ * H)):
            j, h = u // H, u % H
            m = e.matmul(S[:, 2 * (n % 2) + u % 6 // 3, (u % 3) * C:(u % 3 + 1) * C], Qst[p][0:96, h, j * P:(j + 1) * P],
                         Kst[p][0:96, 4 * (h % 4) + h // 4, 0:C], start=True, stop=True)
        m.then_inc(mxp, 1)

    def pe_O(e, b, i, slot, seq):
        j, part = i // 3, i % 3
        bank = BANK[f"O{3 * j}"]
        if i == 0:
            wait(e, ate, b.at(4, 4))
        if part == 0:
            w_take(e, bank, slot, seq, x1s, 4, j + 1, b.c - slot.c)
        seqs = [t for k in range(KC) for t in split3(k)]
        for n in range(4 * part, 4 * part + 4):
            ap, wp, k = seqs[n]
            m = e.matmul(W[:, bank, :], aT[ap][:, k, j * P:(j + 1) * P], wo_s[:, wp, k, :], start=(n == 0), stop=(n == 11))
        if part == 2:
            m.then_inc(op_, 1)

    def pe_MT(e, b, i, slot, seq):
        wait(e, mxr, b.at(11, 11))
        bank = BANK["MT0"]
        w_take(e, bank, slot, seq, mte, 1, 1, b.c - slot.c)
        for j in range(NJ):
            m = e.transpose(W[0:H, bank, j * P:(j + 1) * P], mx_sb[:, j * H:(j + 1) * H], ident[:, :])
        m.then_inc(mtp, 1)

    def pe_R(e, b, i, slot, seq):
        if b.first:
            wait(e, g_set, 5)
        bank = BANK["R0"]
        wait(e, mskd, b.at(1, 1))
        w_take(e, bank, slot, seq, rev, 1, 1, b.c - slot.c)
        mm = msk[:, :, :].rearrange("p j e -> p (j e)")
        e.matmul(W[:, bank, 0:NJ * NE], tri[:, :], mm, start=True, stop=False)
        for d in range(1, NJ):
            m = e.matmul(W[:, bank, d * NE:NJ * NE], ones[:, :], mm[:, 0:(NJ - d) * NE], start=False, stop=(d == NJ - 1))
        for j in range(NJ):
            m = e.matmul(W[:, bank, NJ * NE:(NJ + 1) * NE], ones[:, :], mm[:, j * NE:(j + 1) * NE], start=(j == 0), stop=(j == NJ - 1))
        m.then_inc(rp, 1)

    def pe_ST(e, b, n, slot, seq):
        p = b.par
        if b.first and n == 0:
            wait(e, g_set, 5)
        if n == 0:
            wait(e, mrow[p], b.half(16, 16))
        if n < 2:
            wait(e, mxr, b.at(11, 11))
        else:
            wait(e, exd, b.at(10, n - 1))
        for u in (2 * n, 2 * n + 1):
            G, r, bank = u // 5, u % 5, 2 * (n % 2) + u % 2
            if r < 4:
                m = e.matmul(S[:, bank, :], Kst[p][0:97, 4 * r + G, 0:P], Qst[p][0:97, 4 * G + r, :], start=True, stop=True)
            else:
                for g in range(4):
                    m = e.matmul(S[32 * g:32 * g + 32, bank, :], Kst[p][0:97, 4 * g + G, P:CP], Qst[p][0:97, 4 * G + g, :],
                                 start=True, stop=True)
        m.then_inc(stp, 1)

    def pe_PV(e, b, w, slot, seq):
        p, G, q = b.par, w // 2, w % 2
        wait(e, pld, b.at(10, (5 * G + 4) // 2 + 1))
        wait(e, nmd, b.at(8, w - 1))
        for jj in range(2):
            j = 2 * q + jj
            tok = slice(j * P, (j + 1) * P)
            o = PVp[:, q, jj * 132:(jj + 1) * 132]
            for n, (pp, vv) in enumerate(((0, 0), (0, 1), (1, 0))):
                e.matmul(o, Pst[pp][:, (5 * G + 4) % 10, tok], Vr[p][:, vv, G, :], start=(n == 0), stop=(n == 2))
            for g in range(4):
                for pp, vv in ((0, 0), (0, 1), (1, 0)):
                    m = e.matmul(o[:, g * 33:(g + 1) * 33], Pst[pp][:, (5 * G + g) % 10, tok], Vm[p][:, 4 * G + g, vv, :],
                                 start=False, stop=True, skip_group_check=True)
        m.then_inc(pvt, 1)

    def pe_AT(e, b, G, slot, seq):
        wait(e, nmd, b.at(8, 2 * G + 2))
        pe_T(e, f"AT{G}", b, slot, seq, lambda j, k: att[:, j, 4 * k:4 * k + 4, :].rearrange("p h d -> p (h d)"), G, atp, ate)

    def pe_YT(e, b, i, slot, seq):
        if i == 0:
            wait(e, nap[1], b.at(1, 1))
        pe_T(e, f"YT{i}", b, slot, seq, lambda j, k: xn2[b.par][:, j, k * P:(k + 1) * P], i, t2p, t2e)

    def pe_LG(e, b, i, slot, seq):
        bank = BANK["LG0"]
        wait(e, t2e, b.at(4, 4))
        w_take(e, bank, slot, seq, lge, 1, 1, b.c - slot.c)
        for j in range(NJ):
            seqs = [t for k in range(KC) for t in split3(k)]
            for n, (xp, wp, k) in enumerate(seqs):
                m = e.matmul(W[:, bank, j * NE:(j + 1) * NE], x2T[xp][:, k, j * P:(j + 1) * P], wr_s[:, wp, k, :],
                             start=(n == 0), stop=(n == 11))
        m.then_inc(lgp, 1)

    def act_hi(e, b, i, step, dst, done, free, hi_sem, bias=None):
        wait(e, done, b.at(4, i + 1))
        if i == 0:
            free()
        if bias is None:
            e.activation(dst[:, i, :], W[:, BANK[step], :], ACT.Copy).then_inc(hi_sem, 1)
        else:
            e.activation(dst[:, i, :], W[:, BANK[step], :], ACT.Identity, bias=bias).then_inc(hi_sem, 1)

    def act_XTh(e, b, i):
        act_hi(e, b, i, f"XT{i}", xnT[0], t1p, lambda: wait(e, qp, b.at(4)), t1h)

    def act_Qh(e, b, G):
        act_hi(e, b, G, f"Q{3 * G}", qs[0], qp, lambda: wait(e, restack[1 - b.par], (b + -1).half(192, 192)), qhe, bqs[:, G:G + 1])

    def act_YTh(e, b, i):
        act_hi(e, b, i, f"YT{i}", x2T[0], t2p, lambda: wait(e, lgp, b.at(1)), t2h)

    def act_ATh(e, b, i):
        act_hi(e, b, i, f"AT{i}", aT[0], atp, lambda: wait(e, op_, b.at(4)), ath)
        if b.reg is None and b.c == NB - 1 and i == KC - 1:
            wait(e, pvt, 8 * NB)
            wait(e, st_we, 16 * NB)
            wait(e, nap[0], NB)
            for n in range(NE):
                e.dma_start(we_s[:, n * WN:(n + 1) * WN], we_d[n].rearrange("p l k n -> p (l k n)")).then_inc(ld_ew, 16)
            e.dma_start(be_s[:, :], be.rearrange("(a e) n -> a (e n)", a=1).broadcast_to([P, NE * D])).then_inc(ld_ew, 16)

    def act_EX(e, b, n):
        wait(e, stp, b.at(10, n + 1))
        wait(e, pld, b.at(10, n - 1))
        e.activation(P32[n % 2][:, :, :], S[:, 2 * (n % 2):2 * (n % 2) + 2, :], ACT.Exp, scale=1.0 / (SS * ROOT)).then_inc(exd, 1)

    def act_PH(e, b, n):
        wait(e, exd, b.at(10, n + 1))
        done = (2 * n - 9) // 5 if n >= 5 else (2 * n + 11) // 5 - 4
        wait(e, pvt, b.at(8, 2 * done + 2))
        r = 2 * (n % 5)
        e.activation(Pst[0][:, r:r + 2, :], P32[n % 2][:, :, :], ACT.Copy).then_inc(phd, 1)

    def act_RX(e, b, i):
        wait(e, rch, b.at(RCH, RCH))
        e.activation(ex9[:, :, :], lgd[:, :, :], ACT.Exp).then_inc(rex, 1)

    def dve_lo(e, b, i, step, dst, hi, hi_sem, ev):
        wait(e, hi_sem, b.at(4, i + 1))
        e.tensor_tensor(dst[:, i, :], W[:, BANK[step], :], hi[:, i, :], ALU.subtract).then_inc(ev, 1)

    def dve_Ql(e, b, G):
        wait(e, qhe, b.at(4, G + 1))
        e.scalar_tensor_tensor(qs[1][:, G, :], W[:, BANK[f"Q{3 * G}"], :], bqs[:, G:G + 1], qs[0][:, G, :], ALU.add, ALU.subtract).then_inc(qle, 1)

    def dve_DMX(e, b, n):
        wait(e, mxp, b.at(11, n + 1))
        if n == 0:
            wait(e, mtp, b.at(1))
        k = 3 if n < 10 else 2
        if n < 10:
            e.tensor_reduce(mx_sb[:, 6 * n:6 * n + 6].rearrange("p (a k) -> p a k", a=2),
                            S[:, 2 * (n % 2):2 * (n % 2) + 2, 0:3 * C].rearrange("p a (k c) -> p a k c", c=C),
                            AX, ALU.max).then_inc(mxr, 1)
        else:
            e.tensor_reduce(mx_sb[:, 60:63], S[:, 0, 0:3 * C].rearrange("p (k c) -> p k c", c=C), AX, ALU.max)
            e.tensor_reduce(mx_sb[:, 63:64], S[:, 1, 0:C], AX, ALU.max).then_inc(mxr, 1)

    def dve_Oe(e, b, j):
        wait(e, op_, b.at(4, j + 1))
        if j == 0:
            wait(e, xrb, b.at(1, 1))
        e.scalar_tensor_tensor(xR[b.par][:, j, :], W[:, BANK[f"O{3 * j}"], :], OSC, xR[b.par][:, j, :], ALU.mult, ALU.add).then_inc(x1s, 1)

    def dve_MTe(e, b, i):
        wait(e, mtp, b.at(1, 1))
        wait(e, mrow[1 - b.par], (b + -1).half(16, 16))
        e.tensor_scalar(mT[:, :], W[0:H, BANK["MT0"], :], 1.0 / SS, MSHIFT, ALU.mult, ALU.subtract).then_inc(mte, 1)

    RCH = 4 + 8 + 1

    def dve_RT(e, b, i):
        if b.first:
            wait(e, g_set, 9)
        ch = Chain(e, rch, b, RCH)
        wait(e, lgp, b.at(1, 1))
        wait(e, rcd2, b.at(RC2))
        e.scalar_tensor_tensor(lg[:, :, 0:NE], W[:, BANK["LG0"], 0:NJ * NE].rearrange("p (j e) -> p j e", e=NE), ESC,
                               br_b[:, :].rearrange("p (o e) -> p o e", o=1).broadcast_to([P, NJ, NE]),
                               ALU.mult, ALU.add).then_inc(lge, 1)
        wait(e, lge, b.at(1, 1))
        hold(e)
        for j in range(NJ):
            ch.do(e.max(top8[:, j, :], lg[:, j, 0:NE]))
        ch.sync()
        hold(e)
        for j in range(NJ):
            ch.do(e.max_index(topi[:, j, :], top8[:, j, :], lg[:, j, 0:NE]))
        ch.do(e.tensor_copy(lg[:, :, NE:NE + 1], top8[:, :, 1:2]))
        ch.sync()
        ch.do(e.tensor_tensor(lgd[:, :, :], lg[:, :, :], top8[:, :, 0:1].broadcast_to([P, NJ, NE + 1]), ALU.subtract))
        ch.do(e.tensor_copy(topf[:, :, :].rearrange("p k j -> p j k"), topi[:, :, 0:TOPK]))
        ch.sync()
        for k in range(TOPK):
            ch.do(e.tensor_tensor(oneh[:, k, :, :], io8[:, :, :],
                                  topf[:, k, :].rearrange("p (j o) -> p j o", o=1).broadcast_to([P, NJ, NE]), ALU.is_equal))
        ch.sync()
        ch.end()
        e.tensor_tensor(msk[:, :, :], oneh[:, 0, :, :], oneh[:, 1, :, :], ALU.add).then_inc(mskd, 1)

    RC2 = 10

    def dve_RR(e, b, _):
        p = b.par
        ch = Chain(e, rcd2, b, RC2)
        wait(e, rp, b.at(1, 1))
        wait(e, rev, b.at(1))
        ch.do(e.tensor_tensor(posb[:, :, :], W[:, BANK["R0"], 0:NJ * NE].rearrange("p (j e) -> p j e", e=NE),
                              base[:, :].rearrange("p (o e) -> p o e", o=1).broadcast_to([P, NJ, NE]), ALU.add))
        ch.sync()
        e.tensor_tensor(base[:, :], base[:, :], W[:, BANK["R0"], NJ * NE:(NJ + 1) * NE], ALU.add).then_inc(rev, 1)
        for k in range(TOPK):
            i = e.tensor_tensor(seld[:, k, :, :], oneh[:, k, :, :], posb[:, :, :], ALU.mult)
            ch.do(i)
        wait(e, rex, b.at(1, 1))
        for k in range(TOPK):
            wait(e, scat[p][k], b.half(64))
        ch.do(e.tensor_reduce(sm[:, 0, :], ex9[:, :, 0:NE], AX, ALU.add))
        ch.sync()
        ch.do(e.tensor_reduce(idf[:, :, :], seld[:, :, :, :], AX, ALU.add))
        ch.do(e.reciprocal(wts[p][:, 0, :], sm[:, 0, :]))
        ch.sync()
        ch.do(e.tensor_tensor(wts[p][:, 1, :], wts[p][:, 0, :], ex9[:, :, NE], ALU.mult))
        ch.do(e.tensor_copy(xn2[p][:, :, D:D + 1], wts[p][:, 0, :].rearrange("p (j o) -> p j o", o=1)))
        ch.do(e.tensor_copy(xn2[p][:, :, D + 1:RW], tok[:, :].rearrange("p (j o) -> p j o", o=1)))
        ch.sync()
        ch.do(e.tensor_scalar(tok[:, :], tok[:, :], float(TB), None, ALU.add))
        e.tensor_copy(idx[p][:, :], idf[:, :, :].rearrange("p k j -> p (k j)")).then_inc(ridx, 1)
        ch.end()

    def dve_SA(e, b, j):
        if j == 0:
            wait(e, ld_xA[b.par], b.half(16, 16))
        dve_norm_stats(e, 0, xA[b.par], j)

    def dve_SN(e, b, j):
        wait(e, x1s, b.at(4, j + 1))
        dve_norm_stats(e, 1, xR[b.par], j)

    def dve_PL(e, b, n):
        wait(e, phd, b.at(10, n + 1))
        r = 2 * (n % 5)
        e.tensor_tensor(Pst[1][:, r:r + 2, :], P32[n % 2][:, :, :], Pst[0][:, r:r + 2, :], ALU.subtract).then_inc(pld, 1)

    def dve_NM(e, b, w):
        G, q = w // 2, w % 2
        wait(e, pvt, b.at(8, w + 1))
        if w == 0:
            wait(e, atp, b.at(4))
        src = PVp[:, q, 0:264].rearrange("p (j g c) -> p j g c", j=2, c=33)
        e.reciprocal(rcp[:, q, :, :], src[:, :, :, HD]).then_inc(rcd, 1)
        wait(e, rcd, b.at(8, w + 1))
        e.tensor_tensor(att[:, 2 * q:2 * q + 2, 4 * G:4 * G + 4, :], src[:, :, :, 0:HD],
                        rcp[:, q, :, :].rearrange("p j (g o) -> p j g o", o=1).broadcast_to([P, 2, 4, HD]), ALU.mult).then_inc(nmd, 1)

    def tables(e):
        k = [0]

        def do(ins):
            ins.then_inc(tbd, 1)
            k[0] += 1
            wait(e, tbd, k[0])

        reg0, cnt, nt, cum, first, tmp = (tb[:, i, :] for i in range(6))
        row = lambda v: v[0:1, :]
        wide = lambda v: v.rearrange("p (o e) -> p o e", o=1).broadcast_to([1, NT, NE])
        deep = lambda v: v.rearrange("p (n o) -> p n o", o=1).broadcast_to([1, NT, NE])
        wait(e, rev, NB)
        e.tensor_copy(baseI[:, :], base[0:1, :]).then_inc(tbz, 1)
        do(e.tensor_scalar(reg0, io8[:, 0, :], float(REGION), None, ALU.mult))
        do(e.tensor_tensor(cnt, base[:, :], reg0, ALU.subtract))
        do(e.tensor_scalar(tbi[:, 0, :], cnt, float(TILE - 1), None, ALU.add))
        do(e.tensor_scalar(tbi[:, 1, :], tbi[:, 0, :], TILE.bit_length() - 1, None, ALU.arith_shift_right))
        do(e.tensor_copy(nt, tbi[:, 1, :]))
        do(e.tensor_copy(cum, nt))
        for n in range(1, NE):
            do(e.tensor_tensor(cum[:, n:n + 1], cum[:, n - 1:n], nt[:, n:n + 1], ALU.add))
        do(e.scalar_tensor_tensor(tmp, cum, -float(TILE), reg0, ALU.mult, ALU.add))
        do(e.scalar_tensor_tensor(first, nt, float(TILE), tmp, ALU.mult, ALU.add))
        do(e.tensor_tensor(tg[:, :, :], deep(tile_no[:, :]), wide(row(cum)), ALU.is_ge))
        do(e.tensor_reduce(te[:, 0, :], tg[:, :, :], AX, ALU.add))
        do(e.tensor_tensor(tg[:, :, :], wide(io8[0:1, 0, :]), deep(te[:, 0, :]), ALU.is_equal))
        do(e.tensor_tensor(tg[:, :, :], tg[:, :, :], wide(row(first)), ALU.mult))
        do(e.tensor_reduce(te[:, 1, :], tg[:, :, :], AX, ALU.add))
        do(e.tensor_scalar(te[:, 2, :], te[:, 0, :], NE - 0.5, float(SPARE), ALU.is_ge, ALU.mult))
        do(e.tensor_tensor(te[:, 1, :], te[:, 1, :], te[:, 2, :], ALU.add))
        do(e.scalar_tensor_tensor(te[:, 2, :], tile_no[:, :], float(TILE), te[:, 1, :], ALU.mult, ALU.add))
        do(e.tensor_scalar(te[:, 2, :], te[:, 2, :], float(SPARE), None, ALU.min))
        do(e.tensor_copy(row_t[:, :], te[:, 2, :]))
        do(e.tensor_scalar(exp_t[:, :], te[:, 0, :], float(NE - 1), None, ALU.min))

    def pool_XB(e, b, _):
        p = b.par
        wait(e, ld_xR[p], b.half(16, 16))
        hold(e)
        for j in range(NJ):
            i = e.tensor_tensor(xR[p][:, j, :], xR[p][:, j, :], bo_b[:, :], ALU.add)
        i.then_inc(xrb, 1)

    def pool_NA(e, b, n):
        if n:
            for k in range(TOPK):
                wait(e, scat[b.par][k], b.half(64))
            wait(e, t2p, b.at(4, -4))
            pool_norm_apply(e, 1, b, xR[b.par], xn2[b.par][:, :, 0:D])
        else:
            wait(e, t1p, b.at(4))
            pool_norm_apply(e, 0, b, xA[b.par], xn1)

    def scatter(e, p, k):
        for j in range(NJ):
            e.indirect_dma_start(xs_d.ap(), bass.IndirectOffsetOnAxis(ap=idx[p][:, k * NJ + j:k * NJ + j + 1], axis=0),
                                 xn2[p][:, j, :], None).then_inc(scat[p][k], 16)

    def pool_SC(e, b, _):
        wait(e, ridx, b.at(1, 1))
        hold(e)
        scatter(e, b.par, 0)

    def pool_SD(e, b, _):
        p = b.par
        wait(e, scat[p][0], b.half(64, 64))
        hold(e)
        e.tensor_copy(xn2[p][:, :, D:D + 1], wts[p][:, 1, :].rearrange("p (j o) -> p j o", o=1)).then_inc(wcol, 1)
        wait(e, wcol, b.at(1, 1))
        hold(e)
        scatter(e, p, 1)

    def pool_WH(e, b, _):
        wait(e, ld_we, b.at(16, 16))
        wait(e, st_we, b.at(16))
        hold(e)
        e.tensor_scalar(wst[:, :], wst[:, :], WS, None, ALU.mult).then_inc(wech, 1)
        wait(e, wech, b.at(3, 1))
        hold(e)
        e.tensor_scalar(wsp[:, 0, :], wst[:, :], 1.0, None, ALU.mult).then_inc(wech, 1)
        wait(e, wech, b.at(3, 2))
        hold(e)
        e.tensor_tensor(wsp[:, 1, :], wst[:, :], wsp[:, 0, :], ALU.subtract).then_inc(wech, 1)
        if b.reg is None and b.c == NB - 1:
            wait(e, wech, 3 * NB)
            e.memset(wst[:, 0:D + 1], 0.0).then_inc(zset, 1)
            e.memset(wst[:, D + 1:RW], NOWHERE).then_inc(zset, 1)

    def blk_rows(src, b):
        return src[bass.ds(b.at(TB), TB), :].rearrange("(j p) d -> p j d", p=P)

    def sp_XA(e, b, _):
        wait(e, nap[0], b.at(1, -1))
        e.dma_start(xA[b.par][:, :, :], blk_rows(x, b)).then_inc(ld_xA[b.par], 16)

    def sp_KV(e, b, _):
        p = b.par
        wait(e, pvt, b.at(8, -8))
        bt = b.c // 4 if b.reg is None else (b.reg * 2 + b.c) // 4
        e.dma_start(Kst[p][0:96, :, :].rearrange("p (g G) c -> p g (G c)", g=4), k_d[:, :, bass.ds(bt, 1), :].rearrange("p g o n -> p (g o) n")).then_inc(ld_kv[p], 16)
        e.dma_start(Vm[p][:, :, :, :].rearrange("p h l c -> p (h l c)"), vm_d[bass.ds(bt, 1), :, :].rearrange("o p n -> (o p) n")).then_inc(ld_kv[p], 16)
        e.dma_start(Vr[p][:, :, :, :].rearrange("p l g c -> p (l g c)"), vr_d[bass.ds(bt, 1), :, :].rearrange("o p n -> (o p) n")).then_inc(ld_kv[p], 16)

    def sp_RS(e, b, _):
        p = b.par
        wait(e, qle, b.at(4, 4))
        wait(e, stp, b.at(10, -10))
        for g in range(4):
            for part, row in ((0, 0), (0, 32), (1, 64)):
                e.dma_start(Qst[p][row:row + 32, g::4, :], qs[part][32 * g:32 * g + 32, :, :]).then_inc(restack[p], 16)

    def sp_XR(e, b, _):
        wait(e, st_x1[b.par], b.half(16))
        wait(e, nap[1], b.at(1, -1))
        e.dma_start(xR[b.par][:, :, :], blk_rows(x, b)).then_inc(ld_xR[b.par], 16)

    def sp_XS(e, b, _):
        wait(e, x1s, b.at(4, 4))
        e.dma_start(blk_rows(out, b), xR[b.par][:, :, :]).then_inc(st_x1[b.par], 16)

    def expert_of(b):
        return b.c // 2 if b.reg is None else b.reg + b.c // 2

    def sp_WL(e, b, _):
        wait(e, wech, b.at(3))
        e.dma_start(wst[:, :].rearrange("p (k n) -> p k n", n=D),
                    weT[bass.ds(expert_of(b), 1), (b.c % 2) * TILE:(b.c % 2 + 1) * TILE, :].rearrange("o (k p) n -> p (o k) n", p=P)).then_inc(ld_we, 16)

    def sp_WW(e, b, _):
        wait(e, wech, b.at(3, 3))
        e.dma_start(we_d[bass.ds(expert_of(b), 1), :, :, 2 * (b.c % 2):2 * (b.c % 2) + 2, :].rearrange("o p l k n -> (o p) l (k n)"),
                    wsp[:, :, :]).then_inc(st_we, 16)

    def sp_MR(e, b, _):
        wait(e, mte, b.at(1, 1))
        e.dma_start(Qst[b.par][96:97, :, :], mT[:, :]).then_inc(mrow[b.par], 16)

    PE = dict(MX=pe_MX, O=pe_O, XT=pe_XT, R=pe_R, MT=pe_MT, Q=pe_Q, ST=pe_ST, YT=pe_YT, LG=pe_LG, PV=pe_PV, AT=pe_AT)
    AE = dict(XTh=act_XTh, Qh=act_Qh, YTh=act_YTh, ATh=act_ATh, EX=act_EX, PH=act_PH, RX=act_RX,
              NN=lambda e, b, n: act_norm(e, n, b))
    VE = dict(DMX=dve_DMX, Oe=dve_Oe, Ql=dve_Ql, MTe=dve_MTe, RT=dve_RT, RR=dve_RR, PL=dve_PL, NM=dve_NM,
              XTl=lambda e, b, i: dve_lo(e, b, i, f"XT{i}", xnT[1], xnT[0], t1h, t1e),
              YTl=lambda e, b, i: dve_lo(e, b, i, f"YT{i}", x2T[1], x2T[0], t2h, t2e),
              ATl=lambda e, b, i: dve_lo(e, b, i, f"AT{i}", aT[1], aT[0], ath, ate),
              SA=dve_SA, SN=dve_SN, NV=lambda e, b, n: dve_norm_var(e, n, b),
              NC=lambda e, b, n: dve_norm_coef(e, n, b, (XS, XS2)[n]))
    GE = dict(XB=pool_XB, NA=pool_NA, SC=pool_SC, SD=pool_SD, WH=pool_WH)
    SE = dict(XA=sp_XA, KV=sp_KV, RS=sp_RS, XR=sp_XR, XS=sp_XS, MR=sp_MR, WL=sp_WL, WW=sp_WW)

    def slots(e, order, steps, banks=False):
        todo = []
        for word in order.split():
            kind = word.rstrip("0123456789+-") or word
            at = word[len(kind):]
            i, off = (at[:-2], int(at[-2:])) if at[-2:-1] in ("+", "-") else (at, 0)
            todo.append((kind, int(i), off))
        offs = [off for _, _, off in todo]

        def slot(s, seq):
            for kind, i, off in todo:
                b = s + off
                if b.here():
                    if banks:
                        steps[kind](e, b, i, s, seq)
                    else:
                        steps[kind](e, b, i)

        first, last = -max(offs), NB - 1 - min(offs)
        lo = 2 - min(offs)
        n = (NB - max(offs) - lo) // 2
        for s in range(first, lo):
            slot(Blk(s), s)
        with e.Fori(0, n) as it:
            for u in range(2):
                slot(Blk(lo + u, it), lo + u)
        if banks:
            w_skip(2 * n - 2)
        for s in range(lo + 2 * n, last + 1):
            slot(Blk(s), s)

    with nc.Block() as block:
        @block.sync
        def _(e):
            start_counts(e, attend_sems)
            slots(e, ORDER_SP, SE)
            wait(e, zset, 2)
            zeros = zrow.rearrange("p (o d) -> p o d", o=1).broadcast_to([P, 2, RW])
            e.dma_start(xs_d[SPARE:ROWS, :].rearrange("(n p) d -> p n d", p=P), zeros).then_inc(zst, 16)
            wait(e, tbz, 1)
            for n in range(NE):
                r = e.value_load(baseI[0:1, n:n + 1], min_val=0, max_val=SPARE - TILE)
                e.dma_start(xs_d[bass.ds(r, TILE), :].rearrange("(n p) d -> p n d", p=P), zeros).then_inc(zst, 16)
            wait(e, zst, 16 * (NE + 1))
            wait(e, ld_ew, 16 * (NE + 1))
            for p in range(2):
                wait(e, st_x1[p], 16 * NB // 2)
                for k in range(TOPK):
                    wait(e, scat[p][k], 64 * NB // 2)

        @block.gpsimd
        def _(e):
            e.memset(Kst[0][96:97, :, :], -SS).then_inc(g_set, 1)
            wait(e, g_set, 1)
            e.memset(Kst[1][96:97, :, :], -SS).then_inc(g_set, 1)
            wait(e, g_set, 2)
            e.memset(ones[:, :], 1.0).then_inc(g_set, 1)
            e.memset(tri[:, :], 1.0).then_inc(g_set, 1)
            wait(e, g_set, 4)
            e.affine_select(out=tri[:, :], in_=tri[:, :], compare_op=ALU.is_gt, fill=0.0, base=0,
                            pattern=[[1, P]], channel_multiplier=-1).then_inc(g_set, 1)
            e.iota(io8[:, :, :], [[0, NJ], [1, NE]], base=0, channel_multiplier=0, allow_small_or_imprecise_dtypes=True).then_inc(g_set, 1)
            e.iota(base[:, :], [[REGION, NE]], base=0, channel_multiplier=0, allow_small_or_imprecise_dtypes=True).then_inc(g_set, 1)
            e.iota(tile_no[:, :], [[1, NT]], base=0, channel_multiplier=0, allow_small_or_imprecise_dtypes=True).then_inc(g_set, 1)
            e.iota(tok[:, :], [[P, NJ]], base=0, channel_multiplier=1, allow_small_or_imprecise_dtypes=True).then_inc(g_set, 1)
            slots(e, ORDER_POOL, GE)

        @block.scalar
        def _(e):
            e.preload_act_table_set("natural_log_exp_and_others")
            slots(e, ORDER_ACT, AE)

        @block.vector
        def _(e):
            slots(e, ORDER_DVE, VE)
            tables(e)

        @block.tensor
        def _(e):
            slots(e, ORDER_PE, PE, True)
    attend.close()

    TU = 4
    NTURN = 2 * MAXT // TU
    with ExitStack() as ex:
        t = ex.enter_context
        xg = [t(nc.sbuf_tensor(f"xg{i}", [P, RW], F32)) for i in range(TU)]
        gT = [[t(nc.sbuf_tensor(f"gT{i}_{n}", [P, KC, P], F16)) for n in ("hi", "lo")] for i in range(2)]
        wt = [t(nc.sbuf_tensor(f"wt{i}", [P, 2], F32)) for i in range(TU)]
        to = [t(nc.sbuf_tensor(f"to{i}", [P, 1], I32)) for i in range(TU)]
        yb = [t(nc.sbuf_tensor(f"yb{i}", [P, D], F32)) for i in range(2)]
        yw = [t(nc.sbuf_tensor(f"yw{i}", [P, D], F32)) for i in range(TU)]
        Tp = t(nc.psum_tensor("Tp", [P, 2, 512], F32))
        Yp = t(nc.psum_tensor("Yp", [P, 2, 512], F32))
        expert_sems = len(held)
        ld_g = [sem(f"ld_g{i}", t) for i in range(TU)]
        add_y = [sem(f"add_y{i}", t) for i in range(2)]
        gp, gh, gl = sem("gp", t, 4), sem("gh", t, 4), sem("gl", t, 4)
        yp, ye, ywd = sem("yp", t, 4), sem("ye", t, 4), sem("ywd", t, 4)
        wtd, tod = sem("wtd", t), sem("tod", t, 4)
        block = t(nc.Block())

        def tile(it, u):
            return it * TU + u

        def sp_load(e, it, u):
            i = tile(it, u)
            r = e.value_load(row_t[0:1, bass.ds(it * (TU // 2) + u // 2, 1)], min_val=0, max_val=SPARE)
            wait(e, gp, i + (1 - TU))
            wait(e, wtd, i + (1 - TU))
            e.dma_start(xg[u % TU][:, :], xs_d[bass.ds(r + (u % 2) * P, P), :]).then_inc(ld_g[u % TU], 16)

        @block.sync
        def _(e):
            start_counts(e, expert_sems)
            for u in range(TU):
                sp_load(e, 0, u)
            with e.Fori(0, NTURN) as it:
                for u in range(TU):
                    sp_load(e, it, u + TU)
            for u in range(TU):
                wait(e, ld_g[u], 16 * (NTURN + 1))

        @block.gpsimd
        def _(e):
            def turn(it, u, q, first=False):
                i = tile(it, u)
                wait(e, wtd, i + 1)
                if not first:
                    wait(e, add_y[q], it * 32)
                hold(e)
                e.tensor_copy(to[u][:, :], wt[u][:, 1:2]).then_inc(tod, 1)

            def add(it, u):
                i = tile(it, u)
                wait(e, ywd, i + 1)
                wait(e, tod, i + 1)
                hold(e)
                e.indirect_dma_start(out, bass.IndirectOffsetOnAxis(ap=to[u][:, :], axis=0), yw[u][:, :], None,
                                     bounds_check=N - 1, oob_is_err=False, compute_op=ALU.add).then_inc(add_y[u // 2], 16)

            def body(it, first):
                for q in range(2):
                    turn(it, 2 * q, q, first)
                    turn(it, 2 * q + 1, q, first)
                    if q:
                        wait(e, add_y[0], it * 32 + 32)
                    elif not first:
                        wait(e, add_y[1], it * 32)
                    add(it, 2 * q)
                    add(it, 2 * q + 1)

            body(0, True)
            with e.Fori(0, NTURN - 1) as it:
                body(it + 1, False)
            for q in range(2):
                wait(e, add_y[q], 32 * NTURN)

        @block.scalar
        def _(e):
            def hi(it, u):
                i = tile(it, u)
                wait(e, gp, i + 1)
                wait(e, yp, i - 1)
                e.activation(gT[u % 2][0][:, :, :].rearrange("p k n -> p (k n)"), Tp[:, u % 2, :], ACT.Copy).then_inc(gh, 1)

            def weigh(it, u, first=False):
                i = tile(it, u)
                wait(e, ye, i + 1)
                if not first:
                    wait(e, add_y[u // 2], it * 32)
                e.activation(yw[u][:, :], yb[u % 2][:, :], ACT.Copy, scale=wt[u][:, 0:1]).then_inc(ywd, 1)

            def body(it, first):
                for u in range(TU):
                    hi(it, u + 1)
                    weigh(it, u, first)

            hi(0, 0)
            body(0, True)
            with e.Fori(0, NTURN - 1) as it:
                body(it + 1, False)

        @block.vector
        def _(e):
            def lo(it, u):
                i = tile(it, u)
                wait(e, gh, i + 1)
                e.tensor_tensor(gT[u % 2][1][:, :, :].rearrange("p k n -> p (k n)"), Tp[:, u % 2, :],
                                gT[u % 2][0][:, :, :].rearrange("p k n -> p (k n)"), ALU.subtract).then_inc(gl, 1)

            def scale_bias(it, u):
                i = tile(it, u)
                wait(e, ld_g[u], it * 16 + 16)
                wait(e, ywd, i + (1 - TU))
                wait(e, tod, i + (1 - TU))
                e.tensor_copy(wt[u][:, :], xg[u][:, D:RW]).then_inc(wtd, 1)
                n = e.value_load(exp_t[0:1, bass.ds(it * (TU // 2) + u // 2, 1)], min_val=0, max_val=NE - 1)
                wait(e, yp, i + 1)
                wait(e, ywd, i - 1)
                e.scalar_tensor_tensor(yb[u % 2][:, :], Yp[:, u % 2, :], ESC, be_s[:, bass.ds(n * D, D)], ALU.mult, ALU.add).then_inc(ye, 1)

            lo(0, 0)
            with e.Fori(0, NTURN) as it:
                for u in range(TU):
                    lo(it, u + 1)
                    scale_bias(it, u)

        @block.tensor
        def _(e):
            def turn(it, u):
                i = tile(it, u)
                wait(e, ld_g[u % TU], it * 16 + 16 * (u // TU + 1))
                wait(e, gl, i - 1)
                for k in range(KC):
                    m = e.transpose(Tp[:, u % 2, k * P:(k + 1) * P], xg[u % TU][:, k * P:(k + 1) * P], ident[:, :])
                m.then_inc(gp, 1)

            turn(0, 0)
            with e.Fori(0, NTURN) as it:
                for u in range(TU):
                    turn(it, u + 1)
                    i = tile(it, u)
                    n = e.value_load(exp_t[0:1, bass.ds(it * (TU // 2) + u // 2, 1)], min_val=0, max_val=NE - 1)
                    wait(e, gl, i + 1)
                    wait(e, ye, i - 1)
                    seqs = [q for k in range(KC) for q in split3(k)]
                    for c, (xp, wp, k) in enumerate(seqs):
                        m = e.matmul(Yp[:, u % 2, :], gT[u % 2][xp][:, k, :], we_s[:, bass.ds(n * WN + (wp * KC + k) * D, D)],
                                     start=(c == 0), stop=(c == 11))
                    m.then_inc(yp, 1)
    top.close()


_P = "L0_xattn_"
_F = "L0_ffn_"


def kernel(**inputs):
    import concourse.bacc as bacc
    from concourse.bass_utils import run_bass_kernel_spmd

    ctx = np.asarray(inputs["ctx_1024"]).reshape(B * C, D)
    rem = np.concatenate([ctx.reshape(B, C, D)[:, P:C], ctx.reshape(B, C, D)[:, P:P + CP - C]], axis=1)
    arrays = {
        "x": np.asarray(inputs["x"]).reshape(N, D),
        "ctxT": ctx.T, "ctxR": rem.reshape(B * (CP - P), D).T,
        "wqT": np.asarray(inputs[_P + "Wq"]).T, "bq": np.asarray(inputs[_P + "bq"]).reshape(NG, P).T,
        "wkT": np.asarray(inputs[_P + "Wk"]).T, "bk": np.asarray(inputs[_P + "bk"]).reshape(NG, P).T,
        "wvT": np.asarray(inputs[_P + "Wv"]).T, "bv": inputs[_P + "bv"],
        "woT": np.asarray(inputs[_P + "Wo"]).T, "bo": inputs[_P + "bo"],
        "weT": np.asarray(inputs[_F + "W_experts"]).transpose(0, 2, 1), "be": inputs[_F + "b_experts"],
        "wrT": np.asarray(inputs[_F + "W_router"]).T, "br": inputs[_F + "b_router"],
    }
    arrays = {"in_" + n: np.ascontiguousarray(v) for n, v in arrays.items()}
    nc = bacc.Bacc("TRN2", target_bir_lowering=False, num_devices=1)
    args = [nc.dram_tensor(n, v.shape, mybir.dt.from_np(v.dtype), kind="ExternalInput").ap() for n, v in arrays.items()]
    args.append(nc.dram_tensor("out", (N, D), F32, kind="ExternalOutput").ap())
    build(nc, *args)
    got = run_bass_kernel_spmd(nc, [arrays], core_ids=[0]).results[0]["out"]
    return got.reshape(B, T, D)
```

```python
import math
from contextlib import ExitStack

import concourse.bass as bass
import numpy as np
from concourse import mybir

F32, F16 = mybir.dt.float32, mybir.dt.float16
I32, U32 = mybir.dt.int32, mybir.dt.uint32
ALU = mybir.AluOpType
ACT = mybir.ActivationFunctionType
AX = mybir.AxisListType.X

B, T, D, C = 4, 2048, 512, 154
H, HD = 16, 32
NE, TOPK = 8, 2
N = B * T
P = 128
TB = 512
NB = N // TB
NJ = TB // P
KC = D // P
NG = H // 4
CR = C - P
CP = 160
EPS = 1e-5

XS, WS1 = 2.0, 8.0
QS = XS * WS1
KS = 4.0
SS = QS * KS
PSC = 4096.0
VS = 16.0
WS = 64.0
XS2 = 32.0
OSC = 1.0 / (VS * WS)
ESC = 1.0 / (XS2 * WS)
ROOT = math.sqrt(HD)
MSHIFT = math.log(PSC) * ROOT

RW = D + 2
REGION = N + P
MAXT = N * TOPK // P + NE
AHEAD = 4
SPARE = NE * REGION
ROWS = SPARE + P
NOWHERE = float(1 << 20)


ORDER_PE = """
    YT1-2 PV2-1 PV3-1 ST8-1 AT0-1 YT2-2 ST9-1 PV4-1 YT3-2 AT1-1 PV5-1 MX0 PV6-1 AT2-1 PV7-1 MX1 MX2 AT3-1 LG0-2
    MX3 O0-1 O1-1 O2-1 O3-1 MX4 XT2+1 O4-1 O5-1 MX5 MX6 O6-1 XT3+1 O7-1 MX7 O8-1 MX8 O9-1 MX9 O10-1 MX10 O11-1
    Q0+1 MT0 Q1+1 Q2+1 Q3+1 Q4+1 Q5+1 ST0 ST1 Q6+1 ST2 R0-2 Q7+1 Q8+1 ST3 ST4 Q9+1 Q10+1 Q11+1 ST5 XT0+2 PV0 XT1+2
    PV1 ST6 YT0-1 ST7
"""
ORDER_ACT = """
    EX2 Qh2+1 PH2 EX3 PH3 Qh3+1 EX4 XTh0+2 PH4 XTh1+2 EX5 PH5 EX6 YTh0-1 YTh1-1 PH6 EX7 PH7 EX8 ATh0 YTh2-1 PH8
    EX9 PH9 YTh3-1 ATh1 ATh2 ATh3 XTh2+2 XTh3+2 NN0+3 Qh0+2 Qh1+2 NN1 EX0+1 PH0+1 RX0-1 EX1+1 PH1+1
"""
ORDER_DVE = """
    NM1-1 PL5-1 YTl0-2 YTl1-2 NV0+2 PL6-1 NM2-1 PL7-1 NM3-1 ATl0-1 YTl2-2 PL8-1 NM4-1 PL9-1 NM5-1 YTl3-2 ATl1-1
    DMX0 NM6-1 NM7-1 ATl2-1 DMX1 ATl3-1 RT0-2 DMX2 Oe0-1 DMX3 DMX4 XTl2+1 Oe1-1 DMX5 DMX6 XTl3+1 DMX7 Oe2-1 DMX8
    DMX9 DMX10 Oe3-1 SN0-1 MTe0 NC0+2 SN1-1 SN2-1 SN3-1 Ql0+1 NV1-1 SA0+3 Ql1+1 NC1-1 SA1+3 PL0 RR0-2 PL1 SA2+3
    SA3+3 Ql2+1 PL2 Ql3+1 PL3 XTl0+2 NM0 PL4 XTl1+2
"""
ORDER_POOL = """
    SD0-3 WH0 NA1-1 NA0+2 SC0-2 XB0
"""
ORDER_SP = """
    KV0 RS0 WW0-1 XR0 MR0 WL0+1 XA0+4 XS0-1
"""
BANK = {"XT0": 0, "O0": 0, "Q0": 0, "YT0": 0, "AT0": 1, "XT1": 1, "O3": 1, "Q3": 1, "YT1": 1, "AT1": 0, "XT2": 0,
        "O6": 0, "Q6": 0, "YT2": 0, "AT2": 1, "XT3": 1, "O9": 1, "Q9": 1, "YT3": 1, "AT3": 0, "R0": 1, "MT0": 1,
        "LG0": 1}


class Blk:

    def __init__(self, c, reg=None):
        self.c, self.reg = c, reg

    def __add__(self, k):
        return Blk(self.c + k, self.reg)

    @property
    def par(self):
        return self.c % 2

    @property
    def first(self):
        return self.reg is None and self.c == 0

    def at(self, n, k=0):
        return n * self.c + k if self.reg is None else self.reg * (2 * n) + (n * self.c + k)

    def half(self, n, k=0):
        return n * (self.c // 2) + k if self.reg is None else self.reg * n + (n * (self.c // 2) + k)

    def here(self, last=NB - 1):
        return self.reg is not None or 0 <= self.c <= last


def build(nc, x, ctxT, wqT, bq, wkT, bk, wvT, bv, woT, bo, weT, be, wrT, br, out):
    top = ExitStack()
    keep = top.enter_context
    k_d = nc.dram_tensor("k_scratch", (96, 4, B, NG * CP), F16)
    vm_d = nc.dram_tensor("vm_scratch", (B, P, H * 2 * 33), F16)
    vr_d = nc.dram_tensor("vr_scratch", (B, P, 2 * NG * 4 * 33), F16)
    xs_d = nc.dram_tensor("dispatched", (ROWS, RW), F32)
    we_d = nc.dram_tensor("we_scratch", (NE, P, 2, KC, D), F16)

    tick = {}

    def sem(name, ctx=keep, prime=0):
        s = ctx(nc.semaphore(name))
        primes[name] = prime
        names[id(s)] = name
        held.append(s)
        return s

    primes, names, held = {}, {}, []

    def start_counts(e, first):
        for s in held[first:]:
            if primes[names[id(s)]]:
                e.sem_inc(s, primes[names[id(s)]])

    def wait(e, s, v):
        if isinstance(v, int) and v <= 0:
            return
        e.wait_ge(s, v + primes[names[id(s)]])
        if e is nc.sync and not isinstance(v, int):
            hold(e)

    def hold(e):
        e.sem_inc(tick[id(e)], 1)

    for nm, e in (("dve", nc.vector), ("pool", nc.gpsimd), ("sp", nc.sync)):
        tick[id(e)] = keep(nc.semaphore("tick_" + nm))

    row_t = keep(nc.sbuf_tensor("row_t", [1, MAXT + AHEAD], I32))
    exp_t = keep(nc.sbuf_tensor("exp_t", [1, MAXT + AHEAD], I32))
    new_t = keep(nc.sbuf_tensor("new_t", [1, MAXT + AHEAD], I32))
    ident = keep(nc.sbuf_tensor("ident", [P, P], F32))

    WN = 2 * KC * D
    we_s = keep(nc.sbuf_tensor("we_s", [P, NE * WN], F16))
    be_s = keep(nc.sbuf_tensor("be_s", [P, NE * D], F32))
    carved = [0]

    def carve(n, size):
        first = carved[0]
        carved[0] += n * size
        return we_s[:, first:carved[0]].rearrange("p (n c) -> p n c", c=size)

    attend = ExitStack()
    a = attend.enter_context
    wq_s = a(nc.sbuf_tensor("wq_s", [P, 2, KC, D], F16))
    wo_s = a(nc.sbuf_tensor("wo_s", [P, 2, KC, D], F16))
    wr_s = a(nc.sbuf_tensor("wr_s", [P, 2, KC, NE], F16))
    bqs = a(nc.sbuf_tensor("bqs", [P, NG], F32))
    bo_b = a(nc.sbuf_tensor("bo_b", [P, D], F32))
    br_b = a(nc.sbuf_tensor("br_b", [P, NE], F32))

    xA = [be_s[:, i * NJ * D:(i + 1) * NJ * D].rearrange("p (j d) -> p j d", d=D) for i in range(2)]
    xR_s = a(nc.sbuf_tensor("xR_s", [P, 2 * NJ * D], F32))
    xR = [xR_s[:, i * NJ * D:(i + 1) * NJ * D].rearrange("p (j d) -> p j d", d=D) for i in range(2)]
    xn1 = a(nc.sbuf_tensor("xn1", [P, NJ, D], F32))
    xnT = [carve(KC, TB), a(nc.sbuf_tensor("xnT_lo", [P, KC, TB], F16))]
    qs = [carve(NG, TB) for _ in range(2)]
    Qst = [carve(H, TB) for _ in range(2)]
    Kst = [a(nc.sbuf_tensor(f"Kst{i}", [97, H, CP], F16)) for i in range(2)]
    Vm = [a(nc.sbuf_tensor(f"Vm{i}", [P, H, 2, 33], F16)) for i in range(2)]
    Vr = [a(nc.sbuf_tensor(f"Vr{i}", [P, 2, NG, 4 * 33], F16)) for i in range(2)]
    mx_sb = a(nc.sbuf_tensor("mx_sb", [P, NJ * H], F32))
    mT = a(nc.sbuf_tensor("mT", [H, TB], F16))
    P32_s = a(nc.sbuf_tensor("P32_s", [P, 2, 2, TB], F32))
    P32 = [P32_s[:, i, :, :] for i in range(2)]
    Pst = [carve(10, TB) for _ in range(2)]
    assert carved[0] == NE * WN
    att = a(nc.sbuf_tensor("att", [P, NJ, H, HD], F32))
    aT = [a(nc.sbuf_tensor("aT_" + n, [P, KC, TB], F16)) for n in ("hi", "lo")]
    xn2 = [a(nc.sbuf_tensor(f"xn2_{i}", [P, NJ, RW], F32)) for i in range(2)]
    x2T = [a(nc.sbuf_tensor("x2T_" + n, [P, KC, TB], F16)) for n in ("hi", "lo")]
    rcp = a(nc.sbuf_tensor("rcp", [P, 2, 2, 4], F32))
    stats = [a(nc.sbuf_tensor(f"stats{i}", [P, NJ, 6], F32)) for i in range(2)]
    aggr = [a(nc.sbuf_tensor(f"aggr{i}", [P, NJ, 2], F32)) for i in range(2)]
    nrm = [a(nc.sbuf_tensor(f"nrm{i}", [P, 7, NJ], F32)) for i in range(2)]
    lg = a(nc.sbuf_tensor("lg", [P, NJ, NE + 1], F32))
    top8 = a(nc.sbuf_tensor("top8", [P, NJ, 8], F32))
    topi = a(nc.sbuf_tensor("topi", [P, NJ, 8], U32))
    topf = a(nc.sbuf_tensor("topf", [P, TOPK, NJ], F32))
    lgd = a(nc.sbuf_tensor("lgd", [P, NJ, NE + 1], F32))
    ex9 = a(nc.sbuf_tensor("ex9", [P, NJ, NE + 1], F32))
    sm = a(nc.sbuf_tensor("sm", [P, 2, NJ], F32))
    wts = [a(nc.sbuf_tensor(f"wts{i}", [P, TOPK, NJ], F32)) for i in range(2)]
    tok = a(nc.sbuf_tensor("tok", [P, NJ], F32))
    wst = a(nc.sbuf_tensor("wst", [P, 2 * D], F32))
    zrow = wst[:, 0:RW]
    wsp = a(nc.sbuf_tensor("wsp", [P, 2, 2 * D], F16))
    io8 = a(nc.sbuf_tensor("io8", [P, NJ, NE], F32))
    oneh = a(nc.sbuf_tensor("oneh", [P, TOPK, NJ, NE], F32))
    msk = a(nc.sbuf_tensor("msk", [P, NJ, NE], F16))
    posb = a(nc.sbuf_tensor("posb", [P, NJ, NE], F32))
    seld = a(nc.sbuf_tensor("seld", [P, TOPK, NJ, NE], F32))
    idf = a(nc.sbuf_tensor("idf", [P, TOPK, NJ], F32))
    idx = [a(nc.sbuf_tensor(f"idx{i}", [P, TOPK * NJ], I32)) for i in range(2)]
    base = a(nc.sbuf_tensor("base", [P, NE], F32))
    tri = a(nc.sbuf_tensor("tri", [P, P], F16))
    ones = a(nc.sbuf_tensor("ones", [P, P], F16))
    baseI = a(nc.sbuf_tensor("baseI", [1, NE], I32))
    NT = MAXT + AHEAD
    tile_no = a(nc.sbuf_tensor("tile_no", [1, NT], F32))
    tb = a(nc.sbuf_tensor("tb", [P, 6, NE], F32))
    tbi = a(nc.sbuf_tensor("tbi", [P, 2, NE], I32))
    tg = att[0:1, :, :, :].rearrange("p j h d -> p (j h d)")[:, 0:NT * NE].rearrange("p (n e) -> p n e", e=NE)
    te = att[0:1, :, :, :].rearrange("p j h d -> p (j h d)")[:, NT * NE:NT * (NE + 3)].rearrange("p (i n) -> p i n", i=3)

    S = a(nc.psum_tensor("S", [P, 4, 512], F32))
    PVp = a(nc.psum_tensor("PVp", [P, 2, 512], F32))
    W = a(nc.psum_tensor("W", [P, 2, 512], F32))

    def flat(first, *shape):
        n = int(np.prod(shape))
        v = xR_s[:, first:first + n]
        return v.rearrange("p (k n) -> p k n", n=shape[-1]) if len(shape) > 1 else v

    ctx_sb = flat(0, KC, B * C)
    bv_b = flat(KC * B * C, D)
    v32 = [flat(KC * B * C + (1 + i) * D, D) for i in range(2)]
    w_sb = {"k": att[:, :, :, :].rearrange("p j h d -> p j (h d)"), "o": P32_s[:, :, :, :].rearrange("p i u n -> p (i u) n")}
    for i, n in enumerate("qv"):
        w_sb[n] = xn2[i][:, :, :].rearrange("p j r -> p (j r)")[:, 0:KC * D].rearrange("p (k n) -> p k n", n=D)
    kk = [Pst[0].rearrange("p n c -> p (n c)")[:, i * B * NG * CP:(i + 1) * B * NG * CP].rearrange("p (b G c) -> p b G c", G=NG, c=CP)
          for i in range(2)]
    *vm, vr, zero = [v.rearrange("p n c -> p (n c)")[:, i * H * 66:(i + 1) * H * 66] for v in (Qst[1], Pst[1]) for i in range(3)]
    vm = [v.rearrange("p (h l c) -> p h l c", l=2, c=33) for v in vm]
    vr = vr.rearrange("p (l h c) -> p l h c", l=2, c=33)
    wr32 = a(nc.sbuf_tensor("wr32", [P, KC, NE], F32))
    bk_s = a(nc.sbuf_tensor("bk_s", [P, NG], F32))

    def s_(name, prime=0):
        return sem(name, a, prime)

    attend_sems = len(held)
    g_set = s_("g_set")
    ld_xA = [s_(f"ld_xA{i}") for i in range(2)]
    ld_xR = [s_(f"ld_xR{i}") for i in range(2)]
    ld_k = [s_(f"ld_k{i}") for i in range(2)]
    ld_v = [s_(f"ld_v{i}") for i in range(2)]
    restack = [s_(f"restack{i}") for i in range(2)]
    mrow = [s_(f"mrow{i}") for i in range(2)]
    st_x1 = [s_(f"st_x1_{i}") for i in range(2)]
    scat = [[s_(f"scat{i}_{k}") for k in range(TOPK)] for i in range(2)]
    zset, ld_ew = s_("zset"), s_("ld_ew")
    ld_we, wech, st_we, wcol = s_("ld_we"), s_("wech"), s_("st_we"), s_("wcol")
    nch = [s_(f"nch{i}") for i in range(2)]
    nvar = [s_(f"nvar{i}") for i in range(2)]
    nln = [s_(f"nln{i}") for i in range(2)]
    nrs = [s_(f"nrs{i}") for i in range(2)]
    nap = [s_(f"nap{i}") for i in range(2)]
    xrb = s_("xrb")
    t1p, t1h, t1e = s_("t1p"), s_("t1h"), s_("t1e")
    qp, qhe, qle = s_("qp"), s_("qhe"), s_("qle")
    mxp, mxr, mtp, mte = s_("mxp"), s_("mxr"), s_("mtp"), s_("mte")
    stp, exd, phd, pld = s_("stp"), s_("exd"), s_("phd"), s_("pld")
    pvt, rcd, nmd = s_("pvt"), s_("rcd"), s_("nmd")
    atp, ath, ate = s_("atp"), s_("ath"), s_("ate")
    op_, x1s = s_("op_"), s_("x1s")
    t2p, t2h, t2e = s_("t2p"), s_("t2h"), s_("t2e")
    lgp, lge, rch, rex = s_("lgp"), s_("lge"), s_("rch"), s_("rex")
    rcd2, mskd, rp, rev, ridx = s_("rcd2"), s_("mskd"), s_("rp"), s_("rev"), s_("ridx")
    tbd, tbz, zst = s_("tbd"), s_("tbz"), s_("zst")

    L = {n: s_("ld_" + n) for n in ("bias", "bo", "ctx", "q", "o", "k", "v", "r")}
    p_id, p_hi, p_bk, p_ks, p_kp = (s_(n) for n in ("p_id", "p_hi", "p_bk", "p_ks", "p_kp"))
    p_kh, p_kl, p_vp, p_v32, p_vh = (s_(n) for n in ("p_kh", "p_kl", "p_vp", "p_v32", "p_vh"))
    p_v, p_set, p_kd, p_vz, p_lo = (s_(n) for n in ("p_v", "p_set", "p_kd", "p_vz", "p_lo"))
    p_vd = [s_(f"p_vd{i}") for i in range(2)]
    p_vr = s_("p_vr")
    KREM = B * CR
    parts_of = (("q", wq_s, WS1), ("o", wo_s, WS), ("r", wr_s, WS))

    def wait_values_stored(e):
        for i in range(2):
            wait(e, p_vd[i], 16 * B // 2)
        wait(e, p_vr, 16 * 4 * B)

    def sp_load_weights(e, n, src):
        e.dma_start(w_sb[n], src.rearrange("(k p) n -> p k n", p=P)).then_inc(L[n], 16)

    def sp_prepare(e):
        e.dma_start(ctx_sb, ctxT.rearrange("(k p) n -> p k n", p=P)).then_inc(L["ctx"], 16)
        sp_load_weights(e, "k", wkT)
        sp_XA(e, Blk(0), 0)
        sp_load_weights(e, "q", wqT)
        sp_load_weights(e, "v", wvT)
        sp_XA(e, Blk(1), 0)
        sp_load_weights(e, "o", woT)
        wait(e, p_kh, NG)
        wait(e, p_kl, NG)
        for g in range(4):
            for part, row in ((0, 0), (1, 32), (0, 64)):
                e.dma_start(k_d[row:row + 32, g, :, :].rearrange("r b n -> r (b n)"),
                            kk[part][32 * g:32 * g + 32, :, :, :].rearrange("r b G c -> r (b G c)")).then_inc(p_kd, 16)

    def pool_prepare(e):
        e.memset(ident[:, :], 0.0).then_inc(p_id, 1)
        wait(e, p_id, 1)
        e.affine_select(out=ident[:, :], in_=ident[:, :], compare_op=ALU.not_equal, fill=1.0, base=0,
                        pattern=[[-1, P]], channel_multiplier=1).then_inc(p_id, 1)
        e.memset(zero, 0.0).then_inc(p_set, 1)
        for v in vm:
            e.memset(v[:, :, 0, 32:33], 1.0).then_inc(p_set, 1)
            e.memset(v[:, :, 1, 32:33], 0.0).then_inc(p_set, 1)
        e.memset(vr[:, 0, :, 32:33], 1.0).then_inc(p_set, 1)
        e.memset(vr[:, 1, :, 32:33], 0.0).then_inc(p_set, 1)

    def act_prepare(e):
        e.dma_start(bk_s[:, :], bk).then_inc(L["bias"], 16)
        e.dma_start(bqs[:, :], bq).then_inc(L["bias"], 16)
        e.dma_start(bv_b, bv.rearrange("(a n) -> a n", a=1).broadcast_to([P, D])).then_inc(L["bias"], 16)
        e.dma_start(bo_b[:, :], bo.rearrange("(a n) -> a n", a=1).broadcast_to([P, D])).then_inc(L["bo"], 16)
        e.dma_start(br_b[:, :], br.rearrange("(a n) -> a n", a=1).broadcast_to([P, NE])).then_inc(L["bo"], 16)
        e.dma_start(wr32[:, :, :], wrT.rearrange("(k p) n -> p k n", p=P)).then_inc(L["r"], 16)
        wait(e, L["k"], 16)
        for k in range(KC):
            e.activation(w_sb["k"][:, k, :], w_sb["k"][:, k, :], ACT.Copy, scale=KS).then_inc(p_ks, 1)
        act_norm(e, 0, Blk(0))
        wait(e, p_bk, 1)
        for G in range(NG):
            wait(e, p_kp, G + 1)
            for rem in range(2):
                i = e.activation(key_part(0, G, rem), keys_of(G, rem), ACT.Identity, bias=bk_s[:, G:G + 1])
            i.then_inc(p_lo, 1)
            if G == 1:
                act_split(e, 0)
        wait(e, p_set, 3 + 2 * B)
        for b in range(B):
            e.dma_start(vr_d[b, :, :], zero).then_inc(p_vz, 16)

    def keys_of(G, rem):
        c = CR if rem else P
        return S[:, 2 * (G % 2) + rem, 0:B * c].rearrange("p (b c) -> p b c", c=c)

    def key_part(i, G, rem):
        return kk[i][:, :, G, P:C] if rem else kk[i][:, :, G, 0:P]

    def act_split(e, n):
        name, dst, scale = parts_of[n]
        wait(e, L[name], 16)
        src = w_sb[name] if name in w_sb else wr32[:, :, :]
        e.activation(dst[:, 0, :, :], src, ACT.Copy, scale=scale).then_inc(p_hi, 1)

    def dve_split(e, n):
        name, dst, scale = parts_of[n]
        wait(e, p_hi, n + 1)
        src = w_sb[name] if name in w_sb else wr32[:, :, :]
        e.scalar_tensor_tensor(dst[:, 1, :, :], src, scale, dst[:, 0, :, :], ALU.mult, ALU.subtract).then_inc(p_bk, 1)

    def dve_prepare(e):
        wait(e, L["bias"], 48)
        e.tensor_scalar(bk_s[:, :], bk_s[:, :], KS, None, ALU.mult).then_inc(p_bk, 1)
        e.tensor_scalar(bqs[:, :], bqs[:, :], QS, None, ALU.mult).then_inc(p_bk, 1)
        e.tensor_scalar(bv_b, bv_b, VS, None, ALU.mult).then_inc(p_bk, 1)
        for j in range(NJ):
            dve_SA(e, Blk(0), j)
        dve_norm_var(e, 0, Blk(0))
        for G in range(NG):
            if G == 1:
                dve_norm_coef(e, 0, Blk(0), XS)
            wait(e, p_lo, G + 1)
            for rem in range(2):
                i = e.scalar_tensor_tensor(key_part(1, G, rem), keys_of(G, rem), bk_s[:, G:G + 1], key_part(0, G, rem),
                                           ALU.add, ALU.subtract)
            i.then_inc(p_v32, 1)
            wait(e, p_v32, G + 1)
            e.tensor_copy(kk[0][:, :, G, C:CP], kk[0][:, :, G, P:P + CP - C]).then_inc(p_kh, 1)
            e.tensor_copy(kk[1][:, :, G, C:CP], kk[1][:, :, G, P:P + CP - C]).then_inc(p_kl, 1)
            if G == 1:
                dve_split(e, 0)
            if G >= 2:
                for j in (2 * G - 4, 2 * G - 3):
                    dve_SA(e, Blk(1), j)

    def dve_values(e):
        wait(e, p_set, 3 + 2 * B)
        wait(e, p_bk, 3)
        for b in range(B + 1):
            rows = P if b < B else KREM
            wait(e, p_vp, b + 1)
            e.scalar_tensor_tensor(v32[b % 2][0:rows], PVp[0:rows, b % 2, :], VS, bv_b[0:rows],
                                   ALU.mult, ALU.add).then_inc(p_v32, 1)
            wait(e, p_v32, NG + b + 1)
            v = v32[b % 2][0:rows].rearrange("p (h d) -> p h d", d=HD)
            hi, lo = (vm[b][:, :, 0, 0:HD], vm[b][:, :, 1, 0:HD]) if b < B else (vr[0:rows, 0, :, 0:HD], vr[0:rows, 1, :, 0:HD])
            e.tensor_copy(hi, v).then_inc(p_vh, 1)
            wait(e, p_vh, b + 1)
            e.tensor_tensor(lo, v, hi, ALU.subtract).then_inc(p_v, 1)

    def act_values(e):
        for b in range(B):
            wait(e, p_v, b + 1)
            e.dma_start(vm_d[b, :, :], vm[b].rearrange("p h l c -> p (h l c)")).then_inc(p_vd[b % 2], 16)

    def sp_values_rem(e):
        wait(e, p_v, B + 1)
        wait(e, p_vz, 16 * B)
        for b in range(B):
            for g in range(4):
                e.dma_start(vr_d[b, 32 * g:32 * g + CR, :].rearrange("r (k g c) -> r k g c", g=4, c=33)[:, :, g, :],
                            vr[CR * b:CR * b + CR, :, :, :].rearrange("r l (G g) c -> r (l G) g c", g=4)[:, :, g, :]).then_inc(p_vr, 16)

    def pe_prepare(e):
        wait(e, L["ctx"], 16)
        for G in range(NG):
            if G >= 2:
                wait(e, p_v32, G - 1)
            for k in range(KC):
                if G == 0:
                    wait(e, p_ks, k + 1)
                for rem in range(2):
                    m = e.matmul(S[:, 2 * (G % 2) + rem, 0:(KREM if rem else B * P)], w_sb["k"][:, k, G * P:(G + 1) * P],
                                 ctx_sb[:, k, B * P:] if rem else ctx_sb[:, k, 0:B * P], start=(k == 0), stop=(k == KC - 1))
            m.then_inc(p_kp, 1)
        wait(e, p_id, 2)

    def pe_values(e):
        wait(e, L["v"], 16)
        for b in range(B + 1):
            if b >= 2:
                wait(e, p_v32, NG + b - 1)
            rows = P if b < B else KREM
            for k in range(KC):
                lhs = ctx_sb[:, k, b * P:b * P + rows]
                m = e.matmul(PVp[0:rows, b % 2, :], lhs, w_sb["v"][:, k, :], start=(k == 0), stop=(k == KC - 1))
            m.then_inc(p_vp, 1)

    class Chain:

        def __init__(self, e, s, blk, n):
            self.e, self.s, self.blk, self.n, self.k = e, s, blk, n, 0

        def do(self, ins):
            ins.then_inc(self.s, 1)
            self.k += 1

        def sync(self):
            wait(self.e, self.s, self.blk.at(self.n, self.k))

        def end(self):
            assert self.k == self.n, (self.k, self.n)

    NCH = 2 * NJ + 6

    def dve_norm_stats(e, n, src, j):
        e.bn_stats(stats[n][:, j, :], src[:, j, :]).then_inc(nch[n], 1)

    def dve_norm_var(e, n, b):
        ch = Chain(e, nch[n], b, NCH)
        ch.k = NJ
        ch.sync()
        hold(e)
        for j in range(NJ):
            ch.do(e.bn_aggr(aggr[n][:, j, :], stats[n][:, j, :]))
        ch.sync()
        ch.do(e.tensor_scalar(nrm[n][:, 0, :], aggr[n][:, :, 1], EPS, None, ALU.add))
        ch.sync()
        e.tensor_copy(nrm[n][:, 1, :], nrm[n][:, 0, :]).then_inc(nvar[n], 1)

    def dve_norm_coef(e, n, b, scale):
        v = nrm[n]
        ch = Chain(e, nch[n], b, NCH)
        ch.k = 2 * NJ + 1
        wait(e, nrs[n], b.at(1, 1))
        ch.do(e.tensor_tensor(v[:, 3, :], v[:, 2, :], v[:, 2, :], ALU.mult))
        ch.sync()
        ch.do(e.tensor_tensor(v[:, 4, :], v[:, 3, :], v[:, 0, :], ALU.mult))
        ch.sync()
        ch.do(e.tensor_scalar(v[:, 3, :], v[:, 4, :], -0.5 * scale, 1.5 * scale, ALU.mult, ALU.add))
        ch.sync()
        wait(e, nap[n], b.at(1))
        ch.do(e.tensor_tensor(v[:, 5, :], v[:, 3, :], v[:, 2, :], ALU.mult))
        ch.sync()
        ch.do(e.scalar_tensor_tensor(v[:, 6, :], aggr[n][:, :, 0], -1.0, v[:, 5, :], ALU.mult, ALU.mult))
        ch.end()

    def act_norm(e, n, b):
        wait(e, nvar[n], b.at(1, 1))
        e.activation(nrm[n][:, 1, :], nrm[n][:, 1, :], ACT.Ln).then_inc(nln[n], 1)
        wait(e, nln[n], b.at(1, 1))
        e.activation(nrm[n][:, 2, :], nrm[n][:, 1, :], ACT.Exp, scale=-0.5).then_inc(nrs[n], 1)

    def pool_norm_apply(e, n, b, src, dst):
        wait(e, nch[n], b.at(NCH, NCH))
        hold(e)
        for j in range(NJ):
            i = e.tensor_scalar(dst[:, j, :], src[:, j, :], nrm[n][:, 5, j:j + 1], nrm[n][:, 6, j:j + 1], ALU.mult, ALU.add)
        i.then_inc(nap[n], 1)

    wprev = {0: None, 1: None}

    def w_take(e, bank, slot, seq, s, n, k, off):
        if wprev[bank] is not None:
            s0, n0, k0, off0, seq0 = wprev[bank]
            wait(e, s0, (slot + (off0 - (seq - seq0))).at(n0, k0))
        wprev[bank] = (s, n, k, off, seq)

    def w_skip(n):
        for bank in range(2):
            wprev[bank] = (*wprev[bank][:4], wprev[bank][4] + n)

    def pe_T(e, step, b, slot, seq, src, i, done, ev):
        w_take(e, BANK[step], slot, seq, ev, 4, i + 1, b.c - slot.c)
        for j in range(NJ):
            m = e.transpose(W[:, BANK[step], j * P:(j + 1) * P], src(j, i), ident[:, :])
        m.then_inc(done, 1)

    def split3(k):
        return ((0, 0, k), (1, 0, k), (0, 1, k))

    def pe_XT(e, b, i, slot, seq):
        if i == 0:
            wait(e, nap[0], b.at(1, 1))
        pe_T(e, f"XT{i}", b, slot, seq, lambda j, k: xn1[:, j, k * P:(k + 1) * P], i, t1p, t1e)

    def pe_Q(e, b, i, slot, seq):
        G, part = i // 3, i % 3
        bank = BANK[f"Q{3 * G}"]
        if b.first and i == 0:
            wait(e, p_bk, 4)
        if i == 0:
            wait(e, t1e, b.at(4, 4))
        if part == 0:
            w_take(e, bank, slot, seq, qle, 4, G + 1, b.c - slot.c)
        seqs = [t for k in range(KC) for t in split3(k)]
        for n in range(4 * part, 4 * part + 4):
            wp, xp, k = seqs[n]
            m = e.matmul(W[:, bank, :], wq_s[:, wp, k, G * P:(G + 1) * P], xnT[xp][:, k, :], start=(n == 0), stop=(n == 11))
        if part == 2:
            m.then_inc(qp, 1)

    def pe_MX(e, b, n, slot, seq):
        p = b.par
        if b.first and n == 0:
            pe_values(e)
            wait(e, p_v32, NG)
        if n == 0:
            wait(e, restack[p], b.half(192, 192))
            wait(e, ld_k[p], b.half(16, 16))
        if n < 2:
            wait(e, exd, b.at(10, n - 1))
        else:
            wait(e, mxr, b.at(11, n - 1))
        for u in range(6 * n, min(6 * n + 6, NJ * H)):
            j, h = u // H, u % H
            m = e.matmul(S[:, 2 * (n % 2) + u % 6 // 3, (u % 3) * C:(u % 3 + 1) * C], Qst[p][0:96, h, j * P:(j + 1) * P],
                         Kst[p][0:96, 4 * (h % 4) + h // 4, 0:C], start=True, stop=True)
        m.then_inc(mxp, 1)

    def pe_O(e, b, i, slot, seq):
        j, part = i // 3, i % 3
        bank = BANK[f"O{3 * j}"]
        if b.first and i == 0:
            wait(e, p_bk, 5)
        if i == 0:
            wait(e, ate, b.at(4, 4))
        if part == 0:
            w_take(e, bank, slot, seq, x1s, 4, j + 1, b.c - slot.c)
        seqs = [t for k in range(KC) for t in split3(k)]
        for n in range(4 * part, 4 * part + 4):
            ap, wp, k = seqs[n]
            m = e.matmul(W[:, bank, :], aT[ap][:, k, j * P:(j + 1) * P], wo_s[:, wp, k, :], start=(n == 0), stop=(n == 11))
        if part == 2:
            m.then_inc(op_, 1)

    def pe_MT(e, b, i, slot, seq):
        wait(e, mxr, b.at(11, 11))
        bank = BANK["MT0"]
        w_take(e, bank, slot, seq, mte, 1, 1, b.c - slot.c)
        for j in range(NJ):
            m = e.transpose(W[0:H, bank, j * P:(j + 1) * P], mx_sb[:, j * H:(j + 1) * H], ident[:, :])
        m.then_inc(mtp, 1)

    def pe_R(e, b, i, slot, seq):
        if b.first:
            wait(e, g_set, 5)
        bank = BANK["R0"]
        wait(e, mskd, b.at(1, 1))
        w_take(e, bank, slot, seq, rev, 1, 1, b.c - slot.c)
        mm = msk[:, :, :].rearrange("p j e -> p (j e)")
        e.matmul(W[:, bank, 0:NJ * NE], tri[:, :], mm, start=True, stop=False)
        for d in range(1, NJ):
            m = e.matmul(W[:, bank, d * NE:NJ * NE], ones[:, :], mm[:, 0:(NJ - d) * NE], start=False, stop=(d == NJ - 1))
        for j in range(NJ):
            m = e.matmul(W[:, bank, NJ * NE:(NJ + 1) * NE], ones[:, :], mm[:, j * NE:(j + 1) * NE], start=(j == 0), stop=(j == NJ - 1))
        m.then_inc(rp, 1)

    def pe_ST(e, b, n, slot, seq):
        p = b.par
        if b.first and n == 0:
            wait(e, g_set, 5)
        if n == 0:
            wait(e, mrow[p], b.half(16, 16))
        if n < 2:
            wait(e, mxr, b.at(11, 11))
        else:
            wait(e, exd, b.at(10, n - 1))
        for u in (2 * n, 2 * n + 1):
            G, r, bank = u // 5, u % 5, 2 * (n % 2) + u % 2
            if r < 4:
                m = e.matmul(S[:, bank, :], Kst[p][0:97, 4 * r + G, 0:P], Qst[p][0:97, 4 * G + r, :], start=True, stop=True)
            else:
                for g in range(4):
                    m = e.matmul(S[32 * g:32 * g + 32, bank, :], Kst[p][0:97, 4 * g + G, P:CP], Qst[p][0:97, 4 * G + g, :],
                                 start=True, stop=True)
        m.then_inc(stp, 1)

    def pe_PV(e, b, w, slot, seq):
        p, G, q = b.par, w // 2, w % 2
        wait(e, pld, b.at(10, (5 * G + 4) // 2 + 1))
        if w == 0:
            wait(e, ld_v[p], b.half(32, 32))
        wait(e, nmd, b.at(8, w - 1))
        for jj in range(2):
            j = 2 * q + jj
            tok = slice(j * P, (j + 1) * P)
            o = PVp[:, q, jj * 132:(jj + 1) * 132]
            for n, (pp, vv) in enumerate(((0, 0), (0, 1), (1, 0))):
                e.matmul(o, Pst[pp][:, (5 * G + 4) % 10, tok], Vr[p][:, vv, G, :], start=(n == 0), stop=(n == 2))
            for g in range(4):
                for pp, vv in ((0, 0), (0, 1), (1, 0)):
                    m = e.matmul(o[:, g * 33:(g + 1) * 33], Pst[pp][:, (5 * G + g) % 10, tok], Vm[p][:, 4 * G + g, vv, :],
                                 start=False, stop=True, skip_group_check=True)
        m.then_inc(pvt, 1)

    def pe_AT(e, b, G, slot, seq):
        wait(e, nmd, b.at(8, 2 * G + 2))
        pe_T(e, f"AT{G}", b, slot, seq, lambda j, k: att[:, j, 4 * k:4 * k + 4, :].rearrange("p h d -> p (h d)"), G, atp, ate)

    def pe_YT(e, b, i, slot, seq):
        if i == 0:
            wait(e, nap[1], b.at(1, 1))
        pe_T(e, f"YT{i}", b, slot, seq, lambda j, k: xn2[b.par][:, j, k * P:(k + 1) * P], i, t2p, t2e)

    def pe_LG(e, b, i, slot, seq):
        bank = BANK["LG0"]
        wait(e, t2e, b.at(4, 4))
        if b.first:
            wait(e, p_bk, 6)
        w_take(e, bank, slot, seq, lge, 1, 1, b.c - slot.c)
        for j in range(NJ):
            seqs = [t for k in range(KC) for t in split3(k)]
            for n, (xp, wp, k) in enumerate(seqs):
                m = e.matmul(W[:, bank, j * NE:(j + 1) * NE], x2T[xp][:, k, j * P:(j + 1) * P], wr_s[:, wp, k, :],
                             start=(n == 0), stop=(n == 11))
        m.then_inc(lgp, 1)

    def act_hi(e, b, i, step, dst, done, free, hi_sem, bias=None):
        wait(e, done, b.at(4, i + 1))
        if i == 0:
            free()
        if bias is None:
            e.activation(dst[:, i, :], W[:, BANK[step], :], ACT.Copy).then_inc(hi_sem, 1)
        else:
            e.activation(dst[:, i, :], W[:, BANK[step], :], ACT.Identity, bias=bias).then_inc(hi_sem, 1)

    def act_XTh(e, b, i):
        if b.reg is None and b.c == 1 and i == 1:
            act_split(e, 1)
            act_split(e, 2)
        if b.reg is None and b.c == 1 and i == 2:
            act_values(e)
        act_hi(e, b, i, f"XT{i}", xnT[0], t1p, lambda: wait(e, qp, b.at(4)), t1h)

    def act_Qh(e, b, G):
        if b.first and G == 0:
            wait(e, p_bk, 2)
        act_hi(e, b, G, f"Q{3 * G}", qs[0], qp, lambda: wait(e, restack[1 - b.par], (b + -1).half(192, 192)), qhe, bqs[:, G:G + 1])

    def act_YTh(e, b, i):
        act_hi(e, b, i, f"YT{i}", x2T[0], t2p, lambda: wait(e, lgp, b.at(1)), t2h)

    def act_ATh(e, b, i):
        act_hi(e, b, i, f"AT{i}", aT[0], atp, lambda: wait(e, op_, b.at(4)), ath)
        if b.reg is None and b.c == NB - 1 and i == KC - 1:
            act_load_experts(e, 5, NE)
        elif b.reg is None and b.c == NB - 1 and i == 0:
            wait(e, stp, 10 * NB)
            act_load_experts(e, 3, 5)

    def act_load_experts(e, first, last):
        if last == NE:
            wait(e, pvt, 8 * NB)
        wait(e, st_we, 32 * last)
        for n in range(first, last):
            e.dma_start(we_s[:, n * WN:(n + 1) * WN], we_d[n].rearrange("p l k n -> p (l k n)")).then_inc(ld_ew, 16)

    def act_EX(e, b, n):
        if b.reg is None and b.c == NB - 1 and n == 0:
            wait(e, qp, 4 * NB)
            wait(e, restack[(NB - 1) % 2], 192 * NB // 2)
            wait(e, stp, 10 * (NB - 1))
            wait(e, nap[0], NB)
            act_load_experts(e, 0, 3)
            e.dma_start(be_s[:, :], be.rearrange("(a e) n -> a (e n)", a=1).broadcast_to([P, NE * D])).then_inc(ld_ew, 16)
        wait(e, stp, b.at(10, n + 1))
        wait(e, pld, b.at(10, n - 1))
        e.activation(P32[n % 2][:, :, :], S[:, 2 * (n % 2):2 * (n % 2) + 2, :], ACT.Exp, scale=1.0 / (SS * ROOT)).then_inc(exd, 1)

    def act_PH(e, b, n):
        wait(e, exd, b.at(10, n + 1))
        done = (2 * n - 9) // 5 if n >= 5 else (2 * n + 11) // 5 - 4
        wait(e, pvt, b.at(8, 2 * done + 2))
        r = 2 * (n % 5)
        e.activation(Pst[0][:, r:r + 2, :], P32[n % 2][:, :, :], ACT.Copy).then_inc(phd, 1)

    def act_RX(e, b, i):
        wait(e, rch, b.at(RCH, RCH))
        e.activation(ex9[:, :, :], lgd[:, :, :], ACT.Exp).then_inc(rex, 1)

    def dve_XTl(e, b, i):
        dve_lo(e, b, i, f"XT{i}", xnT[1], xnT[0], t1h, t1e)
        if b.reg is None and b.c == 1 and i == 1:
            dve_split(e, 1)
            dve_split(e, 2)

    def dve_lo(e, b, i, step, dst, hi, hi_sem, ev):
        wait(e, hi_sem, b.at(4, i + 1))
        e.tensor_tensor(dst[:, i, :], W[:, BANK[step], :], hi[:, i, :], ALU.subtract).then_inc(ev, 1)

    def dve_Ql(e, b, G):
        wait(e, qhe, b.at(4, G + 1))
        e.scalar_tensor_tensor(qs[1][:, G, :], W[:, BANK[f"Q{3 * G}"], :], bqs[:, G:G + 1], qs[0][:, G, :], ALU.add, ALU.subtract).then_inc(qle, 1)

    def dve_DMX(e, b, n):
        if b.first and n == 0:
            dve_values(e)
        wait(e, mxp, b.at(11, n + 1))
        if n == 0:
            wait(e, mtp, b.at(1))
        k = 3 if n < 10 else 2
        if n < 10:
            e.tensor_reduce(mx_sb[:, 6 * n:6 * n + 6].rearrange("p (a k) -> p a k", a=2),
                            S[:, 2 * (n % 2):2 * (n % 2) + 2, 0:3 * C].rearrange("p a (k c) -> p a k c", c=C),
                            AX, ALU.max).then_inc(mxr, 1)
        else:
            e.tensor_reduce(mx_sb[:, 60:63], S[:, 0, 0:3 * C].rearrange("p (k c) -> p k c", c=C), AX, ALU.max)
            e.tensor_reduce(mx_sb[:, 63:64], S[:, 1, 0:C], AX, ALU.max).then_inc(mxr, 1)

    def dve_Oe(e, b, j):
        wait(e, op_, b.at(4, j + 1))
        if j == 0:
            wait(e, xrb, b.at(1, 1))
        e.scalar_tensor_tensor(xR[b.par][:, j, :], W[:, BANK[f"O{3 * j}"], :], OSC, xR[b.par][:, j, :], ALU.mult, ALU.add).then_inc(x1s, 1)

    def dve_MTe(e, b, i):
        wait(e, mtp, b.at(1, 1))
        wait(e, mrow[1 - b.par], (b + -1).half(16, 16))
        e.tensor_scalar(mT[:, :], W[0:H, BANK["MT0"], :], 1.0 / SS, MSHIFT, ALU.mult, ALU.subtract).then_inc(mte, 1)

    RCH = 4 + 8 + 1

    def dve_RT(e, b, i):
        if b.first:
            wait(e, g_set, 9)
        ch = Chain(e, rch, b, RCH)
        wait(e, lgp, b.at(1, 1))
        wait(e, rcd2, b.at(RC2))
        e.scalar_tensor_tensor(lg[:, :, 0:NE], W[:, BANK["LG0"], 0:NJ * NE].rearrange("p (j e) -> p j e", e=NE), ESC,
                               br_b[:, :].rearrange("p (o e) -> p o e", o=1).broadcast_to([P, NJ, NE]),
                               ALU.mult, ALU.add).then_inc(lge, 1)
        wait(e, lge, b.at(1, 1))
        hold(e)
        for j in range(NJ):
            ch.do(e.max(top8[:, j, :], lg[:, j, 0:NE]))
        ch.sync()
        hold(e)
        for j in range(NJ):
            ch.do(e.max_index(topi[:, j, :], top8[:, j, :], lg[:, j, 0:NE]))
        ch.do(e.tensor_copy(lg[:, :, NE:NE + 1], top8[:, :, 1:2]))
        ch.sync()
        ch.do(e.tensor_tensor(lgd[:, :, :], lg[:, :, :], top8[:, :, 0:1].broadcast_to([P, NJ, NE + 1]), ALU.subtract))
        ch.do(e.tensor_copy(topf[:, :, :].rearrange("p k j -> p j k"), topi[:, :, 0:TOPK]))
        ch.sync()
        for k in range(TOPK):
            ch.do(e.tensor_tensor(oneh[:, k, :, :], io8[:, :, :],
                                  topf[:, k, :].rearrange("p (j o) -> p j o", o=1).broadcast_to([P, NJ, NE]), ALU.is_equal))
        ch.sync()
        ch.end()
        e.tensor_tensor(msk[:, :, :], oneh[:, 0, :, :], oneh[:, 1, :, :], ALU.add).then_inc(mskd, 1)

    RC2 = 10

    def dve_RR(e, b, _):
        p = b.par
        ch = Chain(e, rcd2, b, RC2)
        wait(e, rp, b.at(1, 1))
        wait(e, rev, b.at(1))
        ch.do(e.tensor_tensor(posb[:, :, :], W[:, BANK["R0"], 0:NJ * NE].rearrange("p (j e) -> p j e", e=NE),
                              base[:, :].rearrange("p (o e) -> p o e", o=1).broadcast_to([P, NJ, NE]), ALU.add))
        ch.sync()
        e.tensor_tensor(base[:, :], base[:, :], W[:, BANK["R0"], NJ * NE:(NJ + 1) * NE], ALU.add).then_inc(rev, 1)
        for k in range(TOPK):
            i = e.tensor_tensor(seld[:, k, :, :], oneh[:, k, :, :], posb[:, :, :], ALU.mult)
            ch.do(i)
        wait(e, rex, b.at(1, 1))
        for k in range(TOPK):
            wait(e, scat[p][k], b.half(64))
        ch.do(e.tensor_reduce(sm[:, 0, :], ex9[:, :, 0:NE], AX, ALU.add))
        ch.sync()
        ch.do(e.tensor_reduce(idf[:, :, :], seld[:, :, :, :], AX, ALU.add))
        ch.do(e.reciprocal(wts[p][:, 0, :], sm[:, 0, :]))
        ch.sync()
        ch.do(e.tensor_tensor(wts[p][:, 1, :], wts[p][:, 0, :], ex9[:, :, NE], ALU.mult))
        ch.do(e.tensor_copy(xn2[p][:, :, D:D + 1], wts[p][:, 0, :].rearrange("p (j o) -> p j o", o=1)))
        ch.do(e.tensor_copy(xn2[p][:, :, D + 1:RW], tok[:, :].rearrange("p (j o) -> p j o", o=1)))
        ch.sync()
        ch.do(e.tensor_scalar(tok[:, :], tok[:, :], float(TB), None, ALU.add))
        e.tensor_copy(idx[p][:, :], idf[:, :, :].rearrange("p k j -> p (k j)")).then_inc(ridx, 1)
        ch.end()

    def dve_SA(e, b, j):
        if j == 0:
            wait(e, ld_xA[b.par], b.half(16, 16))
        dve_norm_stats(e, 0, xA[b.par], j)

    def dve_SN(e, b, j):
        wait(e, x1s, b.at(4, j + 1))
        dve_norm_stats(e, 1, xR[b.par], j)

    def dve_PL(e, b, n):
        if b.first and n == 0:
            wait_values_stored(e)
        wait(e, phd, b.at(10, n + 1))
        r = 2 * (n % 5)
        e.tensor_tensor(Pst[1][:, r:r + 2, :], P32[n % 2][:, :, :], Pst[0][:, r:r + 2, :], ALU.subtract).then_inc(pld, 1)

    def dve_NM(e, b, w):
        G, q = w // 2, w % 2
        wait(e, pvt, b.at(8, w + 1))
        if w == 0:
            wait(e, atp, b.at(4))
        src = PVp[:, q, 0:264].rearrange("p (j g c) -> p j g c", j=2, c=33)
        e.reciprocal(rcp[:, q, :, :], src[:, :, :, HD]).then_inc(rcd, 1)
        wait(e, rcd, b.at(8, w + 1))
        e.tensor_tensor(att[:, 2 * q:2 * q + 2, 4 * G:4 * G + 4, :], src[:, :, :, 0:HD],
                        rcp[:, q, :, :].rearrange("p j (g o) -> p j g o", o=1).broadcast_to([P, 2, 4, HD]), ALU.mult).then_inc(nmd, 1)

    def tables(e):
        k = [0]

        def do(ins):
            ins.then_inc(tbd, 1)
            k[0] += 1
            wait(e, tbd, k[0])

        reg0, cnt, nt, cum, first, tmp = (tb[:, i, :] for i in range(6))
        row = lambda v: v[0:1, :]
        wide = lambda v: v.rearrange("p (o e) -> p o e", o=1).broadcast_to([1, NT, NE])
        deep = lambda v: v.rearrange("p (n o) -> p n o", o=1).broadcast_to([1, NT, NE])
        wait(e, rev, NB)
        e.tensor_copy(baseI[:, :], base[0:1, :]).then_inc(tbz, 1)
        do(e.tensor_scalar(reg0, io8[:, 0, :], float(REGION), None, ALU.mult))
        do(e.tensor_tensor(cnt, base[:, :], reg0, ALU.subtract))
        do(e.tensor_scalar(tbi[:, 0, :], cnt, float(P - 1), None, ALU.add))
        do(e.tensor_scalar(tbi[:, 1, :], tbi[:, 0, :], P.bit_length() - 1, None, ALU.arith_shift_right))
        do(e.tensor_copy(nt, tbi[:, 1, :]))
        do(e.tensor_copy(cum, nt))
        for n in range(1, NE):
            do(e.tensor_tensor(cum[:, n:n + 1], cum[:, n - 1:n], nt[:, n:n + 1], ALU.add))
        do(e.scalar_tensor_tensor(tmp, cum, -float(P), reg0, ALU.mult, ALU.add))
        do(e.scalar_tensor_tensor(first, nt, float(P), tmp, ALU.mult, ALU.add))
        do(e.tensor_tensor(tg[:, :, :], deep(tile_no[:, :]), wide(row(cum)), ALU.is_ge))
        do(e.tensor_reduce(te[:, 0, :], tg[:, :, :], AX, ALU.add))
        do(e.tensor_tensor(tg[:, :, :], wide(io8[0:1, 0, :]), deep(te[:, 0, :]), ALU.is_equal))
        do(e.tensor_tensor(tg[:, :, :], tg[:, :, :], wide(row(first)), ALU.mult))
        do(e.tensor_reduce(te[:, 1, :], tg[:, :, :], AX, ALU.add))
        do(e.tensor_scalar(te[:, 2, :], te[:, 0, :], NE - 0.5, float(SPARE), ALU.is_ge, ALU.mult))
        do(e.tensor_tensor(te[:, 1, :], te[:, 1, :], te[:, 2, :], ALU.add))
        do(e.scalar_tensor_tensor(te[:, 2, :], tile_no[:, :], float(P), te[:, 1, :], ALU.mult, ALU.add))
        do(e.tensor_scalar(te[:, 2, :], te[:, 2, :], float(SPARE), None, ALU.min))
        do(e.tensor_copy(row_t[:, :], te[:, 2, :]))
        do(e.tensor_scalar(exp_t[:, :], te[:, 0, :], float(NE - 1), None, ALU.min))
        do(e.tensor_tensor(te[:, 1, 1:NT], te[:, 0, 1:NT], te[:, 0, 0:NT - 1], ALU.not_equal))
        do(e.tensor_scalar(new_t[:, 1:NT], te[:, 1, 1:NT], 16.0, None, ALU.mult))

    def pool_XB(e, b, _):
        if b.first:
            wait(e, L["bo"], 32)
        p = b.par
        wait(e, ld_xR[p], b.half(16, 16))
        hold(e)
        for j in range(NJ):
            i = e.tensor_tensor(xR[p][:, j, :], xR[p][:, j, :], bo_b[:, :], ALU.add)
        i.then_inc(xrb, 1)

    def pool_NA(e, b, n):
        if n:
            for k in range(TOPK):
                wait(e, scat[b.par][k], b.half(64))
            wait(e, t2p, b.at(4, -4))
            pool_norm_apply(e, 1, b, xR[b.par], xn2[b.par][:, :, 0:D])
        else:
            wait(e, t1p, b.at(4))
            pool_norm_apply(e, 0, b, xA[b.par], xn1)

    def scatter(e, p, k):
        for j in range(NJ):
            e.indirect_dma_start(xs_d.ap(), bass.IndirectOffsetOnAxis(ap=idx[p][:, k * NJ + j:k * NJ + j + 1], axis=0),
                                 xn2[p][:, j, :], None).then_inc(scat[p][k], 16)

    def pool_SC(e, b, _):
        wait(e, ridx, b.at(1, 1))
        hold(e)
        scatter(e, b.par, 0)

    def pool_SD(e, b, _):
        p = b.par
        wait(e, scat[p][0], b.half(64, 64))
        hold(e)
        e.tensor_copy(xn2[p][:, :, D:D + 1], wts[p][:, 1, :].rearrange("p (j o) -> p j o", o=1)).then_inc(wcol, 1)
        wait(e, wcol, b.at(1, 1))
        hold(e)
        scatter(e, p, 1)

    def pool_WH(e, b, _):
        wait(e, ld_we, b.at(16, 16))
        wait(e, st_we, b.at(16))
        hold(e)
        e.tensor_scalar(wst[:, :], wst[:, :], WS, None, ALU.mult).then_inc(wech, 1)
        wait(e, wech, b.at(3, 1))
        hold(e)
        e.tensor_scalar(wsp[:, 0, :], wst[:, :], 1.0, None, ALU.mult).then_inc(wech, 1)
        wait(e, wech, b.at(3, 2))
        hold(e)
        e.tensor_tensor(wsp[:, 1, :], wst[:, :], wsp[:, 0, :], ALU.subtract).then_inc(wech, 1)
        if b.reg is None and b.c == NB - 1:
            wait(e, wech, 3 * NB)
            e.memset(wst[:, 0:D + 1], 0.0).then_inc(zset, 1)
            e.memset(wst[:, D + 1:RW], NOWHERE).then_inc(zset, 1)

    def blk_rows(src, b):
        return src[bass.ds(b.at(TB), TB), :].rearrange("(j p) d -> p j d", p=P)

    def sp_XA(e, b, _):
        wait(e, nap[0], b.at(1, -1))
        e.dma_start(xA[b.par][:, :, :], blk_rows(x, b)).then_inc(ld_xA[b.par], 16)

    def sp_KV(e, b, _):
        p = b.par
        wait(e, pvt, b.at(8, -8))
        bt = b.c // 4 if b.reg is None else (b.reg * 2 + b.c) // 4
        if b.first:
            wait(e, p_kd, 16 * 12)
        e.dma_start(Kst[p][0:96, :, :].rearrange("p (g G) c -> p g (G c)", g=4), k_d[:, :, bass.ds(bt, 1), :].rearrange("p g o n -> p (g o) n")).then_inc(ld_k[p], 16)
        if not b.first:
            sp_values(e, b, bt)

    def sp_values(e, b, bt):
        p = b.par
        if b.first:
            wait_values_stored(e)
        e.dma_start(Vm[p][:, :, :, :].rearrange("p h l c -> p (h l c)"), vm_d[bass.ds(bt, 1), :, :].rearrange("o p n -> (o p) n")).then_inc(ld_v[p], 16)
        e.dma_start(Vr[p][:, :, :, :].rearrange("p l g c -> p (l g c)"), vr_d[bass.ds(bt, 1), :, :].rearrange("o p n -> (o p) n")).then_inc(ld_v[p], 16)

    def sp_RS(e, b, _):
        p = b.par
        wait(e, qle, b.at(4, 4))
        wait(e, stp, b.at(10, -10))
        for g in range(4):
            for part, row in ((0, 0), (0, 32), (1, 64)):
                e.dma_start(Qst[p][row:row + 32, g::4, :], qs[part][32 * g:32 * g + 32, :, :]).then_inc(restack[p], 16)

    def sp_XR(e, b, _):
        if b.first:
            sp_values_rem(e)
            wait(e, p_vp, B + 1)
        wait(e, st_x1[b.par], b.half(16))
        wait(e, nap[1], b.at(1, -1))
        e.dma_start(xR[b.par][:, :, :], blk_rows(x, b)).then_inc(ld_xR[b.par], 16)

    def sp_XS(e, b, _):
        wait(e, x1s, b.at(4, 4))
        e.dma_start(blk_rows(out, b), xR[b.par][:, :, :]).then_inc(st_x1[b.par], 16)

    def expert_of(b):
        return b.c // 2 if b.reg is None else b.reg + b.c // 2

    def sp_WL(e, b, _):
        wait(e, wech, b.at(3))
        e.dma_start(wst[:, :].rearrange("p (k n) -> p k n", n=D),
                    weT[bass.ds(expert_of(b), 1), (b.c % 2) * 2 * P:(b.c % 2 + 1) * 2 * P, :].rearrange("o (k p) n -> p (o k) n", p=P)).then_inc(ld_we, 16)

    def sp_WW(e, b, _):
        wait(e, wech, b.at(3, 3))
        e.dma_start(we_d[bass.ds(expert_of(b), 1), :, :, 2 * (b.c % 2):2 * (b.c % 2) + 2, :].rearrange("o p l k n -> (o p) l (k n)"),
                    wsp[:, :, :]).then_inc(st_we, 16)

    def sp_MR(e, b, _):
        wait(e, mte, b.at(1, 1))
        e.dma_start(Qst[b.par][96:97, :, :], mT[:, :]).then_inc(mrow[b.par], 16)
        if b.first:
            sp_values(e, b, 0)

    PE = dict(MX=pe_MX, O=pe_O, XT=pe_XT, R=pe_R, MT=pe_MT, Q=pe_Q, ST=pe_ST, YT=pe_YT, LG=pe_LG, PV=pe_PV, AT=pe_AT)
    AE = dict(XTh=act_XTh, Qh=act_Qh, YTh=act_YTh, ATh=act_ATh, EX=act_EX, PH=act_PH, RX=act_RX,
              NN=lambda e, b, n: act_norm(e, n, b))
    VE = dict(DMX=dve_DMX, Oe=dve_Oe, Ql=dve_Ql, MTe=dve_MTe, RT=dve_RT, RR=dve_RR, PL=dve_PL, NM=dve_NM,
              XTl=dve_XTl,
              YTl=lambda e, b, i: dve_lo(e, b, i, f"YT{i}", x2T[1], x2T[0], t2h, t2e),
              ATl=lambda e, b, i: dve_lo(e, b, i, f"AT{i}", aT[1], aT[0], ath, ate),
              SA=dve_SA, SN=dve_SN, NV=lambda e, b, n: dve_norm_var(e, n, b),
              NC=lambda e, b, n: dve_norm_coef(e, n, b, (XS, XS2)[n]))
    GE = dict(XB=pool_XB, NA=pool_NA, SC=pool_SC, SD=pool_SD, WH=pool_WH)
    SE = dict(XA=sp_XA, KV=sp_KV, RS=sp_RS, XR=sp_XR, XS=sp_XS, MR=sp_MR, WL=sp_WL, WW=sp_WW)

    def slots(e, order, steps, banks=False, done=()):
        todo = []
        for word in order.split():
            kind = word.rstrip("0123456789+-") or word
            at = word[len(kind):]
            i, off = (at[:-2], int(at[-2:])) if at[-2:-1] in ("+", "-") else (at, 0)
            todo.append((kind, int(i), off))
        offs = [off for _, _, off in todo]

        def slot(s, seq):
            for kind, i, off in todo:
                b = s + off
                if b.here() and (b.reg is not None or (kind, i, b.c) not in done):
                    if banks:
                        steps[kind](e, b, i, s, seq)
                    else:
                        steps[kind](e, b, i)

        first, last = -max(offs), NB - 1 - min(offs)
        lo = 2 - min(offs)
        n = (NB - max(offs) - lo) // 2
        for s in range(first, lo):
            slot(Blk(s), s)
        with e.Fori(0, n) as it:
            for u in range(2):
                slot(Blk(lo + u, it), lo + u)
        if banks:
            w_skip(2 * n - 2)
        for s in range(lo + 2 * n, last + 1):
            slot(Blk(s), s)

    with nc.Block() as block:
        @block.sync
        def _(e):
            start_counts(e, attend_sems)
            sp_prepare(e)
            slots(e, ORDER_SP, SE, done=[("XA", 0, 0), ("XA", 0, 1)])
            wait(e, zset, 2)
            zeros = zrow
            e.dma_start(xs_d[SPARE:ROWS, :], zeros).then_inc(zst, 16)
            wait(e, tbz, 1)
            for n in range(NE):
                r = e.value_load(baseI[0:1, n:n + 1], min_val=0, max_val=SPARE - P)
                e.dma_start(xs_d[bass.ds(r, P), :], zeros).then_inc(zst, 16)
            wait(e, zst, 16 * (NE + 1))
            wait(e, ld_ew, 16 * (NE + 1))
            for p in range(2):
                wait(e, st_x1[p], 16 * NB // 2)
                for k in range(TOPK):
                    wait(e, scat[p][k], 64 * NB // 2)

        @block.gpsimd
        def _(e):
            pool_prepare(e)
            wait(e, p_set, 3 + 2 * B)
            e.memset(Kst[0][96:97, :, :], -SS).then_inc(g_set, 1)
            wait(e, g_set, 1)
            e.memset(Kst[1][96:97, :, :], -SS).then_inc(g_set, 1)
            wait(e, g_set, 2)
            e.memset(ones[:, :], 1.0).then_inc(g_set, 1)
            e.memset(tri[:, :], 1.0).then_inc(g_set, 1)
            wait(e, g_set, 4)
            e.affine_select(out=tri[:, :], in_=tri[:, :], compare_op=ALU.is_gt, fill=0.0, base=0,
                            pattern=[[1, P]], channel_multiplier=-1).then_inc(g_set, 1)
            e.iota(io8[:, :, :], [[0, NJ], [1, NE]], base=0, channel_multiplier=0, allow_small_or_imprecise_dtypes=True).then_inc(g_set, 1)
            e.iota(base[:, :], [[REGION, NE]], base=0, channel_multiplier=0, allow_small_or_imprecise_dtypes=True).then_inc(g_set, 1)
            e.iota(tile_no[:, :], [[1, NT]], base=0, channel_multiplier=0, allow_small_or_imprecise_dtypes=True).then_inc(g_set, 1)
            e.iota(tok[:, :], [[P, NJ]], base=0, channel_multiplier=1, allow_small_or_imprecise_dtypes=True).then_inc(g_set, 1)
            slots(e, ORDER_POOL, GE)

        @block.scalar
        def _(e):
            e.preload_act_table_set("natural_log_exp_and_others")
            act_prepare(e)
            slots(e, ORDER_ACT, AE, done=[("NN", 0, 0)])

        @block.vector
        def _(e):
            dve_prepare(e)
            slots(e, ORDER_DVE, VE, done=[("SA", j, b) for j in range(NJ) for b in range(2)] + [("NV", 0, 0), ("NC", 0, 0)])
            tables(e)

        @block.tensor
        def _(e):
            pe_prepare(e)
            slots(e, ORDER_PE, PE, True)
    attend.close()

    TU = 4
    NTURN = MAXT // TU
    with ExitStack() as ex:
        t = ex.enter_context
        xg = [t(nc.sbuf_tensor(f"xg{i}", [P, RW], F32)) for i in range(TU)]
        gT = [[t(nc.sbuf_tensor(f"gT{i}_{n}", [P, KC, P], F16)) for n in ("hi", "lo")] for i in range(2)]
        wt = [t(nc.sbuf_tensor(f"wt{i}", [P, 2], F32)) for i in range(TU)]
        to = [t(nc.sbuf_tensor(f"to{i}", [P, 1], I32)) for i in range(TU)]
        yb = [t(nc.sbuf_tensor(f"yb{i}", [P, D], F32)) for i in range(2)]
        yw = [t(nc.sbuf_tensor(f"yw{i}", [P, D], F32)) for i in range(TU)]
        Tp = t(nc.psum_tensor("Tp", [P, 2, 512], F32))
        Yp = t(nc.psum_tensor("Yp", [P, 2, 512], F32))
        expert_sems = len(held)
        ld_g = [sem(f"ld_g{i}", t) for i in range(TU)]
        add_y = [sem(f"add_y{i}", t) for i in range(TU)]
        gp, gh, gl = sem("gp", t, 4), sem("gh", t, 4), sem("gl", t, 4)
        yp, ye, ywd = sem("yp", t, 4), sem("ye", t, 4), sem("ywd", t, 4)
        wtd, tod = sem("wtd", t), sem("tod", t, 4)
        block = t(nc.Block())

        def tile(it, u):
            return it * TU + u

        def sp_load(e, it, u):
            i = tile(it, u)
            r = e.value_load(row_t[0:1, bass.ds(i, 1)], min_val=0, max_val=SPARE)
            wait(e, gp, i + (1 - TU))
            wait(e, wtd, i + (1 - TU))
            e.dma_start(xg[u % TU][:, :], xs_d[bass.ds(r, P), :]).then_inc(ld_g[u % TU], 16)

        @block.sync
        def _(e):
            start_counts(e, expert_sems)
            for u in range(TU):
                sp_load(e, 0, u)
            with e.Fori(0, NTURN) as it:
                for u in range(TU):
                    sp_load(e, it, u + TU)
            for u in range(TU):
                wait(e, ld_g[u], 16 * (NTURN + 1))

        @block.gpsimd
        def _(e):
            def token(it, u, first):
                wait(e, wtd, tile(it, u + 1))
                if not first:
                    wait(e, add_y[u], it * 16)
                hold(e)
                e.tensor_copy(to[u][:, :], wt[u][:, 1:2]).then_inc(tod, 1)

            def add(it, u, first):
                i = tile(it, u)
                wait(e, ywd, i + 1)
                wait(e, tod, i + 1)
                if not first and u:
                    new = e.value_load(new_t[0:1, bass.ds(i, 1)], min_val=0, max_val=16)
                    wait(e, add_y[u - 1], it * 16 + new)
                elif not first or u:
                    wait(e, add_y[(u - 1) % TU], it * 16 + (16 if u else 0))
                if not first or u >= 2:
                    wait(e, add_y[(u - 2) % TU], it * 16 + (16 if u >= 2 else 0))
                hold(e)
                e.indirect_dma_start(out, bass.IndirectOffsetOnAxis(ap=to[u][:, :], axis=0), yw[u][:, :], None,
                                     bounds_check=N - 1, oob_is_err=False, compute_op=ALU.add).then_inc(add_y[u], 16)

            def body(it, first):
                for u in range(TU):
                    token(it, u, first)
                    add(it, u, first)

            body(0, True)
            with e.Fori(0, NTURN - 1) as it:
                body(it + 1, False)
            for u in range(TU):
                wait(e, add_y[u], 16 * NTURN)

        @block.scalar
        def _(e):
            def hi(it, u):
                i = tile(it, u)
                wait(e, gp, i + 1)
                wait(e, yp, i - 1)
                e.activation(gT[u % 2][0][:, :, :].rearrange("p k n -> p (k n)"), Tp[:, u % 2, :], ACT.Copy).then_inc(gh, 1)

            def weigh(it, u, first=False):
                i = tile(it, u)
                wait(e, ye, i + 1)
                if not first:
                    wait(e, add_y[u], it * 16)
                e.activation(yw[u][:, :], yb[u % 2][:, :], ACT.Copy, scale=wt[u][:, 0:1]).then_inc(ywd, 1)

            def body(it, first):
                for u in range(TU):
                    hi(it, u + 1)
                    weigh(it, u, first)

            hi(0, 0)
            body(0, True)
            with e.Fori(0, NTURN - 1) as it:
                body(it + 1, False)

        @block.vector
        def _(e):
            def lo(it, u):
                i = tile(it, u)
                wait(e, gh, i + 1)
                e.tensor_tensor(gT[u % 2][1][:, :, :].rearrange("p k n -> p (k n)"), Tp[:, u % 2, :],
                                gT[u % 2][0][:, :, :].rearrange("p k n -> p (k n)"), ALU.subtract).then_inc(gl, 1)

            def weights(it, u):
                i = tile(it, u)
                wait(e, ld_g[u], it * 16 + 16)
                wait(e, ywd, i + (1 - TU))
                wait(e, tod, i + (1 - TU))
                e.tensor_copy(wt[u][:, :], xg[u][:, D:RW]).then_inc(wtd, 1)
                return e.value_load(exp_t[0:1, bass.ds(i, 1)], min_val=0, max_val=NE - 1)

            def scale_bias(it, u, n):
                i = tile(it, u)
                wait(e, yp, i + 1)
                wait(e, ywd, i - 1)
                e.scalar_tensor_tensor(yb[u % 2][:, :], Yp[:, u % 2, :], ESC, be_s[:, bass.ds(n * D, D)], ALU.mult, ALU.add).then_inc(ye, 1)

            lo(0, 0)
            with e.Fori(0, NTURN) as it:
                for u in range(TU):
                    n = weights(it, u)
                    lo(it, u + 1)
                    scale_bias(it, u, n)

        @block.tensor
        def _(e):
            def turn(it, u):
                i = tile(it, u)
                wait(e, ld_g[u % TU], it * 16 + 16 * (u // TU + 1))
                wait(e, gl, i - 1)
                for k in range(KC):
                    m = e.transpose(Tp[:, u % 2, k * P:(k + 1) * P], xg[u % TU][:, k * P:(k + 1) * P], ident[:, :])
                m.then_inc(gp, 1)

            turn(0, 0)
            with e.Fori(0, NTURN) as it:
                for u in range(TU):
                    turn(it, u + 1)
                    i = tile(it, u)
                    n = e.value_load(exp_t[0:1, bass.ds(i, 1)], min_val=0, max_val=NE - 1)
                    wait(e, gl, i + 1)
                    wait(e, ye, i - 1)
                    seqs = [q for k in range(KC) for q in split3(k)]
                    for c, (xp, wp, k) in enumerate(seqs):
                        m = e.matmul(Yp[:, u % 2, :], gT[u % 2][xp][:, k, :], we_s[:, bass.ds(n * WN + (wp * KC + k) * D, D)],
                                     start=(c == 0), stop=(c == 11))
                    m.then_inc(yp, 1)
    top.close()


_P = "L0_xattn_"
_F = "L0_ffn_"


def kernel(**inputs):
    import concourse.bacc as bacc
    from concourse.bass_utils import run_bass_kernel_spmd

    ctx = np.asarray(inputs["ctx_1024"])
    ctx = np.concatenate([ctx[:, 0:P].reshape(B * P, D), ctx[:, P:C].reshape(B * CR, D)])
    arrays = {
        "x": np.asarray(inputs["x"]).reshape(N, D),
        "ctxT": ctx.T,
        "wqT": np.asarray(inputs[_P + "Wq"]).T, "bq": np.asarray(inputs[_P + "bq"]).reshape(NG, P).T,
        "wkT": np.asarray(inputs[_P + "Wk"]).T, "bk": np.asarray(inputs[_P + "bk"]).reshape(NG, P).T,
        "wvT": np.asarray(inputs[_P + "Wv"]).T, "bv": inputs[_P + "bv"],
        "woT": np.asarray(inputs[_P + "Wo"]).T, "bo": inputs[_P + "bo"],
        "weT": np.asarray(inputs[_F + "W_experts"]).transpose(0, 2, 1), "be": inputs[_F + "b_experts"],
        "wrT": np.asarray(inputs[_F + "W_router"]).T, "br": inputs[_F + "b_router"],
    }
    arrays = {"in_" + n: np.ascontiguousarray(v) for n, v in arrays.items()}
    nc = bacc.Bacc("TRN2", target_bir_lowering=False, num_devices=1)
    args = [nc.dram_tensor(n, v.shape, mybir.dt.from_np(v.dtype), kind="ExternalInput").ap() for n, v in arrays.items()]
    args.append(nc.dram_tensor("out", (N, D), F32, kind="ExternalOutput").ap())
    build(nc, *args)
    got = run_bass_kernel_spmd(nc, [arrays], core_ids=[0]).results[0]["out"]
    return got.reshape(B, T, D)
```
